# Optimizing a Trainium2 kernel written in Bass

```python
import numpy as np
import jax
import jax.numpy as jnp

def _softmax(x, axis=-1):
    return jax.nn.softmax(x, axis=axis)

def _gelu(x):
    return jax.nn.gelu(x, approximate=True)

def _silu(x):
    return jax.nn.silu(x)

def _sigmoid(x):
    return jax.nn.sigmoid(x)

def _layernorm(x, axis=-1, eps=1e-05):
    m = jnp.mean(x, axis=axis, keepdims=True)
    v = jnp.var(x, axis=axis, keepdims=True)
    return (x - m) / jnp.sqrt(v + eps)

def _scatter_add(tgt, idx, src, axis=0):
    return tgt.at[idx].add(src)

def _segment_sum(src, seg, n):
    return jax.ops.segment_sum(src, seg, n)
kernel_name = 'mk_decoder_postln_d1_seqx_r4_3ec612'

def setup_inputs(seed: int=0):
    np.random.seed(seed)
    _w = jnp.asarray

    def _rec_inputs():
        import jax
        import jax.numpy as jnp
        _rk = jax.random.key(seed)
        x = -9.806e-05 + 1 * jax.random.normal(jax.random.fold_in(_rk, 1), (8, 256, 256), jnp.float32)
        _lenS = 256 - jax.random.randint(jax.random.fold_in(_rk, 7), (8,), 0, max(1, 256 // 4) + 1, jnp.int32)
        _lenS2 = 256 - jax.random.randint(jax.random.fold_in(_rk, 8), (8,), 0, max(1, 256 // 4) + 1, jnp.int32)
        _ctx_1024P = jax.random.normal(jax.random.fold_in(_rk, 11), (8, 16, 256), jnp.float32)
        _ctx_1024c = jax.random.dirichlet(jax.random.fold_in(_rk, 511), 0.3 * jnp.ones((16,), jnp.float32), (8, 256))
        _ctx_1024t = jnp.einsum('bsk,bkd->bsd', _ctx_1024c, _ctx_1024P)
        _ctx_1024t = _ctx_1024t * jax.lax.rsqrt(jnp.mean(jnp.square(_ctx_1024t)) + 1e-12) * 0.953939
        ctx_1024 = -1.52775e-05 + 0.999936 * (_ctx_1024t + 0.3 * jax.random.normal(jax.random.fold_in(_rk, 611), (8, 256, 256), jnp.float32))
        return (x, ctx_1024)
    x, ctx_1024 = _rec_inputs()

    def _L0_attn_setup():
        import jax, jax.numpy as jnp
        import numpy as np
        D_MODEL = 256
        N_HEAD = 16
        HEAD_DIM = D_MODEL // N_HEAD
        key = jax.random.key(seed)
        k1, k2, k3, k4, k5 = jax.random.split(key, 5)
        s = 1.0 / np.sqrt(D_MODEL)
        return {'x': jax.random.normal(k1, (4, 512, D_MODEL), dtype=jnp.float32), 'w_qkv': jax.random.normal(k2, (D_MODEL, 3 * D_MODEL), dtype=jnp.float32) * s, 'b_qkv': jax.random.normal(k3, (3 * D_MODEL,), dtype=jnp.float32) * 0.02, 'w_proj': jax.random.normal(k4, (D_MODEL, D_MODEL), dtype=jnp.float32) * s, 'b_proj': jax.random.normal(k5, (D_MODEL,), dtype=jnp.float32) * 0.02}
    _L0_attn_all = _L0_attn_setup()
    _L0_attn_in = {k: v for k, v in _L0_attn_all.items() if k in ('w_qkv', 'b_qkv', 'w_proj', 'b_proj')}
    del _L0_attn_all

    def _L0_xattn_setup():
        import jax, jax.numpy as jnp
        import numpy as np
        D = 256
        NUM_ITERS = 3
        EPS = 1e-06
        SCALE = D ** (-0.5)

        def rmsnorm(x, w, eps=EPS):
            return x * jax.lax.rsqrt(jnp.mean(x * x, axis=-1, keepdims=True) + eps) * w

        def gru_cell(x, h, wih, whh, bih, bhh):
            gx = x @ wih.T + bih
            gh = h @ whh.T + bhh
            xr, xz, xn = jnp.split(gx, 3, axis=-1)
            hr, hz, hn = jnp.split(gh, 3, axis=-1)
            r = jax.nn.sigmoid(xr + hr)
            z = jax.nn.sigmoid(xz + hz)
            n = jnp.tanh(xn + r * hn)
            return (1.0 - z) * n + z * h
        key = jax.random.key(seed)
        ks = jax.random.split(key, 8)
        B, K, M, d = (8, 64, 1024, D)
        w_std = d ** (-0.5)
        return {'slots': jax.random.normal(ks[0], (B, K, d), jnp.float32), 'P': jax.random.normal(ks[1], (B, M, d), jnp.float32), 'Wq': jax.random.normal(ks[2], (d, d), jnp.float32) * w_std, 'Wk': jax.random.normal(ks[3], (d, d), jnp.float32) * w_std, 'Wv': jax.random.normal(ks[4], (d, d), jnp.float32) * w_std, 'gru_wih': jax.random.normal(ks[5], (3 * d, d), jnp.float32) * w_std, 'gru_whh': jax.random.normal(ks[6], (3 * d, d), jnp.float32) * w_std, 'gru_bih': jnp.zeros((3 * d,), jnp.float32), 'gru_bhh': jnp.zeros((3 * d,), jnp.float32), 'slot_norm_w': jnp.ones((d,), jnp.float32), 'input_norm_w': jnp.ones((d,), jnp.float32)}
    _L0_xattn_all = _L0_xattn_setup()
    _L0_xattn_in = {k: v for k, v in _L0_xattn_all.items() if k in ('Wq', 'Wk', 'Wv', 'gru_wih', 'gru_whh', 'gru_bih', 'gru_bhh', 'slot_norm_w', 'input_norm_w')}
    del _L0_xattn_all

    def _L0_ffn_setup():
        import jax, jax.numpy as jnp
        import numpy as np
        DMODEL = 256
        N_EXPERTS = 16
        EXPERT_SIZE = 64
        K = 4
        key = jax.random.key(seed)
        k1, k2, k3, k4 = jax.random.split(key, 4)
        std_sel = 1.0 / np.sqrt(DMODEL)
        std_val = 1.0 / np.sqrt(N_EXPERTS * EXPERT_SIZE)
        return {'x': jax.random.normal(k1, (4, 512, DMODEL), dtype=jnp.float32), 'expert_sel': jax.random.normal(k2, (N_EXPERTS, DMODEL), dtype=jnp.float32) * std_sel, 'keys': jax.random.normal(k3, (N_EXPERTS, DMODEL, EXPERT_SIZE), dtype=jnp.float32) * std_sel, 'values': jax.random.normal(k4, (N_EXPERTS, EXPERT_SIZE, DMODEL), dtype=jnp.float32) * std_val, 'route_scale': jnp.ones((1,), dtype=jnp.float32)}
    _L0_ffn_all = _L0_ffn_setup()
    _L0_ffn_in = {k: v for k, v in _L0_ffn_all.items() if k in ('expert_sel', 'keys', 'values', 'route_scale')}
    del _L0_ffn_all
    return {'x': x, 'ctx_1024': ctx_1024, 'L0_attn_w_qkv': _L0_attn_in['w_qkv'], 'L0_attn_b_qkv': _L0_attn_in['b_qkv'], 'L0_attn_w_proj': _L0_attn_in['w_proj'], 'L0_attn_b_proj': _L0_attn_in['b_proj'], 'L0_xattn_Wq': _L0_xattn_in['Wq'], 'L0_xattn_Wk': _L0_xattn_in['Wk'], 'L0_xattn_Wv': _L0_xattn_in['Wv'], 'L0_xattn_gru_wih': _L0_xattn_in['gru_wih'], 'L0_xattn_gru_whh': _L0_xattn_in['gru_whh'], 'L0_xattn_gru_bih': _L0_xattn_in['gru_bih'], 'L0_xattn_gru_bhh': _L0_xattn_in['gru_bhh'], 'L0_xattn_slot_norm_w': _L0_xattn_in['slot_norm_w'], 'L0_xattn_input_norm_w': _L0_xattn_in['input_norm_w'], 'L0_ffn_expert_sel': _L0_ffn_in['expert_sel'], 'L0_ffn_keys': _L0_ffn_in['keys'], 'L0_ffn_values': _L0_ffn_in['values'], 'L0_ffn_route_scale': _L0_ffn_in['route_scale']}

def reference(x, ctx_1024, L0_attn_w_qkv, L0_attn_b_qkv, L0_attn_w_proj, L0_attn_b_proj, L0_xattn_Wq, L0_xattn_Wk, L0_xattn_Wv, L0_xattn_gru_wih, L0_xattn_gru_whh, L0_xattn_gru_bih, L0_xattn_gru_bhh, L0_xattn_slot_norm_w, L0_xattn_input_norm_w, L0_ffn_expert_sel, L0_ffn_keys, L0_ffn_values, L0_ffn_route_scale):
    import jax
    import jax.numpy as jnp

    def _L0_attn_ref(x, w_qkv, b_qkv, w_proj, b_proj):
        import jax, jax.numpy as jnp
        import numpy as np
        D_MODEL = 256
        N_HEAD = 16
        HEAD_DIM = D_MODEL // N_HEAD
        B, T, C = x.shape
        H, Dh = (N_HEAD, HEAD_DIM)
        qkv = x @ w_qkv + b_qkv
        qkv = qkv.reshape(B, T, 3, H, Dh)
        q = qkv[:, :, 0].transpose(0, 2, 1, 3)
        k = qkv[:, :, 1].transpose(0, 2, 1, 3)
        v = qkv[:, :, 2].transpose(0, 2, 1, 3)
        scale = 1.0 / np.sqrt(Dh).astype(np.float32)
        att = jnp.einsum('bhqd,bhkd->bhqk', q, k) * scale
        causal = jnp.tril(jnp.ones((T, T), dtype=bool))
        att = jnp.where(causal, att, -jnp.inf)
        att = jax.nn.softmax(att, axis=-1)
        y = jnp.einsum('bhqk,bhkd->bhqd', att, v)
        y = y.transpose(0, 2, 1, 3).reshape(B, T, C)
        return y @ w_proj + b_proj

    def _L0_xattn_ref(slots, P, Wq, Wk, Wv, gru_wih, gru_whh, gru_bih, gru_bhh, slot_norm_w, input_norm_w):
        import jax, jax.numpy as jnp
        import numpy as np
        D = 256
        NUM_ITERS = 3
        EPS = 1e-06
        SCALE = D ** (-0.5)

        def rmsnorm(x, w, eps=EPS):
            return x * jax.lax.rsqrt(jnp.mean(x * x, axis=-1, keepdims=True) + eps) * w

        def gru_cell(x, h, wih, whh, bih, bhh):
            gx = x @ wih.T + bih
            gh = h @ whh.T + bhh
            xr, xz, xn = jnp.split(gx, 3, axis=-1)
            hr, hz, hn = jnp.split(gh, 3, axis=-1)
            r = jax.nn.sigmoid(xr + hr)
            z = jax.nn.sigmoid(xz + hz)
            n = jnp.tanh(xn + r * hn)
            return (1.0 - z) * n + z * h
        Pn = rmsnorm(P, input_norm_w)
        k_proj = Pn @ Wk.T
        v_proj = Pn @ Wv.T
        for _ in range(NUM_ITERS):
            sn = rmsnorm(slots, slot_norm_w)
            q_proj = sn @ Wq.T
            scores = jnp.einsum('bkd,bmd->bkm', q_proj, k_proj) * SCALE
            attn = jax.nn.softmax(scores, axis=-2)
            attn = attn / (jnp.sum(attn, axis=-1, keepdims=True) + EPS)
            updates = jnp.einsum('bkm,bmd->bkd', attn, v_proj)
            slots = gru_cell(updates, slots, gru_wih, gru_whh, gru_bih, gru_bhh)
        return slots

    def _L0_ffn_ref(x, expert_sel, keys, values, route_scale):
        import jax, jax.numpy as jnp
        import numpy as np
        DMODEL = 256
        N_EXPERTS = 16
        EXPERT_SIZE = 64
        K = 4
        sel_logits = jnp.einsum('btd,ed->bte', x, expert_sel)
        sel_probs = jax.nn.sigmoid(sel_logits)
        _, sel_index = jax.lax.top_k(sel_probs, K)
        sel_val = jnp.take_along_axis(sel_probs, sel_index, axis=-1)
        sel_val = sel_val / jnp.clip(sel_val.sum(-1, keepdims=True), 1e-09)
        sel_val = sel_val * route_scale
        scores_all = jax.nn.relu(jnp.einsum('btd,edh->bteh', x, keys))
        values_all = jnp.einsum('bteh,ehv->btev', scores_all, values)
        sel_idx_exp = sel_index[..., None]
        selected = jnp.take_along_axis(values_all, sel_idx_exp, axis=2)
        out = (selected * sel_val[..., None]).sum(axis=2)
        return out
    x = _layernorm(x + _L0_attn_ref(x, L0_attn_w_qkv, L0_attn_b_qkv, L0_attn_w_proj, L0_attn_b_proj), axis=-1)
    x = _layernorm(x + _L0_xattn_ref(x, ctx_1024, L0_xattn_Wq, L0_xattn_Wk, L0_xattn_Wv, L0_xattn_gru_wih, L0_xattn_gru_whh, L0_xattn_gru_bih, L0_xattn_gru_bhh, L0_xattn_slot_norm_w, L0_xattn_input_norm_w), axis=-1)
    x = _layernorm(x + _L0_ffn_ref(x, L0_ffn_expert_sel, L0_ffn_keys, L0_ffn_values, L0_ffn_route_scale), axis=-1)
    return x

_drawn_inputs = setup_inputs


def setup_inputs(seed=0):
    import zlib

    import numpy as np

    out = dict(_drawn_inputs(seed))
    spreads = {'L0_xattn_gru_bih': (0.0, 0.1),
     'L0_xattn_gru_bhh': (0.0, 0.1),
     'L0_xattn_slot_norm_w': (1.0, 0.6),
     'L0_xattn_input_norm_w': (1.0, 0.2)}
    factors = {'L0_attn_b_proj': 2.747}
    for name, (base, spread) in spreads.items():
        noise = np.random.default_rng([zlib.crc32(name.encode()), seed]).standard_normal(out[name].shape)
        drawn = base * np.exp(spread * noise) if base else spread * noise
        out[name] = jnp.asarray(drawn.astype(out[name].dtype))
    for name, factor in factors.items():
        out[name] = (out[name] * factor).astype(out[name].dtype)
    return out
```

```python
from contextlib import ExitStack

import concourse.bass as bass
from concourse import mybir

F32, F32R, BF16 = mybir.dt.float32, mybir.dt.float32r, mybir.dt.bfloat16
ALU = mybir.AluOpType
ACT = mybir.ActivationFunctionType
AX = mybir.AxisListType

B, T, D = 8, 256, 256
P = 128
H, DH = 16, 16
NT = T // P
NC = D // P
G3 = 3 * D
NE, EH, TOPK = 16, 64, 4
NH = NE * EH // P
ITERS = 3
PAIRS = B // 2
LN_EPS, RMS_EPS = 1e-5, 1e-6
MASKED = -1e30
HI, LO = 0, 1
PASSES = ((HI, HI), (HI, LO), (LO, HI))
UNITS = 2 * ITERS
SQ = 384


ATTN_LINKS = 2 * 3
CROSS_LINKS = UNITS * 4 + 2 * 2
EXPERT_LINKS = 2 * 11


def head(n):
    pair = 4 * (n // 2 % 2) + n // 4
    return 2 * pair + n % 2


def due(per, i, k, back=0, step=1):
    assert 1 <= k <= per
    return (i * per + (1 - back) * per + k) * step


def decoder_layer(nc, x, ctx_in, w_qkv, b_qkv, w_proj, b_proj, wq, wk, wv, wih, whh, bih, bhh,
                  slot_w, input_w, expert_sel, keys, values, route_scale, out):
    stack = ExitStack()
    with stack:
        def sb(name, shape, dt=F32, where=stack):
            return where.enter_context(nc.sbuf_tensor(name, shape, dt))

        def sem(name):
            return stack.enter_context(nc.semaphore(name))

        events = []
        passed = sem("passed")

        def event(name, per, step=1):
            events.append((sem(name), per * step))
            return events[-1][0]

        ident = sb("ident", [P, P])
        ident16 = sb("ident16", [P, P], BF16)
        mask16 = sb("mask16", [P, 2, P], BF16)
        mask32 = sb("mask32", [P, P])
        mean_col = sb("mean_col", [P, 1])
        half_neg = sb("half_neg", [P, 2])
        wqkv_hl = sb("wqkv_hl", [P, 2, NC, G3], F32R)
        wproj_hl = sb("wproj_hl", [P, 2, NC, D], F32R)
        qk_w_hl = sb("qk_w_hl", [P, 2, NC, D], F32R)
        v_w_hl = sb("v_w_hl", [P, 2, NC, G3], F32R)
        whhT_hl = sb("whhT_hl", [P, 2, NC, G3], F32R)
        eselT_hl = sb("eselT_hl", [P, 2, NC, NE], F32R)
        keys_hl = sb("keys_hl", [P, 2, NC, NE * EH], F32R)
        values_hl = sb("values_hl", [P, 2, NH, D], F32R)
        bq_col = sb("bq_col", [P, 2 * NC])
        bv_row = sb("bv_row", [P, D])
        bp_row = sb("bp_row", [P, D])
        bih_col = sb("bih_col", [P, 6])
        bhh_col = sb("bhh_col", [P, 6])
        brz_col = sb("brz_col", [P, 4])
        slot_col = sb("slot_col", [P, NC])
        input_col = sb("input_col", [P, NC])
        route_col = sb("route_col", [P, 1])
        member = sb("member", [P, 2])
        x1T = sb("x1T", [P, NC, B * T])

        s0 = ExitStack()
        st_qkv = sb("st_qkv", [P, NC, G3], where=s0)
        st_proj = sb("st_proj", [P, NC, D], where=s0)
        st_wq = sb("st_wq", [P, NC, D], where=s0)
        st_wk = sb("st_wk", [P, NC, D], where=s0)
        st_wv = sb("st_wv", [P, NC, D], where=s0)
        st_ih = sb("st_ih", [P, 6, D], where=s0)
        st_hh = sb("st_hh", [P, 6, D], where=s0)
        st_ihT = sb("st_ihT", [P, NC, G3], where=s0)
        st_keys = sb("st_keys", [P, NC, NE * EH], where=s0)
        st_values = sb("st_values", [P, NH, D], where=s0)
        st_esel = sb("st_esel", [NE, D], where=s0)
        s0.close()

        s1 = ExitStack()
        x_in = sb("x_in", [P, 2, NT, D], where=s1)
        xr = sb("xr", [P, 2, NT, D], where=s1)
        xT_hl = sb("xT_hl", [P, 2, NC, T], F32R, where=s1)
        q_hl = sb("q_hl", [P, 2, NC, T], F32R, where=s1)
        q_sep = sb("q_sep", [P, 2, 2, NC, 2, T], F32R, where=s1)
        k_hl = sb("k_hl", [P, 2, 2, NC, T], F32R, where=s1)
        v_sb = sb("v_sb", [P, 2, NT, D], where=s1)
        k_op = sb("k_op", [3 * 32, H // 2, T], F32R, where=s1)
        q_op = sb("q_op", [3 * 32, H // 2, 2, T], F32R, where=s1)
        v_pad = sb("v_pad", [P, NT, H, P], where=s1)
        prob = sb("prob", [P, 2, 2, SQ], where=s1)
        probT = sb("probT", [P, 4, SQ], where=s1)
        neg_max = sb("neg_max", [P, H // 2, NT, 2], where=s1)
        row_sum = sb("row_sum", [P, NT, H], where=s1)
        inv_sum = sb("inv_sum", [P, NT, H], where=s1)
        inv_wide = sb("inv_wide", [P, NT, D], where=s1)
        inv_bc = sb("inv_bc", [P, NC, T], where=s1)
        yn = sb("yn", [P, NC, T], where=s1)
        y_hl = sb("y_hl", [P, 2, NC, T], F32R, where=s1)
        u1 = sb("u1", [P, NT, D], where=s1)
        stats1 = sb("stats1", [P, NT, 6], where=s1)
        mv1 = sb("mv1", [P, NT, 2], where=s1)
        std1 = sb("std1", [P, 2, NT], where=s1)
        s1.close()

        x2 = sb("x2", [P, B * NT, D])
        s2 = ExitStack()
        c_in = sb("c_in", [P, 2, NT, D], where=s2)
        junk = sb("junk", [P, 2, NT, D], where=s2)
        c_ss = sb("c_ss", [P, 2, NT], where=s2)
        c_ms = sb("c_ms", [P, 2, NT], where=s2)
        c_rs = sb("c_rs", [P, 2, NT], where=s2)
        cT_hl = sb("cT_hl", [P, 2, NC, T], F32R, where=s2)
        kT_hl = sb("kT_hl", [P, 2, 2, NC, T], F32R, where=s2)
        vg_hl = sb("vg_hl", [P, 2, 2, 6, D], F32R, where=s2)
        slots = sb("slots", [P, 2, NC, T], where=s2)
        slots_hl = sb("slots_hl", [P, 2, 2, NC, T], F32R, where=s2)
        sq = sb("sq", [P, NC, T], where=s2)
        s_ms = sb("s_ms", [P, 2, NT], where=s2)
        s_rs = sb("s_rs", [P, 2, NT], where=s2)
        rs_bc = sb("rs_bc", [P, 2, T], where=s2)
        attn = sb("attn", [P, 2, NT, T], where=s2)
        attn_hl = sb("attn_hl", [P, 2, 2, NT, T], F32R, where=s2)
        s_max = sb("s_max", [P, 2, NT], where=s2)
        s_sum = sb("s_sum", [P, 2, NT], where=s2)
        s_inv = sb("s_inv", [P, 2, NT], where=s2)
        tot = sb("tot", [P, T], where=s2)
        inv_tot = sb("inv_tot", [P, T], where=s2)
        gate_r = sb("gate_r", [P, NC, T], where=s2)
        gate_z = sb("gate_z", [P, NC, T], where=s2)
        cand = sb("cand", [P, NC, T], where=s2)
        diff = sb("diff", [P, NC, T], where=s2)
        stats2 = sb("stats2", [P, NT, 6], where=s2)
        mv2 = sb("mv2", [P, NT, 2], where=s2)
        std2 = sb("std2", [P, 2, NT], where=s2)
        s2.close()

        s3 = ExitStack()
        x2f = sb("x2f", [P, 2, NT, D], where=s3)
        x2T_hl = sb("x2T_hl", [P, 2, 2, NC, T], F32R, where=s3)
        logT = sb("logT", [NE, T], where=s3)
        prb = sb("prb", [P, NT, 24], where=s3)
        prbx = sb("prbx", [P, NT, 24], where=s3)
        top8 = sb("top8", [P, NT, 8], where=s3)
        gate = sb("gate", [P, NT, NE], where=s3)
        gsum = sb("gsum", [P, NT], where=s3)
        ginv = sb("ginv", [P, NT], where=s3)
        gateT_hl = sb("gateT_hl", [P, 2, T], F32R, where=s3)
        spread = sb("spread", [P, NH, P], F32R, where=s3)
        spread32 = sb("spread32", [P, NH, P], where=s3)
        hid = sb("hid", [P, 2, 2, T], where=s3)
        hid_hl = sb("hid_hl", [P, 2, 2, NH, T], F32R, where=s3)
        u3 = sb("u3", [P, NT, D], where=s3)
        y_out = sb("y_out", [P, 2, NT, D], where=s3)
        stats3 = sb("stats3", [P, NT, 6], where=s3)
        mv3 = sb("mv3", [P, NT, 2], where=s3)
        std3 = sb("std3", [P, 2, NT], where=s3)

        bank = [stack.enter_context(nc.psum_tensor(f"bank{n}", [P, 512], F32)) for n in range(8)]

        def halves(b):
            return bank[b][:, :].rearrange("p (a n) -> p a n", a=2)

        w_in = [sem(f"w_in{n}") for n in range(4)]
        consts = sem("consts")
        prep_mm = sem("prep_mm")
        prep_out = sem("prep_out")
        prep_act = sem("prep_act")
        prep_dve = sem("prep_dve")
        done = [sem(f"phase_done{n}") for n in range(3)]

        x_arr = [event(f"x_arr{j}", 1, 16) for j in range(2)]
        xr_ok = event("xr_ok", 2)
        xT_mm, xT_hi, xT_lo = event("xT_mm", 2), event("xT_hi", 2), event("xT_lo", 2)
        q_mm, q_hi, q_lo = event("q_mm", 2), event("q_hi", 2), event("q_lo", 2)
        k_mm, k_hi, k_lo = event("k_mm", 2), event("k_hi", 2), event("k_lo", 2)
        v_mm, v_ok = event("v_mm", 2), event("v_ok", 2)
        vp_ok = event("vp_ok", 2)
        q_set = event("q_set", 2)
        ops_in = [event(f"ops_in{strip}", 2, 16 * 6) for strip in range(4)]
        s_mm, max_ok, exp_ok = event("s_mm", 32), event("max_ok", 32), event("exp_ok", 32)
        pT_mm = event("pT_mm", 32)
        pT_even, pT_odd = event("pT_even", 16), event("pT_odd", 16)
        pv_mm = event("pv_mm", 32)
        inv_ok, ib_mm, ib_ok = event("inv_ok", 2), event("ib_mm", 2), event("ib_ok", 2)
        yn_ok, y_hi, y_lo = event("yn_ok", 2), event("y_hi", 2), event("y_lo", 2)
        pr_mm, u1_ok = event("pr_mm", 2), event("u1_ok", 2)
        var1, rstd1, x1_ok = event("var1", 2), event("rstd1", 2), event("x1_ok", 2)
        x1T_mm, x1T_ok = event("x1T_mm", 2), event("x1T_ok", 2)
        c_arr = [event(f"c_arr{j}", 1, 16) for j in range(2)]
        c_sq, c_mean, c_rstd, c_ok = event("c_sq", 2), event("c_mean", 2), event("c_rstd", 2), event("c_ok", 2)
        cT_mm, cT_hi, cT_lo = event("cT_mm", 2), event("cT_hi", 2), event("cT_lo", 2)
        kT_mm, kT_hi, kT_lo = event("kT_mm", 2), event("kT_hi", 2), event("kT_lo", 2)
        vg_mm, vg_hi, vg_lo = event("vg_mm", 6), event("vg_hi", 6), event("vg_lo", 6)
        sl_ok, sl_hi, sl_lo = event("sl_ok", 8), event("sl_hi", 6), event("sl_lo", 6)
        sq_ok, sqs_ok = event("sq_ok", UNITS), event("sqs_ok", UNITS)
        ss_mm, ms_ok, rs_ok = event("ss_mm", UNITS), event("ms_ok", UNITS), event("rs_ok", UNITS)
        rb_mm, rb_ok = event("rb_mm", UNITS), event("rb_ok", UNITS)
        sc_mm, sc_ok = event("sc_mm", UNITS), event("sc_ok", UNITS)
        smax_ok, e_ok, z_ok = event("smax_ok", UNITS), event("e_ok", UNITS), event("z_ok", UNITS)
        tt_mm, tt_ok = event("tt_mm", UNITS), event("tt_ok", UNITS)
        at_ok, at_hi, at_lo = event("at_ok", UNITS), event("at_hi", UNITS), event("at_lo", UNITS)
        r_mm, z_mm, hn_mm, xn_mm = (event(n, UNITS) for n in ("r_mm", "z_mm", "hn_mm", "xn_mm"))
        r_ok, zt_ok, g_ok, np_ok, n_ok = (event(n, UNITS) for n in ("r_ok", "zt_ok", "g_ok", "np_ok", "n_ok"))
        uu_ok, uT_mm = event("uu_ok", 2), event("uT_mm", 2)
        var2, rstd2, x2_ok = event("var2", 2), event("rstd2", 2), event("x2_ok", 2)
        xf_ok = event("xf_ok", 2)
        tT_mm, tT_hi, tT_lo = event("tT_mm", 2), event("tT_hi", 2), event("tT_lo", 2)
        lg_mm, lg_ok, lT_mm, lx_ok = event("lg_mm", 2), event("lg_ok", 2), event("lT_mm", 2), event("lx_ok", 2)
        gt_ok, gT_mm, gT_hi, gT_lo = event("gt_ok", 2), event("gT_mm", 2), event("gT_hi", 2), event("gT_lo", 2)
        h_mm, h_relu, gb_mm = event("h_mm", 8), event("h_relu", 8), event("gb_mm", 8)
        h_ok, h_hi, h_lo = event("h_ok", 8), event("h_hi", 8), event("h_lo", 8)
        o_mm, u3_ok = event("o_mm", 2), event("u3_ok", 2)
        var3, rstd3, y_ok = event("var3", 2), event("rstd3", 2), event("y_ok", 2)
        stored = [event(f"stored{j}", 1, 16) for j in range(2)]

        attn_chain, cross_chain, expert_chain = sem("attn_chain"), sem("cross_chain"), sem("expert_chain")
        links = [0]

        def next_link():
            links[0] += 1
            return links[0]


        jobs1 = []
        for j in range(2):
            jobs1 += [(("xT", j), 0, xT_lo, 2, j + 1), (("q", j), 1, q_lo, 2, j + 1),
                      (("k", j), 2, k_lo, 2, j + 1), (("v", j), 0, v_ok, 2, j + 1)]
        for j in range(2):
            for hp in range(H // 2 + 2):
                if hp < H // 2:
                    for qt in range(NT):
                        n = 16 * j + 2 * hp + qt
                        jobs1.append((("s", n), 4 + qt, exp_ok, 32, n + 1))
                if 1 <= hp <= H // 2:
                    for e in range(2):
                        n = 16 * j + 2 * (hp - 1) + e
                        jobs1.append((("pT", n), 6 + e, (pT_even, pT_odd)[e], 16, n // 2 + 1))
                if hp == 2:
                    jobs1.append((("y", j), 3, yn_ok, 2, j + 1))
            jobs1 += [(("ib", j), 1, ib_ok, 2, j + 1), (("pr", j), 2, u1_ok, 2, j + 1),
                      (("x1T", j), 0, x1T_ok, 2, j + 1)]
        jobs2 = []
        for j in range(2):
            jobs2 += [(("cT", j), 0, cT_lo, 2, j + 1), (("kT", j), 1, kT_lo, 2, j + 1)]
            jobs2 += [(("vg", 3 * j + g), 4 + g, vg_lo, 6, 3 * j + g + 1) for g in range(3)]

        def front(u):
            return [(("ss", u), 0, ms_ok, UNITS, u + 1), (("sc", u), 3, sc_ok, UNITS, u + 1), (("rb", u), 1, rb_ok, UNITS, u + 1)]

        def mid(u):
            return [(("r", u), 4, r_ok, UNITS, u + 1), (("z", u), 5, zt_ok, UNITS, u + 1), (("hn", u), 6, g_ok, UNITS, u + 1),
                    (("tt", u), 2, tt_ok, UNITS, u + 1)]

        def back(u):
            return [(("xn", u), 7, np_ok, UNITS, u + 1)]

        jobs2 += front(0) + mid(0)
        for u in range(UNITS):
            jobs2 += (front(u + 1) if u + 1 < UNITS else []) + back(u) + (mid(u + 1) if u + 1 < UNITS else [])
        jobs2 += [(("uT", j), j, x2_ok, 2, j + 1) for j in range(2)]
        jobs3 = []
        for j in range(2):
            jobs3 += [(("tT", j), 0, tT_lo, 2, j + 1), (("lg", j), 1, lg_ok, 2, j + 1),
                      (("lT", j), 2, lx_ok, 2, j + 1), (("gT", j), 3, gT_lo, 2, j + 1)]
            for g in range(4):
                n = 4 * j + g
                jobs3 += [(("h", n), 4 + g % 2, h_relu, 8, n + 1), (("gb", n), 6 + g % 2, h_ok, 8, n + 1)]
        jobs3 += [(("o", j), j, u3_ok, 2, j + 1) for j in range(2)]

        def bank_free(jobs, i, key):
            at = [job[0] for job in jobs].index(key)
            b = jobs[at][1]
            before = [job for job in jobs[:at] if job[1] == b]
            last = [job for job in jobs if job[1] == b][-1]
            _, _, signal, per, k = before[-1] if before else last
            return b, signal, due(per, i, k, back=0 if before else 1)

        def split3(pe, dst, left, right, first, last):
            for n, (a, b) in enumerate(PASSES):
                mm = pe.matmul(dst, left(a), right(b), start=first and n == 0, stop=last and n == 2,
                               skip_group_check=True)
            return mm

        def transpose4(pe, b, src):
            for c in range(2):
                for t in range(2):
                    mm = pe.transpose(halves(b)[:, c, t * P:(t + 1) * P], src(t, c), ident[:, :])
            return mm

        def f32(ap):
            return ap.bitcast(F32)

        block = stack.enter_context(nc.Block())

        @block.sync
        def _(sp):
            for signal, count in events:
                sp.sem_inc(signal, count)
            def rows(w, n):
                return w.rearrange("(c p) n -> p c n", p=P)
            with nc.allow_non_contiguous_dma("biases by column"):
                sp.dma_start(st_qkv[:, :, :], rows(w_qkv, NC)).then_inc(w_in[0], 16)
                sp.dma_start(st_wk[:, :, :], rows(wk, NC)).then_inc(w_in[1], 16)
                sp.dma_start(st_wq[:, :, :], rows(wq, NC)).then_inc(w_in[1], 16)
                sp.dma_start(st_wv[:, :, :], rows(wv, NC)).then_inc(w_in[1], 16)
                sp.dma_start(st_ih[:, :, :], rows(wih, 6)).then_inc(w_in[1], 16)
                sp.dma_start(st_hh[:, :, :], rows(whh, 6)).then_inc(w_in[1], 16)
                sp.dma_start(st_esel[:, :], expert_sel).then_inc(w_in[1], 16)
                sp.dma_start(bq_col[:, :], b_qkv[0:2 * D].rearrange("(c p) -> p c", p=P)).then_inc(w_in[0], 16)
                sp.dma_start(bv_row[:, :], b_qkv[2 * D:3 * D].partition_broadcast(P)).then_inc(w_in[0], 16)
                sp.dma_start(bp_row[:, :], b_proj.partition_broadcast(P)).then_inc(w_in[0], 16)
                sp.dma_start(bih_col[:, :], bih.rearrange("(c p) -> p c", p=P)).then_inc(w_in[2], 16)
                sp.dma_start(bhh_col[:, :], bhh.rearrange("(c p) -> p c", p=P)).then_inc(w_in[2], 16)
                sp.dma_start(slot_col[:, :], slot_w.rearrange("(c p) -> p c", p=P)).then_inc(w_in[2], 16)
                sp.dma_start(input_col[:, :], input_w.rearrange("(c p) -> p c", p=P)).then_inc(w_in[2], 16)
                sp.dma_start(route_col[:, :], route_scale.partition_broadcast(P)).then_inc(w_in[2], 16)
                sp.dma_start(st_proj[:, :, :], rows(w_proj, NC)).then_inc(w_in[3], 16)
                for c in range(NC):
                    sp.dma_start(st_keys[:, c, :].rearrange("p (e h) -> p e h", e=NE),
                                 keys[:, c * P:(c + 1) * P, :].rearrange("e p h -> p e h")).then_inc(w_in[3], 16)
                sp.dma_start(st_values[:, :, :],
                             values.rearrange("e h v -> (e h) v").rearrange("(c p) v -> p c v", p=P)
                             ).then_inc(w_in[3], 16)
            sp.wait_ge(done[0], 4)

            with sp.Fori(0, PAIRS) as i:
                for j in range(2):
                    sp.wait_ge(x1T_ok, due(2, i, j + 1, back=1))
                    sp.sem_inc(passed, 1)
                    sp.dma_start(x_in[:, j, :, :], x[i * 2 + j, :, :].rearrange("(t p) d -> p t d", p=P)).then_inc(x_arr[j], 16)
                for j in range(2):
                    sp.wait_ge(k_lo, due(2, i, j + 1))
                    sp.sem_inc(passed, 1)
                    sp.wait_ge(q_set, due(2, i, j + 1))
                    sp.sem_inc(passed, 1)
                    for strip in range(4):
                        if j:
                            sp.wait_ge(s_mm, due(32, i, 4 * (strip + 1)))
                            sp.sem_inc(passed, 1)
                        else:
                            sp.wait_ge(s_mm, due(32, i, 16 + 4 * (strip + 1), back=1))
                            sp.sem_inc(passed, 1)
                        rows_in = slice(32 * strip, 32 * strip + 32)
                        for quad, part in enumerate((HI, LO, HI)):
                            sp.dma_start(f32(k_op[32 * quad:32 * quad + 32, :, :]).rearrange("p (c s) t -> p c s t", s=4)[:, :, strip, :],
                                         f32(k_hl[rows_in, j, part, :, :])).then_inc(ops_in[strip], 16)
                        for quad, part in enumerate((HI, HI, LO)):
                            sp.dma_start(f32(q_op[32 * quad:32 * quad + 32, :, :, :]).rearrange("p (c s) e t -> p c s (e t)", s=4)[:, :, strip, :],
                                         f32(q_sep[rows_in, j, part, :, :, :]).rearrange("p c e t -> p c (e t)")
                                         ).then_inc(ops_in[strip], 16)
            sp.wait_ge(done[1], 4)
            with sp.Fori(0, PAIRS) as i:
                for j in range(2):
                    sp.wait_ge(cT_mm, due(2, i, j + 1, back=1))
                    sp.sem_inc(passed, 1)
                    sp.dma_start(c_in[:, j, :, :], ctx_in[i * 2 + j, :, :].rearrange("(t p) d -> p t d", p=P)).then_inc(c_arr[j], 16)
            sp.wait_ge(done[2], 4)
            with sp.Fori(0, PAIRS) as i:
                for j in range(2):
                    sp.wait_ge(y_ok, due(2, i, j + 1))
                    sp.sem_inc(passed, 1)
                    sp.dma_start(out[i * 2 + j, :, :].rearrange("(t p) d -> p t d", p=P), y_out[:, j, :, :]).then_inc(stored[j], 16)
            for j in range(2):
                sp.wait_ge(stored[j], 16 * (PAIRS + 1))

        @block.gpsimd
        def _(pool):
            pool.memset(ident[:, :], 0.0).then_inc(consts, 1)
            pool.memset(mask32[:, :], 0.0).then_inc(consts, 1)
            pool.wait_ge(consts, 2)
            pool.affine_select(out=ident[:, :], in_=ident[:, :], compare_op=ALU.not_equal, fill=1.0,
                               base=0, pattern=[[-1, P]], channel_multiplier=1).then_inc(consts, 1)
            pool.affine_select(out=mask32[:, :], in_=mask32[:, :], compare_op=ALU.is_ge, fill=MASKED,
                               base=0, pattern=[[-1, P]], channel_multiplier=1).then_inc(consts, 1)
            pool.wait_ge(consts, 4)
            pool.tensor_copy(ident16[:, :], ident[:, :]).then_inc(consts, 1)
            for e in range(2):
                pool.tensor_copy(mask16[:, e, :], mask32[:, :]).then_inc(consts, 1)
            pool.memset(mean_col[:, :], 1.0 / D).then_inc(consts, 1)
            pool.memset(half_neg[:, :], -0.5).then_inc(consts, 1)
            pool.wait_ge(consts, 9)
            pool.drain().then_inc(done[0], 1)
            pool.wait_ge(done[0], 4)
            pool.memset(v_pad[:, :, :, :], 0.0).then_inc(consts, 1)
            pool.wait_ge(consts, 10)

            def rstd(i, var, ev, std, k, slot):
                pool.wait_ge(var, due(2, i, k))
                pool.tensor_tensor(std[:, 1, :], std[:, 0, :], half_neg[:, :], ALU.pow).then_inc(ev, 1)

            with pool.Fori(0, PAIRS) as i:
                def pre(j):
                    pool.wait_ge(x_arr[j], due(1, i, 1, step=16))
                    pool.wait_ge(u1_ok, due(2, i, j + 1, back=1))
                    for t in range(NT):
                        r = pool.tensor_tensor(xr[:, j, t, :], x_in[:, j, t, :], bp_row[:, :], ALU.add)
                    r.then_inc(xr_ok, 1)
                pre(0)
                pre(1)
                for j in range(2):
                    pool.wait_ge(v_ok, due(2, i, j + 1))
                    if j:
                        pool.wait_ge(pv_mm, due(32, i, 16))
                        pool.sem_inc(passed, 1)
                    else:
                        pool.wait_ge(pv_mm, due(32, i, 32, back=1))
                        pool.sem_inc(passed, 1)
                    for t in range(NT):
                        for c in range(NC):
                            dst = v_pad[:, t, 8 * c:8 * c + 8, :].rearrange("p h n -> p (h n)")
                            diag = bass.AP(tensor=dst.tensor, offset=dst.offset,
                                           ap=[list(dst.ap[0]), [P + DH, 8], [1, DH]])
                            r = pool.tensor_tensor(diag, v_sb[:, j, t, c * P:(c + 1) * P].rearrange("p (h d) -> p h d", d=DH),
                                                   bv_row[:, c * P:(c + 1) * P].rearrange("p (h d) -> p h d", d=DH), ALU.add)
                    r.then_inc(vp_ok, 1)
                    pool.wait_ge(y_hi, due(2, i, j + 1))
                    pool.tensor_tensor(y_hl[:, LO, :, :], yn[:, :, :], f32(y_hl[:, HI, :, :]), ALU.subtract).then_inc(y_lo, 1)
                    rstd(i, var1, rstd1, std1, j + 1, j)
            pool.drain().then_inc(done[1], 1)
            pool.wait_ge(done[1], 4)
            with pool.Fori(0, PAIRS) as i:
                for j in range(2):
                    pool.wait_ge(sl_hi, due(6, i, j + 1))
                    pool.wait_ge(sl_ok, due(8, i, j + 1))
                    pool.tensor_tensor(slots_hl[:, j, LO, :, :], slots[:, j, :, :],
                                                    f32(slots_hl[:, j, HI, :, :]), ALU.subtract).then_inc(sl_lo, 1)
                for j in range(2):
                    pool.wait_ge(c_mean, due(2, i, j + 1))
                    pool.tensor_tensor(c_rs[:, j, :], c_ms[:, j, :], half_neg[:, :], ALU.pow).then_inc(c_rstd, 1)

                def norm(u):
                    j = u % 2
                    pool.wait_ge(ms_ok, due(UNITS, i, u + 1))
                    pool.tensor_tensor(s_rs[:, j, :], s_ms[:, j, :], half_neg[:, :], ALU.pow).then_inc(rs_ok, 1)

                def attn_lo(u):
                    j = u % 2
                    pool.wait_ge(at_hi, due(UNITS, i, u + 1))
                    pool.tensor_tensor(attn_hl[:, j, LO, :, :], attn[:, j, :, :],
                                                    f32(attn_hl[:, j, HI, :, :]), ALU.subtract).then_inc(at_lo, 1)
                norm(0)
                for u in range(UNITS):
                    if u + 1 < UNITS:
                        norm(u + 1)
                    attn_lo(u)
                    if u < UNITS - 2:
                        j = u % 2
                        pool.wait_ge(sl_hi, due(6, i, 2 + u + 1))
                        pool.tensor_tensor(slots_hl[:, j, LO, :, :], slots[:, j, :, :],
                                                        f32(slots_hl[:, j, HI, :, :]), ALU.subtract).then_inc(sl_lo, 1)
                for j in range(2):
                    rstd(i, var2, rstd2, std2, j + 1, j)
            pool.drain().then_inc(done[2], 1)
            pool.wait_ge(done[2], 4)
            pool.memset(spread32[:, :, :], 0.0).then_inc(consts, 1)
            pool.memset(f32(gateT_hl[:, :, :]), 0.0).then_inc(consts, 1)
            pool.memset(prb[:, :, NE:], -1.0).then_inc(consts, 1)
            pool.wait_ge(consts, 13)
            for n, off in enumerate((0, 32)):
                rows = spread32[off:off + 32, :, :].rearrange("p c (e m) -> p (c e) m", e=2)
                pool.affine_select(out=rows, in_=rows, compare_op=ALU.not_equal, fill=1.0, base=0,
                                   pattern=[[-1, NE], [0, EH]], channel_multiplier=1).then_inc(consts, 1)
            pool.wait_ge(consts, 15)
            pool.tensor_copy(spread[:, :, :], spread32[:, :, :]).then_inc(consts, 1)
            with pool.Fori(0, PAIRS) as i:
                for j in range(2):
                    for g in range(4):
                        n = 4 * j + g
                        pool.wait_ge(h_hi, due(8, i, n + 1))
                        pool.tensor_tensor(hid_hl[:, j, LO, 2 * g:2 * g + 2, :], hid[:, g % 2, :, :],
                                                       f32(hid_hl[:, j, HI, 2 * g:2 * g + 2, :]), ALU.subtract).then_inc(h_lo, 1)
                for j in range(2):
                    rstd(i, var3, rstd3, std3, j + 1, j)

        @block.scalar
        def _(act):
            def copy(dst, src, **kw):
                return act.activation(dst, src, ACT.Copy, **kw)
            act.wait_ge(w_in[0], 64)
            copy(wqkv_hl[:, HI, :, 0:D], st_qkv[:, :, 0:D], scale=float(DH) ** -0.5).then_inc(prep_act, 1)
            copy(wqkv_hl[:, HI, :, D:], st_qkv[:, :, D:]).then_inc(prep_act, 1)
            act.wait_ge(w_in[3], 64)
            copy(wproj_hl[:, HI, :, :], st_proj[:, :, :]).then_inc(prep_act, 1)
            copy(keys_hl[:, HI, :, :], st_keys[:, :, :]).then_inc(prep_act, 1)
            copy(values_hl[:, HI, :, :], st_values[:, :, :]).then_inc(prep_act, 1)
            act.drain().then_inc(done[0], 1)
            act.wait_ge(done[0], 4)

            with act.Fori(0, PAIRS) as i:
                for j in range(2):
                    act.wait_ge(xT_mm, due(2, i, j + 1))
                    if j:
                        act.wait_ge(v_mm, due(2, i, 1))
                    else:
                        act.wait_ge(v_mm, due(2, i, 2, back=1))
                    copy(xT_hl[:, HI, :, :], halves(0)).then_inc(xT_hi, 1)
                    act.wait_ge(q_mm, due(2, i, j + 1))
                    if j:
                        act.wait_ge(q_set, due(2, i, 1))
                    else:
                        act.wait_ge(q_set, due(2, i, 2, back=1))
                    for c in range(NC):
                        r = act.activation(q_hl[:, HI, c, :], halves(1)[:, c, :], ACT.Identity, bias=bq_col[:, c:c + 1])
                    r.then_inc(q_hi, 1)
                    act.wait_ge(k_mm, due(2, i, j + 1))
                    for strip in range(4):
                        act.wait_ge(ops_in[strip], due(2, i, j + 1, back=1, step=16 * 6))
                    for c in range(NC):
                        r = act.activation(k_hl[:, j, HI, c, :], halves(2)[:, c, :], ACT.Identity, bias=bq_col[:, NC + c:NC + c + 1])
                    r.then_inc(k_hi, 1)
                for j in range(2):
                    def probs_out(h):
                        n = 16 * j + h
                        act.wait_ge(pT_mm, due(32, i, n + 1))
                        if n >= 4:
                            act.wait_ge(pv_mm, due(32, i, n - 3))
                        else:
                            act.wait_ge(pv_mm, due(32, i, 32 + n - 3, back=1))
                        copy(probT[:, h % 4, :], bank[7][:, 0:SQ]).then_inc(pT_odd, 1)
                    for hp in range(H // 2 + 1):
                        if hp < H // 2:
                            for qt in range(NT):
                                n = 16 * j + 2 * hp + qt
                                lo, size = (0, P) if qt == 0 else (P, 2 * P)
                                act.wait_ge(max_ok, due(32, i, n + 1))
                                at = 16 * j + 2 * hp - 2
                                if at >= 2:
                                    act.wait_ge(pT_mm, due(32, i, at))
                                else:
                                    act.wait_ge(pT_mm, due(32, i, 32 + at, back=1))
                                for e in range(2):
                                    r = act.activation(prob[:, hp % 2, e, lo:lo + size], halves(4 + qt)[:, e, 0:size],
                                                       ACT.Exp, bias=neg_max[:, hp, qt, e:e + 1],
                                                       accum_out=row_sum[:, qt, head(2 * hp + e):head(2 * hp + e) + 1])
                                r.then_inc(exp_ok, 1)
                        if hp >= 1:
                            probs_out(2 * hp - 1)
                    act.wait_ge(ib_mm, due(2, i, j + 1))
                    copy(inv_bc[:, :, :], halves(1)).then_inc(ib_ok, 1)
                    act.wait_ge(yn_ok, due(2, i, j + 1))
                    copy(y_hl[:, HI, :, :], yn[:, :, :]).then_inc(y_hi, 1)
                    act.wait_ge(x1T_mm, due(2, i, j + 1))
                    copy(x1T[:, :, bass.ds(i * (2 * T) + j * T, T)], halves(0)).then_inc(x1T_ok, 1)
            act.drain().then_inc(done[1], 1)
            act.wait_ge(done[1], 4)
            with act.Fori(0, PAIRS) as i:
                for j in range(2):
                    act.wait_ge(hn_mm, due(UNITS, i, 5 + j, back=1))
                    copy(slots_hl[:, j, HI, :, :], x1T[:, :, bass.ds(i * (2 * T) + j * T, T)]).then_inc(sl_hi, 1)
                for j in range(2):
                    act.wait_ge(c_arr[j], due(1, i, 1, step=16))
                    for t in range(NT):
                        r = act.activation(junk[:, j, t, :], c_in[:, j, t, :], ACT.Square, accum_out=c_ss[:, j, t:t + 1])
                    r.then_inc(c_sq, 1)
                for j in range(2):
                    act.wait_ge(cT_mm, due(2, i, j + 1))
                    if j:
                        act.wait_ge(vg_mm, due(6, i, 3))
                    else:
                        act.wait_ge(vg_mm, due(6, i, 6, back=1))
                    copy(cT_hl[:, HI, :, :], halves(0)).then_inc(cT_hi, 1)
                    act.wait_ge(kT_mm, due(2, i, j + 1))
                    for c in range(NC):
                        r = act.activation(kT_hl[:, j, HI, c, :], halves(1)[:, c, :], ACT.Identity, scale=slot_col[:, c:c + 1])
                    r.then_inc(kT_hi, 1)
                    for g in range(3):
                        act.wait_ge(vg_mm, due(6, i, 3 * j + g + 1))
                        copy(vg_hl[:, j, HI, 2 * g:2 * g + 2, :], halves(4 + g)).then_inc(vg_hi, 1)

                def start(u):
                    j = u % 2
                    act.wait_ge(sl_ok, due(8, i, u + 1))
                    if u:
                        act.wait_ge(sqs_ok, due(UNITS, i, u))
                    else:
                        act.wait_ge(sqs_ok, due(UNITS, i, UNITS, back=1))
                    act.activation(sq[:, :, :], slots[:, j, :, :], ACT.Square).then_inc(sq_ok, 1)

                def scale(u):
                    act.wait_ge(rb_mm, due(UNITS, i, u + 1))
                    copy(rs_bc[:, u % 2, :], bank[1][:, 0:T]).then_inc(rb_ok, 1)

                def soft(u):
                    j = u % 2
                    act.wait_ge(smax_ok, due(UNITS, i, u + 1))
                    for t in range(NT):
                        r = act.activation(attn[:, j, t, :], attn[:, j, t, :], ACT.Exp, bias=s_max[:, j, t:t + 1],
                                           accum_out=s_sum[:, j, t:t + 1])
                    r.then_inc(e_ok, 1)

                def attn_hi(u):
                    j = u % 2
                    act.wait_ge(at_ok, due(UNITS, i, u + 1))
                    copy(attn_hl[:, j, HI, :, :], attn[:, j, :, :]).then_inc(at_hi, 1)

                def reset_gate(u):
                    act.wait_ge(r_mm, due(UNITS, i, u + 1))
                    for c in range(NC):
                        r = act.activation(gate_r[:, c, :], halves(4)[:, c, :], ACT.Tanh, scale=0.5, bias=brz_col[:, c:c + 1])
                    r.then_inc(r_ok, 1)

                def gates(u):
                    act.wait_ge(np_ok, due(UNITS, i, u + 1))
                    for c in range(NC):
                        r = act.activation(cand[:, c, :], gate_r[:, c, :], ACT.Tanh, bias=bih_col[:, 2 * NC + c:2 * NC + c + 1])
                    r.then_inc(n_ok, 1)
                    act.wait_ge(z_mm, due(UNITS, i, u + 1))
                    for c in range(NC):
                        r = act.activation(gate_z[:, c, :], halves(5)[:, c, :], ACT.Tanh, scale=0.5, bias=brz_col[:, NC + c:NC + c + 1])
                    r.then_inc(zt_ok, 1)

                def slots_hi(u):
                    j = u % 2
                    if u < UNITS - 2:
                        act.wait_ge(sl_ok, due(8, i, 2 + u + 1))
                        copy(slots_hl[:, j, HI, :, :], slots[:, j, :, :]).then_inc(sl_hi, 1)
                start(0)
                scale(0)
                soft(0)
                start(1)
                attn_hi(0)
                for u in range(UNITS):
                    if u + 1 < UNITS:
                        scale(u + 1)
                    reset_gate(u)
                    if u + 1 < UNITS:
                        soft(u + 1)
                    gates(u)
                    if u + 2 < UNITS:
                        start(u + 2)
                    slots_hi(u)
                    if u + 1 < UNITS:
                        attn_hi(u + 1)
            act.drain().then_inc(done[2], 1)
            act.wait_ge(done[2], 4)
            with act.Fori(0, PAIRS) as i:
                for j in range(2):
                    act.wait_ge(u3_ok, due(2, i, j + 1, back=1))
                    copy(x2f[:, j, :, :], x2[:, bass.ds(i * (2 * NT) + j * NT, NT), :]).then_inc(xf_ok, 1)
                for j in range(2):
                    act.wait_ge(tT_mm, due(2, i, j + 1))
                    act.wait_ge(h_mm, due(8, i, 4 * j + 4, back=1))
                    copy(x2T_hl[:, j, HI, :, :], halves(0)).then_inc(tT_hi, 1)
                    act.wait_ge(lT_mm, due(2, i, j + 1))
                    if j:
                        act.wait_ge(gt_ok, due(2, i, 1))
                    else:
                        act.wait_ge(gt_ok, due(2, i, 2, back=1))
                    act.activation(prb[:, :, 0:NE], bank[2][:, 0:NT * NE].rearrange("p (t e) -> p t e", t=NT),
                                                ACT.Exp, scale=-1.0).then_inc(lx_ok, 1)
                    act.wait_ge(gT_mm, due(2, i, j + 1))
                    if j:
                        act.wait_ge(gb_mm, due(8, i, 4))
                    else:
                        act.wait_ge(gb_mm, due(8, i, 8, back=1))
                    copy(gateT_hl[0:NE, 0, :], bank[3][0:NE, 0:T]).then_inc(gT_hi, 1)
                    for g in range(4):
                        n = 4 * j + g
                        act.wait_ge(h_mm, due(8, i, n + 1))
                        if n >= 2:
                            act.wait_ge(h_lo, due(8, i, n - 1))
                        else:
                            act.wait_ge(h_lo, due(8, i, 8 + n - 1, back=1))
                        act.activation(hid[:, g % 2, :, :], halves(4 + g % 2), ACT.Relu).then_inc(h_relu, 1)
                        act.wait_ge(h_ok, due(8, i, n + 1))
                        act.wait_ge(o_mm, due(2, i, j + 1, back=1))
                        copy(hid_hl[:, j, HI, 2 * g:2 * g + 2, :], hid[:, g % 2, :, :]).then_inc(h_hi, 1)

        @block.vector
        def _(dve):
            def sub_hi(dst, src, hi):
                return dve.tensor_tensor(dst, src, f32(hi), ALU.subtract)

            prep = [0]

            def step(ins):
                ins.then_inc(prep_dve, 1)
                prep[0] += 1
                dve.wait_ge(prep_dve, prep[0])

            dve.wait_ge(prep_act, 1)
            step(dve.scalar_tensor_tensor(wqkv_hl[:, LO, :, 0:D], st_qkv[:, :, 0:D], float(DH) ** -0.5,
                                          f32(wqkv_hl[:, HI, :, 0:D]), ALU.mult, ALU.subtract))
            dve.wait_ge(prep_act, 2)
            step(sub_hi(wqkv_hl[:, LO, :, D:], st_qkv[:, :, D:], wqkv_hl[:, HI, :, D:]))
            step(dve.tensor_scalar(bq_col[:, 0:NC], bq_col[:, 0:NC], float(DH) ** -0.5, None, ALU.mult))
            dve.wait_ge(prep_act, 3)
            step(sub_hi(wproj_hl[:, LO, :, :], st_proj[:, :, :], wproj_hl[:, HI, :, :]))
            dve.wait_ge(prep_act, 4)
            step(sub_hi(keys_hl[:, LO, :, :], st_keys[:, :, :], keys_hl[:, HI, :, :]))
            dve.wait_ge(prep_act, 5)
            step(sub_hi(values_hl[:, LO, :, :], st_values[:, :, :], values_hl[:, HI, :, :]))
            dve.wait_ge(w_in[2], 80)
            step(dve.tensor_tensor(brz_col[:, :], bih_col[:, 0:4], bhh_col[:, 0:4], ALU.add))
            step(dve.tensor_scalar(brz_col[:, :], brz_col[:, :], 0.5, None, ALU.mult))
            step(dve.tensor_scalar(slot_col[:, :], slot_col[:, :], float(D) ** -0.5, None, ALU.mult))
            dve.wait_ge(consts, 9)
            for e in range(2):
                step(dve.tensor_reduce(member[:, e:e + 1], ident[:, :].rearrange("p (h e d) -> p e h d", e=2, d=DH)[:, e, :, :],
                                       AX.XY, ALU.add))
            filled = [0]

            def bank_full():
                filled[0] += 1
                dve.wait_ge(prep_mm, filled[0])

            def into_hl(hi, lo, src, scale=None):
                n = src.free_size() if callable(src.free_size) else src.free_size
                if scale is None:
                    step(dve.tensor_copy(hi, src))
                    step(dve.tensor_tensor(lo, src, f32(hi), ALU.subtract))
                else:
                    step(dve.tensor_scalar(hi, src, scale, None, ALU.mult))
                    step(dve.scalar_tensor_tensor(lo, src, scale, f32(hi), ALU.mult, ALU.subtract))
            for c in range(NC):
                for half in range(2):
                    n0 = half * 4
                    m = 4 if half == 0 else 2
                    bank_full()
                    into_hl(whhT_hl[:, HI, c, n0 * P:(n0 + m) * P], whhT_hl[:, LO, c, n0 * P:(n0 + m) * P], bank[2 * c + half][:, 0:m * P])
            for c in range(NC):
                for half in range(2):
                    n0 = half * 4
                    m = 4 if half == 0 else 2
                    bank_full()
                    step(dve.tensor_copy(st_ihT[:, c, n0 * P:(n0 + m) * P], bank[4 + 2 * c + half][:, 0:m * P]))
            dve.drain().then_inc(prep_out, 1)
            bank_full()
            into_hl(eselT_hl[:, HI, :, :], eselT_hl[:, LO, :, :], bank[0][:, 0:NC * NE].rearrange("p (c e) -> p c e", c=NC))
            for c in range(NC):
                bank_full()
                into_hl(qk_w_hl[:, HI, c, :], qk_w_hl[:, LO, c, :], bank[1 + c][:, 0:D], input_col[:, c:c + 1])
            for c in range(NC):
                bank_full()
                into_hl(v_w_hl[:, HI, c, 0:512], v_w_hl[:, LO, c, 0:512], bank[3 + 2 * c][:, :], input_col[:, c:c + 1])
                bank_full()
                into_hl(v_w_hl[:, HI, c, 512:], v_w_hl[:, LO, c, 512:], bank[4 + 2 * c][:, 0:D], input_col[:, c:c + 1])
            dve.drain().then_inc(done[0], 1)
            dve.wait_ge(done[0], 4)

            def layer_norm(i, chain, per, src, stats, mv, std, var, rstd, k, result, ok):
                for t in range(NT):
                    ins = dve.bn_stats(stats[:, t, :], src(t))
                ins.then_inc(chain, 1)
                dve.wait_ge(chain, i * per + next_link())
                dve.sem_inc(passed, 1)
                for t in range(NT):
                    ins = dve.bn_aggr(mv[:, t, :], stats[:, t, :])
                ins.then_inc(chain, 1)
                dve.wait_ge(chain, i * per + next_link())
                dve.tensor_scalar(std[:, 0, :], mv[:, :, 1], LN_EPS, None, ALU.add).then_inc(var, 1)
                dve.wait_ge(rstd, due(2, i, k))
                for t in range(NT):
                    ins = dve.tensor_scalar(result(t), src(t), mv[:, t, 0:1], std[:, 1, t:t + 1], ALU.subtract, ALU.mult)
                ins.then_inc(ok, 1)

            with dve.Fori(0, PAIRS) as i:
                links[0] = 0
                for j in range(2):
                    dve.wait_ge(xT_hi, due(2, i, j + 1))
                    sub_hi(xT_hl[:, LO, :, :], halves(0), xT_hl[:, HI, :, :]).then_inc(xT_lo, 1)
                    dve.wait_ge(q_hi, due(2, i, j + 1))
                    for c in range(NC):
                        r = dve.scalar_tensor_tensor(q_hl[:, LO, c, :], halves(1)[:, c, :], bq_col[:, c:c + 1],
                                                     f32(q_hl[:, HI, c, :]), ALU.add, ALU.subtract)
                    r.then_inc(q_lo, 1)
                    dve.wait_ge(q_lo, due(2, i, j + 1))
                    for strip in range(4):
                        dve.wait_ge(ops_in[strip], due(2, i, j + 1, back=1, step=16 * 6))
                    for e in range(2):
                        r = dve.tensor_scalar(q_sep[:, j, :, :, e, :].rearrange("p a c t -> p (a c) t"),
                                              f32(q_hl[:, :, :, :]).rearrange("p a c t -> p (a c) t"),
                                              member[:, e:e + 1], None, ALU.mult)
                    r.then_inc(q_set, 1)
                    dve.wait_ge(k_hi, due(2, i, j + 1))
                    for c in range(NC):
                        r = dve.scalar_tensor_tensor(k_hl[:, j, LO, c, :], halves(2)[:, c, :], bq_col[:, NC + c:NC + c + 1],
                                                     f32(k_hl[:, j, HI, c, :]), ALU.add, ALU.subtract)
                    r.then_inc(k_lo, 1)
                    dve.wait_ge(v_mm, due(2, i, j + 1))
                    dve.wait_ge(vp_ok, due(2, i, j + 1, back=1))
                    for t in range(NT):
                        r = dve.tensor_copy(v_sb[:, j, t, :], halves(0)[:, t, :])
                    r.then_inc(v_ok, 1)
                for j in range(2):
                    def probs_out(h):
                        n = 16 * j + h
                        dve.wait_ge(pT_mm, due(32, i, n + 1))
                        if n >= 4:
                            dve.wait_ge(pv_mm, due(32, i, n - 3))
                        else:
                            dve.wait_ge(pv_mm, due(32, i, 32 + n - 3, back=1))
                        dve.tensor_copy(probT[:, h % 4, :], bank[6][:, 0:SQ]).then_inc(pT_even, 1)
                    for hp in range(H // 2 + 1):
                        if hp < H // 2:
                            for qt in range(NT):
                                n = 16 * j + 2 * hp + qt
                                dve.wait_ge(s_mm, due(32, i, n + 1))
                                size = P if qt == 0 else 2 * P
                                dve.wait_ge(exp_ok, due(32, i, n - 15 if n >= 16 else n + 17, back=0 if n >= 16 else 1))
                                dve.tensor_reduce(neg_max[:, hp, qt, :], halves(4 + qt)[:, :, 0:size],
                                                                AX.X, ALU.max, negate=True).then_inc(max_ok, 1)
                        if hp >= 1:
                            probs_out(2 * hp - 2)
                    dve.wait_ge(exp_ok, due(32, i, 16 * (j + 1)))
                    dve.reciprocal(inv_sum[:, :, :], row_sum[:, :, :]).then_inc(attn_chain, 1)
                    dve.wait_ge(attn_chain, i * ATTN_LINKS + next_link())
                    dve.tensor_copy(inv_wide[:, :, :].rearrange("p t (h d) -> p (t h) d", d=DH),
                                                  inv_sum[:, :, :].rearrange("p t h -> p (t h)").unsqueeze(2)
                                                  .to_broadcast([P, NT * H, DH])).then_inc(inv_ok, 1)
                    dve.wait_ge(ib_ok, due(2, i, j + 1))
                    dve.wait_ge(pv_mm, due(32, i, 16 * (j + 1)))
                    dve.tensor_tensor(yn[:, :, :], halves(3), inv_bc[:, :, :], ALU.mult).then_inc(yn_ok, 1)
                    dve.wait_ge(pr_mm, due(2, i, j + 1))
                    dve.wait_ge(xr_ok, due(2, i, j + 1))
                    dve.tensor_tensor(u1[:, :, :], halves(2), xr[:, j, :, :], ALU.add).then_inc(u1_ok, 1)
                    dve.wait_ge(u1_ok, due(2, i, j + 1))
                    layer_norm(i, attn_chain, ATTN_LINKS, lambda t: u1[:, t, :], stats1, mv1, std1, var1, rstd1, j + 1,
                               lambda t: u1[:, t, :], x1_ok)
                assert links[0] == ATTN_LINKS
            dve.drain().then_inc(done[1], 1)
            dve.wait_ge(done[1], 4)

            with dve.Fori(0, PAIRS) as i:
                links[0] = 0
                for j in range(2):
                    dve.tensor_copy(slots[:, j, :, :], x1T[:, :, bass.ds(i * (2 * T) + j * T, T)]).then_inc(sl_ok, 1)
                for j in range(2):
                    dve.wait_ge(c_sq, due(2, i, j + 1))
                    dve.tensor_scalar(c_ms[:, j, :], c_ss[:, j, :], 1.0 / D, RMS_EPS, ALU.mult, ALU.add).then_inc(c_mean, 1)
                    dve.wait_ge(c_rstd, due(2, i, j + 1))
                    for t in range(NT):
                        r = dve.tensor_scalar(c_in[:, j, t, :], c_in[:, j, t, :], c_rs[:, j, t:t + 1], None, ALU.mult)
                    r.then_inc(c_ok, 1)
                for j in range(2):
                    dve.wait_ge(cT_hi, due(2, i, j + 1))
                    sub_hi(cT_hl[:, LO, :, :], halves(0), cT_hl[:, HI, :, :]).then_inc(cT_lo, 1)
                    dve.wait_ge(kT_hi, due(2, i, j + 1))
                    for c in range(NC):
                        r = dve.scalar_tensor_tensor(kT_hl[:, j, LO, c, :], halves(1)[:, c, :], slot_col[:, c:c + 1],
                                                     f32(kT_hl[:, j, HI, c, :]), ALU.mult, ALU.subtract)
                    r.then_inc(kT_lo, 1)
                    for g in range(3):
                        dve.wait_ge(vg_hi, due(6, i, 3 * j + g + 1))
                        sub_hi(vg_hl[:, j, LO, 2 * g:2 * g + 2, :], halves(4 + g), vg_hl[:, j, HI, 2 * g:2 * g + 2, :]).then_inc(vg_lo, 1)

                def start(u):
                    dve.wait_ge(sq_ok, due(UNITS, i, u + 1))
                    dve.tensor_tensor(sq[:, 0, :], sq[:, 0, :], sq[:, 1, :], ALU.add).then_inc(sqs_ok, 1)

                def mean_square(u):
                    j = u % 2
                    dve.wait_ge(ss_mm, due(UNITS, i, u + 1))
                    dve.tensor_scalar(s_ms[:, j, :], bank[0][:, 0:NT], RMS_EPS, None, ALU.add).then_inc(ms_ok, 1)

                def soft(u):
                    j = u % 2
                    dve.wait_ge(sc_mm, due(UNITS, i, u + 1))
                    dve.wait_ge(rb_ok, due(UNITS, i, u + 1))
                    for t in range(NT):
                        r = dve.tensor_tensor(attn[:, j, t, :], halves(3)[:, t, :], rs_bc[:, j, :], ALU.mult)
                    r.then_inc(sc_ok, 1)
                    dve.wait_ge(sc_ok, due(UNITS, i, u + 1))
                    dve.tensor_reduce(s_max[:, j, :], attn[:, j, :, :], AX.X, ALU.max, negate=True).then_inc(smax_ok, 1)

                def soft_sum(u):
                    j = u % 2
                    dve.wait_ge(e_ok, due(UNITS, i, u + 1))
                    dve.reciprocal(s_inv[:, j, :], s_sum[:, j, :]).then_inc(z_ok, 1)

                def totals(u):
                    dve.wait_ge(tt_mm, due(UNITS, i, u + 1))
                    dve.tensor_scalar(tot[:, :], bank[2][:, 0:T], RMS_EPS, None, ALU.add).then_inc(tt_ok, 1)
                    dve.wait_ge(tt_ok, due(UNITS, i, u + 1))
                    dve.reciprocal(inv_tot[:, :], tot[:, :]).then_inc(cross_chain, 1)

                def weights(u):
                    j = u % 2
                    dve.wait_ge(cross_chain, i * CROSS_LINKS + next_link())
                    for t in range(NT):
                        r = dve.scalar_tensor_tensor(attn[:, j, t, :], attn[:, j, t, :], s_inv[:, j, t:t + 1], inv_tot[:, :],
                                                     ALU.mult, ALU.mult)
                    r.then_inc(at_ok, 1)

                def reset_gate(u):
                    dve.wait_ge(r_ok, due(UNITS, i, u + 1))
                    dve.tensor_scalar(gate_r[:, :, :], gate_r[:, :, :], 0.5, 0.5, ALU.mult, ALU.add).then_inc(cross_chain, 1)
                    dve.wait_ge(cross_chain, i * CROSS_LINKS + next_link())
                    dve.wait_ge(hn_mm, due(UNITS, i, u + 1))
                    for c in range(NC):
                        r = dve.scalar_tensor_tensor(gate_r[:, c, :], halves(6)[:, c, :], bhh_col[:, 2 * NC + c:2 * NC + c + 1],
                                                     gate_r[:, c, :], ALU.add, ALU.mult)
                    r.then_inc(g_ok, 1)

                def gates(u):
                    j = u % 2
                    dve.wait_ge(g_ok, due(UNITS, i, u + 1))
                    dve.wait_ge(xn_mm, due(UNITS, i, u + 1))
                    dve.tensor_tensor(gate_r[:, :, :], halves(7), gate_r[:, :, :], ALU.add).then_inc(np_ok, 1)
                    dve.wait_ge(n_ok, due(UNITS, i, u + 1))
                    dve.tensor_tensor(diff[:, :, :], slots[:, j, :, :], cand[:, :, :], ALU.subtract).then_inc(cross_chain, 1)
                    dve.wait_ge(cross_chain, i * CROSS_LINKS + next_link())
                    dve.wait_ge(zt_ok, due(UNITS, i, u + 1))
                    dve.scalar_tensor_tensor(diff[:, :, :], gate_z[:, :, :], 1.0, diff[:, :, :], ALU.add, ALU.mult).then_inc(cross_chain, 1)
                    dve.wait_ge(cross_chain, i * CROSS_LINKS + next_link())
                    dve.scalar_tensor_tensor(slots[:, j, :, :], diff[:, :, :], 0.5, cand[:, :, :], ALU.mult, ALU.add).then_inc(sl_ok, 1)

                def between(u):
                    if u + 1 < UNITS:
                        start(u + 1)
                    if u < UNITS:
                        totals(u)
                    if u + 1 < UNITS:
                        mean_square(u + 1)
                    if u < UNITS:
                        weights(u)
                start(0)
                mean_square(0)
                soft(0)
                soft_sum(0)
                between(0)
                for u in range(UNITS):
                    if u + 1 < UNITS:
                        soft(u + 1)
                    reset_gate(u)
                    if u + 1 < UNITS:
                        soft_sum(u + 1)
                    gates(u)
                    between(u + 1)
                for j in range(2):
                    dve.wait_ge(sl_ok, due(8, i, 7 + j))
                    dve.tensor_tensor(slots[:, j, :, :], slots[:, j, :, :],
                                                   x1T[:, :, bass.ds(i * (2 * T) + j * T, T)], ALU.add).then_inc(uu_ok, 1)
                for j in range(2):
                    dve.wait_ge(uT_mm, due(2, i, j + 1))
                    layer_norm(i, cross_chain, CROSS_LINKS, lambda t: halves(j)[:, t, :], stats2, mv2, std2, var2, rstd2, j + 1,
                               lambda t: x2[:, bass.ds(i * (2 * NT) + j * NT + t, 1), :], x2_ok)
                assert links[0] == CROSS_LINKS
            dve.drain().then_inc(done[2], 1)
            dve.wait_ge(done[2], 4)

            with dve.Fori(0, PAIRS) as i:
                links[0] = 0
                for j in range(2):
                    dve.wait_ge(tT_hi, due(2, i, j + 1))
                    sub_hi(x2T_hl[:, j, LO, :, :], halves(0), x2T_hl[:, j, HI, :, :]).then_inc(tT_lo, 1)
                    dve.wait_ge(lg_mm, due(2, i, j + 1))
                    dve.tensor_copy(logT[:, :], bank[1][0:NE, 0:T]).then_inc(lg_ok, 1)
                    dve.wait_ge(lx_ok, due(2, i, j + 1))
                    dve.tensor_scalar(prb[:, :, 0:NE], prb[:, :, 0:NE], 1.0, None, ALU.add).then_inc(expert_chain, 1)
                    dve.wait_ge(expert_chain, i * EXPERT_LINKS + next_link())
                    dve.reciprocal(prb[:, :, 0:NE], prb[:, :, 0:NE]).then_inc(expert_chain, 1)
                    dve.wait_ge(expert_chain, i * EXPERT_LINKS + next_link())
                    dve.sem_inc(passed, 1)
                    for t in range(NT):
                        r = dve.max(top8[:, t, :], prb[:, t, 0:NE])
                    r.then_inc(expert_chain, 1)
                    dve.wait_ge(expert_chain, i * EXPERT_LINKS + next_link())
                    dve.memset(top8[:, :, TOPK:], -1.0).then_inc(expert_chain, 1)
                    dve.wait_ge(expert_chain, i * EXPERT_LINKS + next_link())
                    dve.sem_inc(passed, 1)
                    for t in range(NT):
                        r = dve.match_replace(prbx[:, t, :], top8[:, t, :], prb[:, t, :], 0.0)
                    r.then_inc(expert_chain, 1)
                    dve.wait_ge(expert_chain, i * EXPERT_LINKS + next_link())
                    dve.tensor_tensor(gate[:, :, :], prb[:, :, 0:NE], prbx[:, :, 0:NE], ALU.subtract).then_inc(expert_chain, 1)
                    dve.wait_ge(expert_chain, i * EXPERT_LINKS + next_link())
                    dve.tensor_reduce(gsum[:, :], gate[:, :, :], AX.X, ALU.add).then_inc(expert_chain, 1)
                    dve.wait_ge(expert_chain, i * EXPERT_LINKS + next_link())
                    dve.tensor_scalar(gsum[:, :], gsum[:, :], 1e-9, None, ALU.max).then_inc(expert_chain, 1)
                    dve.wait_ge(expert_chain, i * EXPERT_LINKS + next_link())
                    dve.reciprocal(ginv[:, :], gsum[:, :]).then_inc(expert_chain, 1)
                    dve.wait_ge(expert_chain, i * EXPERT_LINKS + next_link())
                    for t in range(NT):
                        r = dve.tensor_scalar(gate[:, t, :], gate[:, t, :], ginv[:, t:t + 1], route_col[:, 0:1], ALU.mult, ALU.mult)
                    r.then_inc(gt_ok, 1)
                    dve.wait_ge(gT_hi, due(2, i, j + 1))
                    sub_hi(gateT_hl[32:32 + NE, 0, :], bank[3][0:NE, 0:T], gateT_hl[0:NE, 0, :]).then_inc(gT_lo, 1)
                    for g in range(4):
                        n = 4 * j + g
                        dve.wait_ge(h_relu, due(8, i, n + 1))
                        dve.wait_ge(gb_mm, due(8, i, n + 1))
                        dve.tensor_tensor(hid[:, g % 2, :, :], halves(6 + g % 2), hid[:, g % 2, :, :], ALU.mult).then_inc(h_ok, 1)
                for j in range(2):
                    dve.wait_ge(o_mm, due(2, i, j + 1))
                    dve.wait_ge(y_ok, due(2, i, 1 if j else 2, back=1 - j))
                    dve.tensor_tensor(u3[:, :, :], halves(j), x2f[:, j, :, :], ALU.add).then_inc(u3_ok, 1)
                    dve.wait_ge(u3_ok, due(2, i, j + 1))
                    dve.wait_ge(stored[j], due(1, i, 1, back=1, step=16))
                    layer_norm(i, expert_chain, EXPERT_LINKS, lambda t: u3[:, t, :], stats3, mv3, std3, var3, rstd3, j + 1,
                               lambda t: y_out[:, j, t, :], y_ok)
                assert links[0] == EXPERT_LINKS

        @block.tensor
        def _(pe):
            pe.wait_ge(consts, 9)
            pe.wait_ge(w_in[1], 96)
            for n, w in enumerate((st_hh, st_ih)):
                for c in range(NC):
                    for half in range(2):
                        for q in range(4 if half == 0 else 2):
                            mm = pe.transpose(bank[4 * n + 2 * c + half][:, q * P:(q + 1) * P],
                                              w[:, 4 * half + q, c * P:(c + 1) * P], ident[:, :])
                        mm.then_inc(prep_mm, 1)
            pe.wait_ge(prep_out, 1)
            for c in range(NC):
                mm = pe.transpose(bank[0][:, c * NE:(c + 1) * NE], st_esel[:, c * P:(c + 1) * P], ident[0:NE, 0:NE])
            mm.then_inc(prep_mm, 1)
            for c in range(NC):
                for o in range(NC):
                    mm = pe.matmul(bank[1 + c][:, 0:D], st_wk[:, o, c * P:(c + 1) * P], st_wq[:, o, :], start=o == 0, stop=o == 1)
                mm.then_inc(prep_mm, 1)
            for c in range(NC):
                for b, lo, size in ((3 + 2 * c, 0, 512), (4 + 2 * c, 512, 256)):
                    for o in range(NC):
                        mm = pe.matmul(bank[b][:, 0:size], st_wv[:, o, c * P:(c + 1) * P], st_ihT[:, o, lo:lo + size],
                                       start=o == 0, stop=o == 1)
                    mm.then_inc(prep_mm, 1)
            pe.drain().then_inc(done[0], 1)
            pe.wait_ge(done[0], 4)
            pe.wait_ge(consts, 10)

            with pe.Fori(0, PAIRS) as i:
                for j in range(2):
                    b, read, count = bank_free(jobs1, i, ("xT", j))
                    pe.wait_ge(read, count)
                    pe.wait_ge(x_arr[j], due(1, i, 1, step=16))
                    transpose4(pe, 0, lambda t, c: x_in[:, j, t, c * P:(c + 1) * P]).then_inc(xT_mm, 1)
                    pe.wait_ge(xT_lo, due(2, i, j + 1))
                    for name, ev, base in (("q", q_mm, 0), ("k", k_mm, D)):
                        b, read, count = bank_free(jobs1, i, (name, j))
                        pe.wait_ge(read, count)
                        for m in range(NC):
                            for c in range(NC):
                                cols = slice(base + m * P, base + (m + 1) * P)
                                mm = split3(pe, halves(b)[:, m, :], lambda a: wqkv_hl[:, a, c, cols],
                                            lambda a: xT_hl[:, a, c, :], c == 0, c == 1)
                        mm.then_inc(ev, 1)
                    b, read, count = bank_free(jobs1, i, ("v", j))
                    pe.wait_ge(read, count)
                    for t in range(NT):
                        for c in range(NC):
                            mm = split3(pe, halves(b)[:, t, :], lambda a: xT_hl[:, a, c, t * P:(t + 1) * P],
                                        lambda a: wqkv_hl[:, a, c, 2 * D:], c == 0, c == 1)
                    mm.then_inc(v_mm, 1)
                for j in range(2):
                    for hp in range(H // 2 + 2):
                        if hp < H // 2:
                            if hp % 2 == 0:
                                pe.wait_ge(ops_in[hp // 2], due(2, i, j + 1, step=16 * 6))
                            pair = head(2 * hp) // 2
                            for qt in range(NT):
                                n = 16 * j + 2 * hp + qt
                                b, read, count = bank_free(jobs1, i, ("s", n))
                                pe.wait_ge(read, count)
                                rows = slice(qt * P, (qt + 1) * P)
                                for e in range(2):
                                    pe.matmul(halves(b)[:, e, :], q_op[:, pair, e, rows], k_op[:, pair, :],
                                              start=e == 0, stop=False, skip_group_check=True)
                                pe.matmul(halves(b)[:, :, rows], ident16[:, :], mask16[:, :, :],
                                                      start=False, stop=True, skip_group_check=True).then_inc(s_mm, 1)
                        if 1 <= hp <= H // 2:
                            for e in range(2):
                                h = 2 * (hp - 1) + e
                                n = 16 * j + h
                                b, read, count = bank_free(jobs1, i, ("pT", n))
                                pe.wait_ge(read, count)
                                pe.wait_ge(exp_ok, due(32, i, 16 * j + 2 * hp))
                                for q, lo in enumerate((0, P, 2 * P)):
                                    mm = pe.transpose(bank[b][:, lo:lo + P], prob[:, (hp - 1) % 2, e, lo:lo + P], ident[:, :])
                                mm.then_inc(pT_mm, 1)
                        if hp >= 2:
                            if hp == 2:
                                b, read, count = bank_free(jobs1, i, ("y", j))
                                pe.wait_ge(read, count)
                                pe.wait_ge(vp_ok, due(2, i, j + 1))
                            for e in range(2):
                                h = 2 * (hp - 2) + e
                                pe.wait_ge((pT_even, pT_odd)[e], due(16, i, 8 * j + h // 2 + 1))
                                c = head(h) // 8
                                pe.matmul(halves(3)[:, c, :], v_pad[:, 0, head(h), :], probT[:, h % 4, 0:T],
                                          start=h == 0, stop=False, skip_group_check=True)
                                pe.matmul(halves(3)[:, c, P:], v_pad[:, 1, head(h), :], probT[:, h % 4, T:],
                                                       start=False, stop=h == H - 1, skip_group_check=True).then_inc(pv_mm, 1)
                    b, read, count = bank_free(jobs1, i, ("ib", j))
                    pe.wait_ge(read, count)
                    pe.wait_ge(inv_ok, due(2, i, j + 1))
                    for c in range(NC):
                        for t in range(NT):
                            mm = pe.matmul(halves(b)[:, c, t * P:(t + 1) * P], inv_wide[:, t, c * P:(c + 1) * P],
                                           ident[:, :], start=True, stop=True)
                    mm.then_inc(ib_mm, 1)
                    b, read, count = bank_free(jobs1, i, ("pr", j))
                    pe.wait_ge(read, count)
                    pe.wait_ge(y_lo, due(2, i, j + 1))
                    for t in range(NT):
                        for c in range(NC):
                            mm = split3(pe, halves(b)[:, t, :], lambda a: y_hl[:, a, c, t * P:(t + 1) * P],
                                        lambda a: wproj_hl[:, a, c, :], c == 0, c == 1)
                    mm.then_inc(pr_mm, 1)
                    b, read, count = bank_free(jobs1, i, ("x1T", j))
                    pe.wait_ge(read, count)
                    pe.wait_ge(x1_ok, due(2, i, j + 1))
                    transpose4(pe, b, lambda t, c: u1[:, t, c * P:(c + 1) * P]).then_inc(x1T_mm, 1)
            pe.drain().then_inc(done[1], 1)
            pe.wait_ge(done[1], 4)

            with pe.Fori(0, PAIRS) as i:
                for j in range(2):
                    b, read, count = bank_free(jobs2, i, ("cT", j))
                    pe.wait_ge(read, count)
                    pe.wait_ge(c_ok, due(2, i, j + 1))
                    transpose4(pe, 0, lambda t, c: c_in[:, j, t, c * P:(c + 1) * P]).then_inc(cT_mm, 1)
                    pe.wait_ge(cT_lo, due(2, i, j + 1))
                    b, read, count = bank_free(jobs2, i, ("kT", j))
                    pe.wait_ge(read, count)
                    for m in range(NC):
                        for c in range(NC):
                            mm = split3(pe, halves(b)[:, m, :], lambda a: qk_w_hl[:, a, c, m * P:(m + 1) * P],
                                        lambda a: cT_hl[:, a, c, :], c == 0, c == 1)
                    mm.then_inc(kT_mm, 1)
                    for g in range(3):
                        b, read, count = bank_free(jobs2, i, ("vg", 3 * j + g))
                        pe.wait_ge(read, count)
                        for half in range(2):
                            t, blk = divmod(2 * g + half, 3)
                            for c in range(NC):
                                mm = split3(pe, halves(b)[:, half, :], lambda a: cT_hl[:, a, c, t * P:(t + 1) * P],
                                            lambda a: v_w_hl[:, a, c, blk * D:(blk + 1) * D], c == 0, c == 1)
                        mm.then_inc(vg_mm, 1)

                def start(u):
                    j = u % 2
                    b, read, count = bank_free(jobs2, i, ("ss", u))
                    pe.wait_ge(read, count)
                    pe.wait_ge(sqs_ok, due(UNITS, i, u + 1))
                    for t in range(NT):
                        mm = pe.matmul(bank[b][:, t:t + 1], sq[:, 0, t * P:(t + 1) * P], mean_col[:, :], start=True, stop=True)
                    mm.then_inc(ss_mm, 1)
                    b, read, count = bank_free(jobs2, i, ("sc", u))
                    pe.wait_ge(read, count)
                    pe.wait_ge(sl_lo, due(6, i, u + 1))
                    pe.wait_ge(kT_lo, due(2, i, j + 1))
                    for t in range(NT):
                        for c in range(NC):
                            mm = split3(pe, halves(b)[:, t, :], lambda a: kT_hl[:, j, a, c, t * P:(t + 1) * P],
                                        lambda a: slots_hl[:, j, a, c, :], c == 0, c == 1)
                    mm.then_inc(sc_mm, 1)
                    b, read, count = bank_free(jobs2, i, ("rb", u))
                    pe.wait_ge(read, count)
                    pe.wait_ge(rs_ok, due(UNITS, i, u + 1))
                    for t in range(NT):
                        mm = pe.matmul(bank[b][:, t * P:(t + 1) * P], s_rs[:, j, t:t + 1].to_broadcast([P, P]), ident[:, :],
                                       start=True, stop=True)
                    mm.then_inc(rb_mm, 1)

                def state(u):
                    j = u % 2
                    for n, name in enumerate(("r", "z", "hn")):
                        b, read, count = bank_free(jobs2, i, (name, u))
                        pe.wait_ge(read, count)
                        for m in range(NC):
                            cols = slice(n * D + m * P, n * D + (m + 1) * P)
                            for c in range(NC):
                                mm = split3(pe, halves(b)[:, m, :], lambda a: whhT_hl[:, a, c, cols],
                                            lambda a: slots_hl[:, j, a, c, :], m == 0 and c == 0, False)
                    mm.then_inc(hn_mm, 1)

                def totals(u):
                    j = u % 2
                    b, read, count = bank_free(jobs2, i, ("tt", u))
                    pe.wait_ge(read, count)
                    pe.wait_ge(z_ok, due(UNITS, i, u + 1))
                    for t in range(NT):
                        mm = pe.matmul(bank[b][:, 0:T], s_inv[:, j, t:t + 1].to_broadcast([P, P]), attn[:, j, t, :],
                                       start=t == 0, stop=t == 1)
                    mm.then_inc(tt_mm, 1)

                def inputs(u):
                    j = u % 2
                    pe.wait_ge(at_lo, due(UNITS, i, u + 1))
                    for n, b, ev in ((0, 4, r_mm), (2, 7, xn_mm), (1, 5, z_mm)):
                        if n == 2:
                            b, read, count = bank_free(jobs2, i, ("xn", u))
                            pe.wait_ge(read, count)
                        for m in range(NC):
                            for t in range(NT):
                                r, q = divmod(n * D + m * P, D)
                                mm = split3(pe, halves(b)[:, m, :], lambda a: vg_hl[:, j, a, 3 * t + r, q:q + P],
                                            lambda a: attn_hl[:, j, a, t, :], n == 2 and m == 0 and t == 0, True)
                        mm.then_inc(ev, 1)
                pe.wait_ge(vg_lo, due(6, i, 6))
                start(0)
                state(0)
                totals(0)
                for u in range(UNITS):
                    if u + 1 < UNITS:
                        start(u + 1)
                    inputs(u)
                    if u + 1 < UNITS:
                        totals(u + 1)
                        state(u + 1)
                for j in range(2):
                    b, read, count = bank_free(jobs2, i, ("uT", j))
                    pe.wait_ge(read, count)
                    pe.wait_ge(uu_ok, due(2, i, j + 1))
                    transpose4(pe, b, lambda c, t: slots[:, j, c, t * P:(t + 1) * P]).then_inc(uT_mm, 1)
            pe.drain().then_inc(done[2], 1)
            pe.wait_ge(done[2], 4)
            pe.wait_ge(consts, 16)

            with pe.Fori(0, PAIRS) as i:
                for j in range(2):
                    b, read, count = bank_free(jobs3, i, ("tT", j))
                    pe.wait_ge(read, count)
                    pe.wait_ge(xf_ok, due(2, i, j + 1))
                    transpose4(pe, b, lambda t, c: x2f[:, j, t, c * P:(c + 1) * P]).then_inc(tT_mm, 1)
                    b, read, count = bank_free(jobs3, i, ("lg", j))
                    pe.wait_ge(read, count)
                    pe.wait_ge(tT_lo, due(2, i, j + 1))
                    for c in range(NC):
                        mm = split3(pe, bank[b][0:NE, 0:T], lambda a: eselT_hl[:, a, c, :], lambda a: x2T_hl[:, j, a, c, :], c == 0, c == 1)
                    mm.then_inc(lg_mm, 1)
                    b, read, count = bank_free(jobs3, i, ("lT", j))
                    pe.wait_ge(read, count)
                    pe.wait_ge(lg_ok, due(2, i, j + 1))
                    pe.sem_inc(passed, 1)
                    for t in range(NT):
                        mm = pe.transpose(bank[b][:, t * NE:(t + 1) * NE], logT[:, t * P:(t + 1) * P], ident[0:NE, 0:NE])
                    mm.then_inc(lT_mm, 1)
                    b, read, count = bank_free(jobs3, i, ("gT", j))
                    pe.wait_ge(read, count)
                    pe.wait_ge(gt_ok, due(2, i, j + 1))
                    for t in range(NT):
                        mm = pe.transpose(bank[b][0:NE, t * P:(t + 1) * P], gate[:, t, :], ident[:, :])
                    mm.then_inc(gT_mm, 1)
                    for g in range(4):
                        n = 4 * j + g
                        b, read, count = bank_free(jobs3, i, ("h", n))
                        pe.wait_ge(read, count)
                        for half in range(2):
                            m = 2 * g + half
                            for c in range(NC):
                                mm = split3(pe, halves(b)[:, half, :], lambda a: keys_hl[:, a, c, m * P:(m + 1) * P],
                                            lambda a: x2T_hl[:, j, a, c, :], c == 0, c == 1)
                        mm.then_inc(h_mm, 1)
                        b, read, count = bank_free(jobs3, i, ("gb", n))
                        pe.wait_ge(read, count)
                        if g == 0:
                            pe.wait_ge(gT_lo, due(2, i, j + 1))
                        for half in range(2):
                            mm = pe.matmul(halves(b)[:, half, :], spread[:, 2 * g + half, :], gateT_hl[:, 0, :], start=True, stop=True)
                        mm.then_inc(gb_mm, 1)
                for j in range(2):
                    b, read, count = bank_free(jobs3, i, ("o", j))
                    pe.wait_ge(read, count)
                    pe.wait_ge(h_lo, due(8, i, 4 * j + 4))
                    for t in range(NT):
                        for m in range(NH):
                            mm = split3(pe, halves(b)[:, t, :], lambda a: hid_hl[:, j, a, m, t * P:(t + 1) * P],
                                        lambda a: values_hl[:, a, m, :], m == 0, m == NH - 1)
                    mm.then_inc(o_mm, 1)
        s3.close()


_INS = ['x', 'ctx_1024', 'L0_attn_w_qkv', 'L0_attn_b_qkv', 'L0_attn_w_proj', 'L0_attn_b_proj', 'L0_xattn_Wq',
        'L0_xattn_Wk', 'L0_xattn_Wv', 'L0_xattn_gru_wih', 'L0_xattn_gru_whh', 'L0_xattn_gru_bih', 'L0_xattn_gru_bhh',
        'L0_xattn_slot_norm_w', 'L0_xattn_input_norm_w', 'L0_ffn_expert_sel', 'L0_ffn_keys', 'L0_ffn_values',
        'L0_ffn_route_scale']


def kernel(**inputs):
    import numpy as _np
    import concourse.bacc as _bacc
    from concourse import mybir as _mybir
    from concourse.bass_utils import run_bass_kernel_spmd as _run

    nc = _bacc.Bacc("TRN2", target_bir_lowering=False, num_devices=1)
    arrays, args = {}, []
    for name in _INS:
        a = _np.ascontiguousarray(inputs[name])
        arrays[f"in_{name}_dram"] = a
        args.append(nc.dram_tensor(f"in_{name}_dram", a.shape, _mybir.dt.from_np(a.dtype), kind="ExternalInput").ap())
    args.append(nc.dram_tensor("out_dram", (B, T, D), _mybir.dt.float32, kind="ExternalOutput").ap())
    decoder_layer(nc, *args)
    r = _run(nc, [arrays], core_ids=[0])
    return r.results[0]["out_dram"]
```

```python
from contextlib import ExitStack

import concourse.bass as bass
from concourse import mybir

F32, F32R, BF16 = mybir.dt.float32, mybir.dt.float32r, mybir.dt.bfloat16
ALU = mybir.AluOpType
ACT = mybir.ActivationFunctionType
AX = mybir.AxisListType

B, T, D = 8, 256, 256
P = 128
H, DH = 16, 16
NT = T // P
NC = D // P
G3 = 3 * D
NE, EH, TOPK = 16, 64, 4
NH = NE * EH // P
ITERS = 3
PAIRS = B // 2
LN_EPS, RMS_EPS = 1e-5, 1e-6
MASKED = -1e30
HI, LO = 0, 1
PASSES = ((HI, HI), (HI, LO), (LO, HI))
HI_FIRST = ((HI, HI), (LO, HI), (HI, LO))
UNITS = 2 * ITERS
SQ = 384


ATTN_LINKS = 2 * 3
CROSS_LINKS = UNITS * 3 + 2 * 2
EXPERT_LINKS = 2 * 11


def head(n):
    pair = 4 * (n // 2 % 2) + n // 4
    return 2 * pair + n % 2


def due(per, i, k, back=0, step=1):
    return (i * per + (1 - back) * per + k) * step


def decoder_layer(nc, x, ctx_in, w_qkv, b_qkv, w_proj, b_proj, wq, wk, wv, wih, whh, bih, bhh,
                  slot_w, input_w, expert_sel, keys, values, route_scale, out):
    stack = ExitStack()
    with stack:
        def sb(name, shape, dt=F32, where=stack):
            return where.enter_context(nc.sbuf_tensor(name, shape, dt))

        def sem(name):
            return stack.enter_context(nc.semaphore(name))

        events = []
        passed = sem("passed")

        def event(name, per, step=1):
            events.append((sem(name), per * step))
            return events[-1][0]

        ident = sb("ident", [P, P])
        ident16 = sb("ident16", [P, P], BF16)
        mask16 = sb("mask16", [P, 2, P], BF16)
        mask32 = sb("mask32", [P, P])
        mean_col = sb("mean_col", [P, 1])
        half_neg = sb("half_neg", [P, 2])
        wqkv_hl = sb("wqkv_hl", [P, 2, NC, G3], F32R)
        wproj_hl = sb("wproj_hl", [P, 2, NC, D], F32R)
        qk_w_hl = sb("qk_w_hl", [P, 2, NC, D], F32R)
        v_w_hl = sb("v_w_hl", [P, 2, NC, G3], F32R)
        whhT_hl = sb("whhT_hl", [P, 2, NC, G3], F32R)
        eselT_hl = sb("eselT_hl", [P, 2, NC, NE], F32R)
        keys_hl = sb("keys_hl", [P, 2, NC, NE * EH], F32R)
        values_hl = sb("values_hl", [P, 2, NH, D], F32R)
        bq_col = sb("bq_col", [P, 2 * NC])
        bv_row = sb("bv_row", [P, D])
        bp_row = sb("bp_row", [P, D])
        bih_col = sb("bih_col", [P, 6])
        bhh_col = sb("bhh_col", [P, 6])
        brz_col = sb("brz_col", [P, 4])
        slot_col = sb("slot_col", [P, NC])
        input_col = sb("input_col", [P, NC])
        route_col = sb("route_col", [P, 1])
        member = sb("member", [P, 2])
        x1T = sb("x1T", [P, NC, B * T])

        s0 = ExitStack()
        st_qkv = sb("st_qkv", [P, NC, G3], where=s0)
        st_proj = sb("st_proj", [P, NC, D], where=s0)
        st_wq = sb("st_wq", [P, NC, D], where=s0)
        st_wk = sb("st_wk", [P, NC, D], where=s0)
        st_wv = sb("st_wv", [P, NC, D], where=s0)
        st_ih = sb("st_ih", [P, 6, D], where=s0)
        st_hh = sb("st_hh", [P, 6, D], where=s0)
        st_ihT = sb("st_ihT", [P, NC, G3], where=s0)
        st_keys = sb("st_keys", [P, NC, NE * EH], where=s0)
        st_values = sb("st_values", [P, NH, D], where=s0)
        st_esel = sb("st_esel", [NE, D], where=s0)
        s0.close()

        s1 = ExitStack()
        x_in = sb("x_in", [P, 2, NT, D], where=s1)
        xr = sb("xr", [P, 2, NT, D], where=s1)
        xT_hl = sb("xT_hl", [P, 2, NC, T], F32R, where=s1)
        q_hl = sb("q_hl", [P, 2, NC, T], F32R, where=s1)
        q_sep = sb("q_sep", [P, 2, 2, NC, 2, T], F32R, where=s1)
        k_hl = sb("k_hl", [P, 2, 2, NC, T], F32R, where=s1)
        v_sb = sb("v_sb", [P, 2, NT, D], where=s1)
        k_op = sb("k_op", [3 * 32, H // 2, T], F32R, where=s1)
        q_op = sb("q_op", [3 * 32, H // 2, 2, T], F32R, where=s1)
        v_pad = sb("v_pad", [P, NT, H, P], where=s1)
        prob = sb("prob", [P, 2, 2, SQ], where=s1)
        probT = sb("probT", [P, 4, SQ], where=s1)
        neg_max = sb("neg_max", [P, H // 2, NT, 2], where=s1)
        row_sum = sb("row_sum", [P, NT, H], where=s1)
        inv_sum = sb("inv_sum", [P, NT, H], where=s1)
        inv_wide = sb("inv_wide", [P, NT, D], where=s1)
        inv_bc = sb("inv_bc", [P, NC, T], where=s1)
        yn = sb("yn", [P, NC, T], where=s1)
        y_hl = sb("y_hl", [P, 2, NC, T], F32R, where=s1)
        u1 = sb("u1", [P, NT, D], where=s1)
        stats1 = sb("stats1", [P, NT, 6], where=s1)
        mv1 = sb("mv1", [P, NT, 2], where=s1)
        std1 = sb("std1", [P, 2, NT], where=s1)
        s1.close()

        x2 = sb("x2", [P, B * NT, D])
        s2 = ExitStack()
        c_in = sb("c_in", [P, 2, NT, D], where=s2)
        junk = sb("junk", [P, 2, NT, D], where=s2)
        c_ss = sb("c_ss", [P, 2, NT], where=s2)
        c_ms = sb("c_ms", [P, 2, NT], where=s2)
        c_rs = sb("c_rs", [P, 2, NT], where=s2)
        c_now = sb("c_now", [P, 2, NT], where=s2)
        cT_hl = sb("cT_hl", [P, 2, NC, T], F32R, where=s2)
        kT_hl = sb("kT_hl", [P, 2, 2, NC, T], F32R, where=s2)
        vg_hl = sb("vg_hl", [P, 2, 2, 6, D], F32R, where=s2)
        slots = sb("slots", [P, 2, NC, T], where=s2)
        slots_hl = sb("slots_hl", [P, 2, 2, NC, T], F32R, where=s2)
        sq = sb("sq", [P, NC, T], where=s2)
        s_ms = sb("s_ms", [P, 2, NT], where=s2)
        s_rs = sb("s_rs", [P, 2, NT], where=s2)
        rs_bc = sb("rs_bc", [P, 2, T], where=s2)
        attn = sb("attn", [P, 2, NT, T], where=s2)
        attn_hl = sb("attn_hl", [P, 2, 2, NT, T], F32R, where=s2)
        s_max = sb("s_max", [P, 2, NT], where=s2)
        s_sum = sb("s_sum", [P, 2, NT], where=s2)
        s_inv = sb("s_inv", [P, 2, NT], where=s2)
        tot = sb("tot", [P, T], where=s2)
        inv_tot = sb("inv_tot", [P, T], where=s2)
        gate_r = sb("gate_r", [P, NC, T], where=s2)
        gate_z = sb("gate_z", [P, NC, T], where=s2)
        cand = sb("cand", [P, NC, T], where=s2)
        diff = sb("diff", [P, NC, T], where=s2)
        stats2 = sb("stats2", [P, NT, 6], where=s2)
        mv2 = sb("mv2", [P, NT, 2], where=s2)
        std2 = sb("std2", [P, 2, NT], where=s2)
        s2.close()

        s3 = ExitStack()
        x2f = sb("x2f", [P, 2, NT, D], where=s3)
        x2T_hl = sb("x2T_hl", [P, 2, 2, NC, T], F32R, where=s3)
        logT = sb("logT", [NE, 2, T], where=s3)
        prb = sb("prb", [P, NT, 24], where=s3)
        prbx = sb("prbx", [P, NT, 24], where=s3)
        top8 = sb("top8", [P, NT, 8], where=s3)
        gate = sb("gate", [P, NT, NE], where=s3)
        gsum = sb("gsum", [P, NT], where=s3)
        ginv = sb("ginv", [P, NT], where=s3)
        gateT_hl = sb("gateT_hl", [P, 2, T], F32R, where=s3)
        spread = sb("spread", [P, NH, P], F32R, where=s3)
        spread32 = sb("spread32", [P, NH, P], where=s3)
        hid = sb("hid", [P, 4, 2, T], where=s3)
        hid_hl = sb("hid_hl", [P, 2, 2, NH, T], F32R, where=s3)
        u3 = sb("u3", [P, NT, D], where=s3)
        y_out = sb("y_out", [P, 2, NT, D], where=s3)
        stats3 = sb("stats3", [P, NT, 6], where=s3)
        mv3 = sb("mv3", [P, NT, 2], where=s3)
        std3 = sb("std3", [P, 2, NT], where=s3)

        bank = [stack.enter_context(nc.psum_tensor(f"bank{n}", [P, 512], F32)) for n in range(8)]

        def halves(b):
            return bank[b][:, :].rearrange("p (a n) -> p a n", a=2)

        w_in = [sem(f"w_in{n}") for n in range(4)]
        consts = sem("consts")
        prep_mm = sem("prep_mm")
        prep_out = sem("prep_out")
        prep_act = sem("prep_act")
        prep_dve = sem("prep_dve")
        done = [sem(f"phase_done{n}") for n in range(3)]

        x_arr = [event(f"x_arr{j}", 1, 16) for j in range(2)]
        xr_ok = event("xr_ok", 2)
        xT_mm, xT_hi, xT_lo = event("xT_mm", 2), event("xT_hi", 2), event("xT_lo", 2)
        q_mm, q_hi, q_lo = event("q_mm", 2), event("q_hi", 2), event("q_lo", 2)
        k_mm, k_hi, k_lo = event("k_mm", 2), event("k_hi", 2), event("k_lo", 2)
        v_mm, v_ok = event("v_mm", 2), event("v_ok", 2)
        vp_ok = event("vp_ok", 2)
        q_set = event("q_set", 2)
        ops_in = [event(f"ops_in{strip}", 2, 16 * 6) for strip in range(4)]
        s_mm, max_ok, exp_ok = event("s_mm", 32), event("max_ok", 32), event("exp_ok", 32)
        pT_mm = event("pT_mm", 32)
        pT_even, pT_odd = event("pT_even", 16), event("pT_odd", 16)
        pv_mm = event("pv_mm", 32)
        inv_ok, ib_mm, ib_ok = event("inv_ok", 2), event("ib_mm", 2), event("ib_ok", 2)
        yn_ok, y_hi, y_lo = event("yn_ok", 2), event("y_hi", 2), event("y_lo", 2)
        pr_mm, u1_ok = event("pr_mm", 2), event("u1_ok", 2)
        var1, rstd1, x1_ok = event("var1", 2), event("rstd1", 2), event("x1_ok", 2)
        x1T_mm, x1T_ok = event("x1T_mm", 2), event("x1T_ok", 2)
        c_arr = [event(f"c_arr{j}", 1, 16) for j in range(2)]
        c_sq, c_mean, c_rstd, c_kept = event("c_sq", 2), event("c_mean", 2), event("c_rstd", 2), event("c_kept", 1)
        cT_mm, cT_hi, cT_lo = event("cT_mm", 2), event("cT_hi", 2), event("cT_lo", 2)
        kT_mm, kT_hi, kT_lo = event("kT_mm", 2), event("kT_hi", 2), event("kT_lo", 2)
        vg_mm, vg_hi, vg_lo = event("vg_mm", 6), event("vg_hi", 6), event("vg_lo", 6)
        sl_ok, sl_hi, sl_lo = event("sl_ok", 8), event("sl_hi", 6), event("sl_lo", 6)
        sq_ok, sqs_ok = event("sq_ok", UNITS), event("sqs_ok", UNITS)
        ss_mm, ms_ok, rs_ok = event("ss_mm", UNITS), event("ms_ok", UNITS), event("rs_ok", UNITS)
        rb_mm, rb_ok = event("rb_mm", UNITS), event("rb_ok", UNITS)
        sc_mm, sc_ok = event("sc_mm", UNITS), event("sc_ok", UNITS)
        smax_ok, e_ok, z_ok = event("smax_ok", UNITS), event("e_ok", UNITS), event("z_ok", UNITS)
        tt_mm, tt_ok, it_ok = event("tt_mm", UNITS), event("tt_ok", UNITS), event("it_ok", UNITS)
        at_ok, at_hi, at_lo = event("at_ok", UNITS), event("at_hi", UNITS), event("at_lo", UNITS)
        r_mm, z_mm, hn_mm, xn_mm = (event(n, UNITS) for n in ("r_mm", "z_mm", "hn_mm", "xn_mm"))
        r_ok, zt_ok, g_ok, np_ok, n_ok = (event(n, UNITS) for n in ("r_ok", "zt_ok", "g_ok", "np_ok", "n_ok"))
        uu_ok, uT_mm = event("uu_ok", 2), event("uT_mm", 2)
        var2, rstd2, x2_ok = event("var2", 2), event("rstd2", 2), event("x2_ok", 2)
        xf_ok = event("xf_ok", 2)
        tT_mm, tT_hi, tT_lo = event("tT_mm", 2), event("tT_hi", 2), event("tT_lo", 2)
        lg_mm, lg_ok, lT_mm, lx_ok = event("lg_mm", 2), event("lg_ok", 2), event("lT_mm", 2), event("lx_ok", 2)
        gt_ok, gT_mm, gT_hi, gT_lo = event("gt_ok", 2), event("gT_mm", 2), event("gT_hi", 2), event("gT_lo", 2)
        h_mm, h_relu, gb_mm = event("h_mm", 8), event("h_relu", 8), event("gb_mm", 8)
        h_ok, h_hi, h_lo = event("h_ok", 8), event("h_hi", 8), event("h_lo", 8)
        o_mm, u3_ok = event("o_mm", 2), event("u3_ok", 2)
        var3, rstd3, y_ok = event("var3", 2), event("rstd3", 2), event("y_ok", 2)
        stored = [event(f"stored{j}", 1, 16) for j in range(2)]

        attn_chain, cross_chain, expert_chain = sem("attn_chain"), sem("cross_chain"), sem("expert_chain")
        links = [0]

        def next_link():
            links[0] += 1
            return links[0]


        jobs1 = []
        for j in range(2):
            jobs1 += [(("xT", j), 0, xT_lo, 2, j + 1), (("q", j), 1, q_lo, 2, j + 1),
                      (("k", j), 2, k_lo, 2, j + 1), (("v", j), 0, v_ok, 2, j + 1)]
        for j in range(2):
            for hp in range(H // 2 + 2):
                if hp < H // 2:
                    for qt in range(NT):
                        n = 16 * j + 2 * hp + qt
                        jobs1.append((("s", n), 4 + qt, exp_ok, 32, n + 1))
                if 1 <= hp <= H // 2:
                    for e in range(2):
                        n = 16 * j + 2 * (hp - 1) + e
                        jobs1.append((("pT", n), 6 + e, (pT_even, pT_odd)[e], 16, n // 2 + 1))
                if hp == 2:
                    jobs1.append((("y", j), 3, yn_ok, 2, j + 1))
            jobs1 += [(("ib", j), 1, ib_ok, 2, j + 1), (("pr", j), 2, u1_ok, 2, j + 1),
                      (("x1T", j), 0, x1T_ok, 2, j + 1)]
        def context(j):
            cT, kT, *vg = ((0, 1, 3, 2, 0), (1, 3, 2, 4, 5))[j]
            jobs = [(("cT", j), cT, cT_lo, 2, 2 + j + 1), (("kT", j), kT, kT_lo, 2, 2 + j + 1)]
            return jobs + [(("vg", 3 * j + g), vg[g], vg_lo, 6, 6 + 3 * j + g + 1) for g in range(3)]

        def front(u):
            return [(("ss", u), 0, ms_ok, UNITS, u + 1), (("sc", u), 3, sc_ok, UNITS, u + 1), (("rb", u), 1, rb_ok, UNITS, u + 1)]

        def mid(u):
            return [(("r", u), 4, r_ok, UNITS, u + 1), (("z", u), 5, zt_ok, UNITS, u + 1), (("hn", u), 6, g_ok, UNITS, u + 1),
                    (("tt", u), 2, tt_ok, UNITS, u + 1)]

        def back(u):
            return [(("xn", u), 7, np_ok, UNITS, u + 1)]

        jobs2 = mid(0)
        for u in range(UNITS):
            jobs2 += (front(u + 1) if u + 1 < UNITS else []) + back(u)
            jobs2 += context(0)[:1] if u == 4 else []
            jobs2 += mid(u + 1) if u + 1 < UNITS else []
            jobs2 += context(0)[1:] + context(1)[:1] if u == 4 else []
        jobs2 += context(1)[1:2] + [(("uT", 0), 0, x2_ok, 2, 1)] + context(1)[2:]
        jobs2 += [(("uT", 1), 6, x2_ok, 2, 2)] + front(UNITS)
        BANK2 = {job[0]: job[1] for job in jobs2}
        EXPERT_ORDER = [("lg", 0), ("h", 0), ("h", 1), ("lT", 0), ("lg", 1), ("h", 2), ("gT", 0), ("h", 3),
                        ("gb", 0), ("lT", 1), ("gb", 1), ("h", 4), ("gb", 2), ("gT", 1), ("gb", 3),
                        ("h", 5), ("gb", 4), ("h", 6), ("gb", 5), ("h", 7), ("gb", 6), ("gb", 7)]
        EXPERT_ORDER += [("tT", 0), ("tT", 1), ("o", 0), ("o", 1)]
        jobs3 = []
        for name, n in EXPERT_ORDER:
            b, signal, per = {"tT": (n, tT_lo, 2), "lg": (2, lg_ok, 2), "lT": (0, lx_ok, 2), "gT": (1 - n, gT_lo, 2),
                              "h": (4 + n % 2, h_relu, 8), "gb": (6 + n % 2, h_ok, 8), "o": (2 + n, u3_ok, 2)}[name]
            jobs3.append(((name, n), b, signal, per, n + 1 + (per if name == "tT" else 0)))

        def bank_free(jobs, i, key, final=False):
            at = [job[0] for job in jobs].index(key)
            b = jobs[at][1]
            before = [job for job in jobs[:at] if job[1] == b and not (final and job[4] > job[3])]
            last = [job for job in jobs if job[1] == b][-1]
            _, _, signal, per, k = before[-1] if before else last
            return b, signal, due(per, i, k, back=0 if before else 1)

        def split3(pe, dst, left, right, first, last):
            for n, (a, b) in enumerate(PASSES):
                mm = pe.matmul(dst, left(a), right(b), start=first and n == 0, stop=last and n == 2,
                               skip_group_check=True)
            return mm

        def transpose4(pe, b, src):
            for c in range(2):
                for t in range(2):
                    mm = pe.transpose(halves(b)[:, c, t * P:(t + 1) * P], src(t, c), ident[:, :])
            return mm

        VG_ROWS = (((0, 2, 0),), ((0, 1, 0), (1, 1, 1)), ((0, 2, 1),))

        def f32(ap):
            return ap.bitcast(F32)

        block = stack.enter_context(nc.Block())

        @block.sync
        def _(sp):
            for signal, count in events:
                sp.sem_inc(signal, count)
            def rows(w, n):
                return w.rearrange("(c p) n -> p c n", p=P)
            with nc.allow_non_contiguous_dma("biases by column"):
                sp.dma_start(st_qkv[:, :, :], rows(w_qkv, NC)).then_inc(w_in[0], 16)
                sp.dma_start(st_wk[:, :, :], rows(wk, NC)).then_inc(w_in[1], 16)
                sp.dma_start(st_wq[:, :, :], rows(wq, NC)).then_inc(w_in[1], 16)
                sp.dma_start(st_wv[:, :, :], rows(wv, NC)).then_inc(w_in[1], 16)
                sp.dma_start(st_ih[:, :, :], rows(wih, 6)).then_inc(w_in[1], 16)
                sp.dma_start(st_hh[:, :, :], rows(whh, 6)).then_inc(w_in[1], 16)
                sp.dma_start(st_esel[:, :], expert_sel).then_inc(w_in[1], 16)
                sp.dma_start(bq_col[:, :], b_qkv[0:2 * D].rearrange("(c p) -> p c", p=P)).then_inc(w_in[0], 16)
                sp.dma_start(bv_row[:, :], b_qkv[2 * D:3 * D].partition_broadcast(P)).then_inc(w_in[0], 16)
                sp.dma_start(bp_row[:, :], b_proj.partition_broadcast(P)).then_inc(w_in[0], 16)
                sp.dma_start(bih_col[:, :], bih.rearrange("(c p) -> p c", p=P)).then_inc(w_in[2], 16)
                sp.dma_start(bhh_col[:, :], bhh.rearrange("(c p) -> p c", p=P)).then_inc(w_in[2], 16)
                sp.dma_start(slot_col[:, :], slot_w.rearrange("(c p) -> p c", p=P)).then_inc(w_in[2], 16)
                sp.dma_start(input_col[:, :], input_w.rearrange("(c p) -> p c", p=P)).then_inc(w_in[2], 16)
                sp.dma_start(route_col[:, :], route_scale.partition_broadcast(P)).then_inc(w_in[2], 16)
                sp.dma_start(st_proj[:, :, :], rows(w_proj, NC)).then_inc(w_in[3], 16)
                for c in range(NC):
                    sp.dma_start(st_keys[:, c, :].rearrange("p (e h) -> p e h", e=NE),
                                 keys[:, c * P:(c + 1) * P, :].rearrange("e p h -> p e h")).then_inc(w_in[3], 16)
                sp.dma_start(st_values[:, :, :],
                             values.rearrange("e h v -> (e h) v").rearrange("(c p) v -> p c v", p=P)
                             ).then_inc(w_in[3], 16)
            sp.wait_ge(done[0], 4)

            with sp.Fori(0, PAIRS) as i:
                for j in range(2):
                    sp.wait_ge(x1T_ok, due(2, i, j + 1, back=1))
                    sp.sem_inc(passed, 1)
                    sp.dma_start(x_in[:, j, :, :], x[i * 2 + j, :, :].rearrange("(t p) d -> p t d", p=P)).then_inc(x_arr[j], 16)
                for j in range(2):
                    sp.wait_ge(k_lo, due(2, i, j + 1))
                    sp.sem_inc(passed, 1)
                    sp.wait_ge(q_set, due(2, i, j + 1))
                    sp.sem_inc(passed, 1)
                    for strip in range(4):
                        if j:
                            sp.wait_ge(s_mm, due(32, i, 4 * (strip + 1)))
                            sp.sem_inc(passed, 1)
                        else:
                            sp.wait_ge(s_mm, due(32, i, 16 + 4 * (strip + 1), back=1))
                            sp.sem_inc(passed, 1)
                        rows_in = slice(32 * strip, 32 * strip + 32)
                        for quad, part in enumerate((HI, LO, HI)):
                            sp.dma_start(f32(k_op[32 * quad:32 * quad + 32, :, :]).rearrange("p (c s) t -> p c s t", s=4)[:, :, strip, :],
                                         f32(k_hl[rows_in, j, part, :, :])).then_inc(ops_in[strip], 16)
                        for quad, part in enumerate((HI, HI, LO)):
                            sp.dma_start(f32(q_op[32 * quad:32 * quad + 32, :, :, :]).rearrange("p (c s) e t -> p c s (e t)", s=4)[:, :, strip, :],
                                         f32(q_sep[rows_in, j, part, :, :, :]).rearrange("p c e t -> p c (e t)")
                                         ).then_inc(ops_in[strip], 16)
            sp.wait_ge(done[1], 4)
            with sp.Fori(0, PAIRS) as i:
                for j in range(2):
                    sp.wait_ge(cT_mm, due(2, i, j + 1, back=1))
                    sp.sem_inc(passed, 1)
                    sp.wait_ge(c_sq, due(2, i, j + 1, back=1))
                    sp.sem_inc(passed, 1)
                    sp.dma_start(c_in[:, j, :, :], ctx_in[i * 2 + j, :, :].rearrange("(t p) d -> p t d", p=P)).then_inc(c_arr[j], 16)
            sp.wait_ge(done[2], 4)
            with sp.Fori(0, PAIRS) as i:
                for j in range(2):
                    sp.wait_ge(y_ok, due(2, i, j + 1))
                    sp.sem_inc(passed, 1)
                    sp.dma_start(out[i * 2 + j, :, :].rearrange("(t p) d -> p t d", p=P), y_out[:, j, :, :]).then_inc(stored[j], 16)
            for j in range(2):
                sp.wait_ge(stored[j], 16 * (PAIRS + 1))

        @block.gpsimd
        def _(pool):
            pool.memset(ident[:, :], 0.0).then_inc(consts, 1)
            pool.memset(mask32[:, :], 0.0).then_inc(consts, 1)
            pool.wait_ge(consts, 2)
            pool.affine_select(out=ident[:, :], in_=ident[:, :], compare_op=ALU.not_equal, fill=1.0,
                               base=0, pattern=[[-1, P]], channel_multiplier=1).then_inc(consts, 1)
            pool.affine_select(out=mask32[:, :], in_=mask32[:, :], compare_op=ALU.is_ge, fill=MASKED,
                               base=0, pattern=[[-1, P]], channel_multiplier=1).then_inc(consts, 1)
            pool.wait_ge(consts, 4)
            pool.tensor_copy(ident16[:, :], ident[:, :]).then_inc(consts, 1)
            for e in range(2):
                pool.tensor_copy(mask16[:, e, :], mask32[:, :]).then_inc(consts, 1)
            pool.memset(mean_col[:, :], 1.0 / D).then_inc(consts, 1)
            pool.memset(half_neg[:, :], -0.5).then_inc(consts, 1)
            pool.wait_ge(consts, 9)
            pool.drain().then_inc(done[0], 1)
            pool.wait_ge(done[0], 4)
            pool.memset(v_pad[:, :, :, :], 0.0).then_inc(consts, 1)
            pool.wait_ge(consts, 10)

            def rstd(i, var, ev, std, k, slot):
                pool.wait_ge(var, due(2, i, k))
                pool.tensor_tensor(std[:, 1, :], std[:, 0, :], half_neg[:, :], ALU.pow).then_inc(ev, 1)

            with pool.Fori(0, PAIRS) as i:
                def pre(j):
                    pool.wait_ge(x_arr[j], due(1, i, 1, step=16))
                    pool.wait_ge(u1_ok, due(2, i, j + 1, back=1))
                    for t in range(NT):
                        r = pool.tensor_tensor(xr[:, j, t, :], x_in[:, j, t, :], bp_row[:, :], ALU.add)
                    r.then_inc(xr_ok, 1)
                pre(0)
                pre(1)
                for j in range(2):
                    pool.wait_ge(v_ok, due(2, i, j + 1))
                    if j:
                        pool.wait_ge(pv_mm, due(32, i, 16))
                        pool.sem_inc(passed, 1)
                    else:
                        pool.wait_ge(pv_mm, due(32, i, 32, back=1))
                        pool.sem_inc(passed, 1)
                    for t in range(NT):
                        for c in range(NC):
                            dst = v_pad[:, t, 8 * c:8 * c + 8, :].rearrange("p h n -> p (h n)")
                            diag = bass.AP(tensor=dst.tensor, offset=dst.offset,
                                           ap=[list(dst.ap[0]), [P + DH, 8], [1, DH]])
                            r = pool.tensor_tensor(diag, v_sb[:, j, t, c * P:(c + 1) * P].rearrange("p (h d) -> p h d", d=DH),
                                                   bv_row[:, c * P:(c + 1) * P].rearrange("p (h d) -> p h d", d=DH), ALU.add)
                    r.then_inc(vp_ok, 1)
                    pool.wait_ge(y_hi, due(2, i, j + 1))
                    pool.tensor_tensor(y_hl[:, LO, :, :], yn[:, :, :], f32(y_hl[:, HI, :, :]), ALU.subtract).then_inc(y_lo, 1)
                    rstd(i, var1, rstd1, std1, j + 1, j)
            pool.drain().then_inc(done[1], 1)
            pool.wait_ge(done[1], 4)
            def cross(i, first=False, last=False):
                def context_scale():
                    for j in range(2):
                        pool.wait_ge(c_mean, due(2, i, 2 + j + 1))
                        pool.tensor_tensor(c_rs[:, j, :], c_ms[:, j, :], half_neg[:, :], ALU.pow).then_inc(c_rstd, 1)

                def next_slots_lo(j):
                    pool.wait_ge(sl_hi, due(6, i, 6 + j + 1))
                    pool.wait_ge(sl_ok, due(8, i, 8 + j + 1))
                    pool.tensor_tensor(slots_hl[:, j, LO, :, :], slots[:, j, :, :],
                                       f32(slots_hl[:, j, HI, :, :]), ALU.subtract).then_inc(sl_lo, 1)

                def norm(u):
                    j = u % 2
                    pool.wait_ge(ms_ok, due(UNITS, i, u + 1))
                    pool.tensor_tensor(s_rs[:, j, :], s_ms[:, j, :], half_neg[:, :], ALU.pow).then_inc(rs_ok, 1)

                def attn_lo(u):
                    j = u % 2
                    pool.wait_ge(at_hi, due(UNITS, i, u + 1))
                    pool.tensor_tensor(attn_hl[:, j, LO, :, :], attn[:, j, :, :],
                                                    f32(attn_hl[:, j, HI, :, :]), ALU.subtract).then_inc(at_lo, 1)
                if first:
                    context_scale()
                for u in range(0 if first else UNITS):
                    if u + 1 < UNITS:
                        norm(u + 1)
                    attn_lo(u)
                    if u < UNITS - 2:
                        j = u % 2
                        pool.wait_ge(sl_hi, due(6, i, 2 + u + 1))
                        pool.tensor_tensor(slots_hl[:, j, LO, :, :], slots[:, j, :, :],
                                                        f32(slots_hl[:, j, HI, :, :]), ALU.subtract).then_inc(sl_lo, 1)
                    if u == 3 and not last:
                        context_scale()
                if not last:
                    next_slots_lo(0)
                    next_slots_lo(1)
                if not first:
                    rstd(i, var2, rstd2, std2, 1, 0)
                if not last:
                    norm(UNITS)
                if not first:
                    rstd(i, var2, rstd2, std2, 2, 1)
            cross(-1, first=True)
            with pool.Fori(0, PAIRS - 1) as i:
                cross(i)
            cross(PAIRS - 1, last=True)
            pool.drain().then_inc(done[2], 1)
            pool.wait_ge(done[2], 4)
            pool.memset(spread32[:, :, :], 0.0).then_inc(consts, 1)
            pool.memset(f32(gateT_hl[:, :, :]), 0.0).then_inc(consts, 1)
            pool.memset(prb[:, :, NE:], -1.0).then_inc(consts, 1)
            pool.wait_ge(consts, 13)
            for n, off in enumerate((0, 32)):
                rows = spread32[off:off + 32, :, :].rearrange("p c (e m) -> p (c e) m", e=2)
                pool.affine_select(out=rows, in_=rows, compare_op=ALU.not_equal, fill=1.0, base=0,
                                   pattern=[[-1, NE], [0, EH]], channel_multiplier=1).then_inc(consts, 1)
            pool.wait_ge(consts, 15)
            pool.tensor_copy(spread[:, :, :], spread32[:, :, :]).then_inc(consts, 1)
            with pool.Fori(0, PAIRS) as i:
                for j in range(2):
                    for g in range(4):
                        n = 4 * j + g
                        pool.wait_ge(h_hi, due(8, i, n + 1))
                        pool.tensor_tensor(hid_hl[:, j, LO, 2 * g:2 * g + 2, :], hid[:, g, :, :],
                                                       f32(hid_hl[:, j, HI, 2 * g:2 * g + 2, :]), ALU.subtract).then_inc(h_lo, 1)
                for j in range(2):
                    rstd(i, var3, rstd3, std3, j + 1, j)

        @block.scalar
        def _(act):
            def copy(dst, src, **kw):
                return act.activation(dst, src, ACT.Copy, **kw)
            act.wait_ge(w_in[0], 64)
            copy(wqkv_hl[:, HI, :, 0:D], st_qkv[:, :, 0:D], scale=float(DH) ** -0.5).then_inc(prep_act, 1)
            copy(wqkv_hl[:, HI, :, D:], st_qkv[:, :, D:]).then_inc(prep_act, 1)
            act.wait_ge(w_in[3], 64)
            copy(wproj_hl[:, HI, :, :], st_proj[:, :, :]).then_inc(prep_act, 1)
            copy(keys_hl[:, HI, :, :], st_keys[:, :, :]).then_inc(prep_act, 1)
            copy(values_hl[:, HI, :, :], st_values[:, :, :]).then_inc(prep_act, 1)
            act.drain().then_inc(done[0], 1)
            act.wait_ge(done[0], 4)

            with act.Fori(0, PAIRS) as i:
                for j in range(2):
                    act.wait_ge(xT_mm, due(2, i, j + 1))
                    if j:
                        act.wait_ge(v_mm, due(2, i, 1))
                    else:
                        act.wait_ge(v_mm, due(2, i, 2, back=1))
                    copy(xT_hl[:, HI, :, :], halves(0)).then_inc(xT_hi, 1)
                    act.wait_ge(q_mm, due(2, i, j + 1))
                    if j:
                        act.wait_ge(q_set, due(2, i, 1))
                    else:
                        act.wait_ge(q_set, due(2, i, 2, back=1))
                    for c in range(NC):
                        r = act.activation(q_hl[:, HI, c, :], halves(1)[:, c, :], ACT.Identity, bias=bq_col[:, c:c + 1])
                    r.then_inc(q_hi, 1)
                    act.wait_ge(k_mm, due(2, i, j + 1))
                    for strip in range(4):
                        act.wait_ge(ops_in[strip], due(2, i, j + 1, back=1, step=16 * 6))
                    for c in range(NC):
                        r = act.activation(k_hl[:, j, HI, c, :], halves(2)[:, c, :], ACT.Identity, bias=bq_col[:, NC + c:NC + c + 1])
                    r.then_inc(k_hi, 1)
                for j in range(2):
                    def probs_out(h):
                        n = 16 * j + h
                        act.wait_ge(pT_mm, due(32, i, n + 1))
                        if n >= 4:
                            act.wait_ge(pv_mm, due(32, i, n - 3))
                        else:
                            act.wait_ge(pv_mm, due(32, i, 32 + n - 3, back=1))
                        copy(probT[:, h % 4, :], bank[7][:, 0:SQ]).then_inc(pT_odd, 1)
                    for hp in range(H // 2 + 1):
                        if hp < H // 2:
                            for qt in range(NT):
                                n = 16 * j + 2 * hp + qt
                                lo, size = (0, P) if qt == 0 else (P, 2 * P)
                                act.wait_ge(max_ok, due(32, i, n + 1))
                                at = 16 * j + 2 * hp - 2
                                if at >= 2:
                                    act.wait_ge(pT_mm, due(32, i, at))
                                else:
                                    act.wait_ge(pT_mm, due(32, i, 32 + at, back=1))
                                for e in range(2):
                                    r = act.activation(prob[:, hp % 2, e, lo:lo + size], halves(4 + qt)[:, e, 0:size],
                                                       ACT.Exp, bias=neg_max[:, hp, qt, e:e + 1],
                                                       accum_out=row_sum[:, qt, head(2 * hp + e):head(2 * hp + e) + 1])
                                r.then_inc(exp_ok, 1)
                        if hp >= 1:
                            probs_out(2 * hp - 1)
                    act.wait_ge(ib_mm, due(2, i, j + 1))
                    copy(inv_bc[:, :, :], halves(1)).then_inc(ib_ok, 1)
                    act.wait_ge(yn_ok, due(2, i, j + 1))
                    copy(y_hl[:, HI, :, :], yn[:, :, :]).then_inc(y_hi, 1)
                    act.wait_ge(x1T_mm, due(2, i, j + 1))
                    copy(x1T[:, :, bass.ds(i * (2 * T) + j * T, T)], halves(0)).then_inc(x1T_ok, 1)
            act.drain().then_inc(done[1], 1)
            act.wait_ge(done[1], 4)
            def context_squares(r):
                for j in range(2):
                    act.wait_ge(c_arr[j], due(1, r, 2, step=16))
                    for t in range(NT):
                        ins = act.activation(junk[:, j, t, :], c_in[:, j, t, :], ACT.Square, accum_out=c_ss[:, j, t:t + 1])
                    ins.then_inc(c_sq, 1)

            def text_hi(r, j):
                act.wait_ge(cT_mm, due(2, r, 2 + j + 1))
                act.wait_ge(vg_mm, due(6, r, 6 + 3 * j))
                copy(cT_hl[:, HI, :, :], halves(BANK2["cT", j])).then_inc(cT_hi, 1)

            def context_hi(r, j):
                act.wait_ge(kT_mm, due(2, r, 2 + j + 1))
                for c in range(NC):
                    ins = act.activation(kT_hl[:, j, HI, c, :], halves(BANK2["kT", j])[:, c, :], ACT.Identity, scale=slot_col[:, c:c + 1])
                ins.then_inc(kT_hi, 1)
                act.wait_ge(c_rstd, due(2, r, 2 + j + 1))
                for g in range(3):
                    act.wait_ge(vg_mm, due(6, r, 6 + 3 * j + g + 1))
                    for first, size, t in VG_ROWS[g]:
                        ins = act.activation(vg_hl[:, j, HI, 2 * g + first:2 * g + first + size, :],
                                             halves(BANK2["vg", 3 * j + g])[:, first:first + size, :],
                                             ACT.Identity, scale=c_rs[:, j, t:t + 1])
                    ins.then_inc(vg_hi, 1)

            def cross(i, first=False, last=False):
                def next_slots_hi(j):
                    act.wait_ge(hn_mm, due(UNITS, i, 5 + j))
                    copy(slots_hl[:, j, HI, :, :], x1T[:, :, bass.ds((i + 1) * (2 * T) + j * T, T)]).then_inc(sl_hi, 1)

                def start(u):
                    j = u % 2
                    act.wait_ge(sl_ok, due(8, i, u + 1 if u < UNITS else 8 + 1))
                    act.wait_ge(sqs_ok, due(UNITS, i, u))
                    act.activation(sq[:, :, :], slots[:, j, :, :], ACT.Square).then_inc(sq_ok, 1)

                def scale(u):
                    act.wait_ge(rb_mm, due(UNITS, i, u + 1))
                    copy(rs_bc[:, u % 2, :], bank[1][:, 0:T]).then_inc(rb_ok, 1)

                def soft(u):
                    j = u % 2
                    act.wait_ge(smax_ok, due(UNITS, i, u + 1))
                    for t in range(NT):
                        r = act.activation(attn[:, j, t, :], attn[:, j, t, :], ACT.Exp, bias=s_max[:, j, t:t + 1],
                                           accum_out=s_sum[:, j, t:t + 1])
                    r.then_inc(e_ok, 1)

                def attn_hi(u):
                    j = u % 2
                    act.wait_ge(at_ok, due(UNITS, i, u + 1))
                    copy(attn_hl[:, j, HI, :, :], attn[:, j, :, :]).then_inc(at_hi, 1)

                def reset_gate(u):
                    act.wait_ge(r_mm, due(UNITS, i, u + 1))
                    for c in range(NC):
                        r = act.activation(gate_r[:, c, :], halves(4)[:, c, :], ACT.Tanh, scale=0.5, bias=brz_col[:, c:c + 1])
                    r.then_inc(r_ok, 1)

                def gates(u):
                    act.wait_ge(np_ok, due(UNITS, i, u + 1))
                    for c in range(NC):
                        r = act.activation(cand[:, c, :], gate_r[:, c, :], ACT.Tanh, bias=bih_col[:, 2 * NC + c:2 * NC + c + 1])
                    r.then_inc(n_ok, 1)
                    act.wait_ge(z_mm, due(UNITS, i, u + 1))
                    for c in range(NC):
                        r = act.activation(gate_z[:, c, :], halves(5)[:, c, :], ACT.Tanh, scale=0.5, bias=brz_col[:, NC + c:NC + c + 1])
                    r.then_inc(zt_ok, 1)

                def slots_hi(u):
                    j = u % 2
                    if u < UNITS - 2:
                        act.wait_ge(sl_ok, due(8, i, 2 + u + 1))
                        copy(slots_hl[:, j, HI, :, :], slots[:, j, :, :]).then_inc(sl_hi, 1)
                if first:
                    context_squares(i)
                    text_hi(i, 0)
                    context_hi(i, 0)
                    text_hi(i, 1)
                else:
                    scale(0)
                    soft(0)
                    start(1)
                    attn_hi(0)
                    for u in range(UNITS):
                        if u + 1 < UNITS:
                            scale(u + 1)
                        reset_gate(u)
                        if u + 1 < UNITS:
                            soft(u + 1)
                        gates(u)
                        if u + 2 < UNITS:
                            start(u + 2)
                        slots_hi(u)
                        if u == 3 and not last:
                            context_squares(i)
                        if u == 4 and not last:
                            text_hi(i, 0)
                        if u + 1 < UNITS:
                            attn_hi(u + 1)
                        if u == 4 and not last:
                            context_hi(i, 0)
                            text_hi(i, 1)
                if not last:
                    next_slots_hi(0)
                    context_hi(i, 1)
                    next_slots_hi(1)
                    start(UNITS)
            cross(-1, first=True)
            with act.Fori(0, PAIRS - 1) as i:
                cross(i)
            cross(PAIRS - 1, last=True)
            act.drain().then_inc(done[2], 1)
            act.wait_ge(done[2], 4)
            def text(i, j):
                act.wait_ge(tT_mm, due(2, i, j + 1, back=1))
                copy(x2f[:, j, :, :], x2[:, bass.ds(i * (2 * NT) + j * NT, NT), :]).then_inc(xf_ok, 1)

            def text_hi(i, j):
                act.wait_ge(tT_mm, due(2, i, j + 1))
                act.wait_ge(h_mm, due(8, i, 4 * j + 4, back=1))
                copy(x2T_hl[:, j, HI, :, :], halves(j)).then_inc(tT_hi, 1)

            def experts(i, last):
                def exp_logits(j):
                    act.wait_ge(lT_mm, due(2, i, j + 1))
                    if j:
                        act.wait_ge(gt_ok, due(2, i, 1))
                    else:
                        act.wait_ge(gt_ok, due(2, i, 2, back=1))
                    act.activation(prb[:, :, 0:NE], bank[0][:, 0:NT * NE].rearrange("p (t e) -> p t e", t=NT),
                                   ACT.Exp, scale=-1.0).then_inc(lx_ok, 1)

                def gates_hi(j):
                    act.wait_ge(gT_mm, due(2, i, j + 1))
                    act.wait_ge(gb_mm, due(8, i, 4 * j + 4, back=1))
                    copy(gateT_hl[0:NE, j, :], bank[1 - j][0:NE, 0:T]).then_inc(gT_hi, 1)

                def relu(n):
                    act.wait_ge(h_mm, due(8, i, n + 1))
                    if n >= 4:
                        act.wait_ge(h_lo, due(8, i, n - 3))
                    else:
                        act.wait_ge(h_lo, due(8, i, 8 + n - 3, back=1))
                    act.activation(hid[:, n % 4, :, :], halves(4 + n % 2), ACT.Relu).then_inc(h_relu, 1)

                def hidden_hi(n):
                    j, g = n // 4, n % 4
                    act.wait_ge(h_ok, due(8, i, n + 1))
                    act.wait_ge(o_mm, due(2, i, j + 1, back=1))
                    copy(hid_hl[:, j, HI, 2 * g:2 * g + 2, :], hid[:, g, :, :]).then_inc(h_hi, 1)
                relu(0)
                relu(1)
                exp_logits(0)
                relu(2)
                gates_hi(0)
                relu(3)
                exp_logits(1)
                hidden_hi(0)
                hidden_hi(1)
                relu(4)
                hidden_hi(2)
                gates_hi(1)
                for n in range(3, 6):
                    hidden_hi(n)
                    relu(n + 2)
                if not last:
                    text(i + 1, 0)
                    text(i + 1, 1)
                hidden_hi(6)
                hidden_hi(7)
                if not last:
                    text_hi(i + 1, 0)
                    text_hi(i + 1, 1)
            text(0, 0)
            text(0, 1)
            text_hi(0, 0)
            text_hi(0, 1)
            with act.Fori(0, PAIRS - 1) as i:
                experts(i, False)
            experts(PAIRS - 1, True)

        @block.vector
        def _(dve):
            def sub_hi(dst, src, hi):
                return dve.tensor_tensor(dst, src, f32(hi), ALU.subtract)

            prep = [0]

            def step(ins):
                ins.then_inc(prep_dve, 1)
                prep[0] += 1
                dve.wait_ge(prep_dve, prep[0])

            dve.wait_ge(prep_act, 1)
            step(dve.scalar_tensor_tensor(wqkv_hl[:, LO, :, 0:D], st_qkv[:, :, 0:D], float(DH) ** -0.5,
                                          f32(wqkv_hl[:, HI, :, 0:D]), ALU.mult, ALU.subtract))
            dve.wait_ge(prep_act, 2)
            step(sub_hi(wqkv_hl[:, LO, :, D:], st_qkv[:, :, D:], wqkv_hl[:, HI, :, D:]))
            step(dve.tensor_scalar(bq_col[:, 0:NC], bq_col[:, 0:NC], float(DH) ** -0.5, None, ALU.mult))
            dve.wait_ge(prep_act, 3)
            step(sub_hi(wproj_hl[:, LO, :, :], st_proj[:, :, :], wproj_hl[:, HI, :, :]))
            dve.wait_ge(prep_act, 4)
            step(sub_hi(keys_hl[:, LO, :, :], st_keys[:, :, :], keys_hl[:, HI, :, :]))
            dve.wait_ge(prep_act, 5)
            step(sub_hi(values_hl[:, LO, :, :], st_values[:, :, :], values_hl[:, HI, :, :]))
            dve.wait_ge(w_in[2], 80)
            step(dve.tensor_tensor(brz_col[:, :], bih_col[:, 0:4], bhh_col[:, 0:4], ALU.add))
            step(dve.tensor_scalar(brz_col[:, :], brz_col[:, :], 0.5, None, ALU.mult))
            step(dve.tensor_scalar(slot_col[:, :], slot_col[:, :], float(D) ** -0.5, None, ALU.mult))
            dve.wait_ge(consts, 9)
            for e in range(2):
                step(dve.tensor_reduce(member[:, e:e + 1], ident[:, :].rearrange("p (h e d) -> p e h d", e=2, d=DH)[:, e, :, :],
                                       AX.XY, ALU.add))
            filled = [0]

            def bank_full():
                filled[0] += 1
                dve.wait_ge(prep_mm, filled[0])

            def into_hl(hi, lo, src, scale=None):
                n = src.free_size() if callable(src.free_size) else src.free_size
                if scale is None:
                    step(dve.tensor_copy(hi, src))
                    step(dve.tensor_tensor(lo, src, f32(hi), ALU.subtract))
                else:
                    step(dve.tensor_scalar(hi, src, scale, None, ALU.mult))
                    step(dve.scalar_tensor_tensor(lo, src, scale, f32(hi), ALU.mult, ALU.subtract))
            for c in range(NC):
                for half in range(2):
                    n0 = half * 4
                    m = 4 if half == 0 else 2
                    bank_full()
                    into_hl(whhT_hl[:, HI, c, n0 * P:(n0 + m) * P], whhT_hl[:, LO, c, n0 * P:(n0 + m) * P], bank[2 * c + half][:, 0:m * P])
            for c in range(NC):
                for half in range(2):
                    n0 = half * 4
                    m = 4 if half == 0 else 2
                    bank_full()
                    step(dve.tensor_copy(st_ihT[:, c, n0 * P:(n0 + m) * P], bank[4 + 2 * c + half][:, 0:m * P]))
            dve.drain().then_inc(prep_out, 1)
            bank_full()
            into_hl(eselT_hl[:, HI, :, :], eselT_hl[:, LO, :, :], bank[0][:, 0:NC * NE].rearrange("p (c e) -> p c e", c=NC))
            for c in range(NC):
                bank_full()
                into_hl(qk_w_hl[:, HI, c, :], qk_w_hl[:, LO, c, :], bank[1 + c][:, 0:D], input_col[:, c:c + 1])
            for c in range(NC):
                bank_full()
                into_hl(v_w_hl[:, HI, c, 0:512], v_w_hl[:, LO, c, 0:512], bank[3 + 2 * c][:, :], input_col[:, c:c + 1])
                bank_full()
                into_hl(v_w_hl[:, HI, c, 512:], v_w_hl[:, LO, c, 512:], bank[4 + 2 * c][:, 0:D], input_col[:, c:c + 1])
            dve.drain().then_inc(done[0], 1)
            dve.wait_ge(done[0], 4)

            def layer_norm(i, chain, per, src, stats, mv, std, var, rstd, k, result, ok):
                for t in range(NT):
                    ins = dve.bn_stats(stats[:, t, :], src(t))
                ins.then_inc(chain, 1)
                dve.wait_ge(chain, i * per + next_link())
                dve.sem_inc(passed, 1)
                for t in range(NT):
                    ins = dve.bn_aggr(mv[:, t, :], stats[:, t, :])
                ins.then_inc(chain, 1)
                dve.wait_ge(chain, i * per + next_link())
                dve.tensor_scalar(std[:, 0, :], mv[:, :, 1], LN_EPS, None, ALU.add).then_inc(var, 1)
                dve.wait_ge(rstd, due(2, i, k))
                for t in range(NT):
                    ins = dve.tensor_scalar(result(t), src(t), mv[:, t, 0:1], std[:, 1, t:t + 1], ALU.subtract, ALU.mult)
                ins.then_inc(ok, 1)

            with dve.Fori(0, PAIRS) as i:
                links[0] = 0
                for j in range(2):
                    dve.wait_ge(xT_hi, due(2, i, j + 1))
                    sub_hi(xT_hl[:, LO, :, :], halves(0), xT_hl[:, HI, :, :]).then_inc(xT_lo, 1)
                    dve.wait_ge(q_hi, due(2, i, j + 1))
                    for c in range(NC):
                        r = dve.scalar_tensor_tensor(q_hl[:, LO, c, :], halves(1)[:, c, :], bq_col[:, c:c + 1],
                                                     f32(q_hl[:, HI, c, :]), ALU.add, ALU.subtract)
                    r.then_inc(q_lo, 1)
                    dve.wait_ge(q_lo, due(2, i, j + 1))
                    for strip in range(4):
                        dve.wait_ge(ops_in[strip], due(2, i, j + 1, back=1, step=16 * 6))
                    for e in range(2):
                        r = dve.tensor_scalar(q_sep[:, j, :, :, e, :].rearrange("p a c t -> p (a c) t"),
                                              f32(q_hl[:, :, :, :]).rearrange("p a c t -> p (a c) t"),
                                              member[:, e:e + 1], None, ALU.mult)
                    r.then_inc(q_set, 1)
                    dve.wait_ge(k_hi, due(2, i, j + 1))
                    for c in range(NC):
                        r = dve.scalar_tensor_tensor(k_hl[:, j, LO, c, :], halves(2)[:, c, :], bq_col[:, NC + c:NC + c + 1],
                                                     f32(k_hl[:, j, HI, c, :]), ALU.add, ALU.subtract)
                    r.then_inc(k_lo, 1)
                    dve.wait_ge(v_mm, due(2, i, j + 1))
                    dve.wait_ge(vp_ok, due(2, i, j + 1, back=1))
                    for t in range(NT):
                        r = dve.tensor_copy(v_sb[:, j, t, :], halves(0)[:, t, :])
                    r.then_inc(v_ok, 1)
                for j in range(2):
                    def probs_out(h):
                        n = 16 * j + h
                        dve.wait_ge(pT_mm, due(32, i, n + 1))
                        if n >= 4:
                            dve.wait_ge(pv_mm, due(32, i, n - 3))
                        else:
                            dve.wait_ge(pv_mm, due(32, i, 32 + n - 3, back=1))
                        dve.tensor_copy(probT[:, h % 4, :], bank[6][:, 0:SQ]).then_inc(pT_even, 1)
                    for hp in range(H // 2 + 1):
                        if hp < H // 2:
                            for qt in range(NT):
                                n = 16 * j + 2 * hp + qt
                                dve.wait_ge(s_mm, due(32, i, n + 1))
                                size = P if qt == 0 else 2 * P
                                dve.wait_ge(exp_ok, due(32, i, n - 15 if n >= 16 else n + 17, back=0 if n >= 16 else 1))
                                dve.tensor_reduce(neg_max[:, hp, qt, :], halves(4 + qt)[:, :, 0:size],
                                                                AX.X, ALU.max, negate=True).then_inc(max_ok, 1)
                        if hp >= 1:
                            probs_out(2 * hp - 2)
                    dve.wait_ge(exp_ok, due(32, i, 16 * (j + 1)))
                    dve.reciprocal(inv_sum[:, :, :], row_sum[:, :, :]).then_inc(attn_chain, 1)
                    dve.wait_ge(attn_chain, i * ATTN_LINKS + next_link())
                    dve.tensor_copy(inv_wide[:, :, :].rearrange("p t (h d) -> p (t h) d", d=DH),
                                                  inv_sum[:, :, :].rearrange("p t h -> p (t h)").unsqueeze(2)
                                                  .to_broadcast([P, NT * H, DH])).then_inc(inv_ok, 1)
                    dve.wait_ge(ib_ok, due(2, i, j + 1))
                    dve.wait_ge(pv_mm, due(32, i, 16 * (j + 1)))
                    dve.tensor_tensor(yn[:, :, :], halves(3), inv_bc[:, :, :], ALU.mult).then_inc(yn_ok, 1)
                    dve.wait_ge(pr_mm, due(2, i, j + 1))
                    dve.wait_ge(xr_ok, due(2, i, j + 1))
                    dve.tensor_tensor(u1[:, :, :], halves(2), xr[:, j, :, :], ALU.add).then_inc(u1_ok, 1)
                    dve.wait_ge(u1_ok, due(2, i, j + 1))
                    layer_norm(i, attn_chain, ATTN_LINKS, lambda t: u1[:, t, :], stats1, mv1, std1, var1, rstd1, j + 1,
                               lambda t: u1[:, t, :], x1_ok)
                assert links[0] == ATTN_LINKS
            dve.drain().then_inc(done[1], 1)
            dve.wait_ge(done[1], 4)

            def context_mean(r):
                for j in range(2):
                    dve.wait_ge(c_sq, due(2, r, 2 + j + 1))
                    dve.tensor_scalar(c_ms[:, j, :], c_ss[:, j, :], 1.0 / D, RMS_EPS, ALU.mult, ALU.add).then_inc(c_mean, 1)

            def text_lo(r, j):
                dve.wait_ge(cT_hi, due(2, r, 2 + j + 1))
                sub_hi(cT_hl[:, LO, :, :], halves(BANK2["cT", j]), cT_hl[:, HI, :, :]).then_inc(cT_lo, 1)

            def context_lo(r, j):
                dve.wait_ge(kT_hi, due(2, r, 2 + j + 1))
                for c in range(NC):
                    ins = dve.scalar_tensor_tensor(kT_hl[:, j, LO, c, :], halves(BANK2["kT", j])[:, c, :], slot_col[:, c:c + 1],
                                                   f32(kT_hl[:, j, HI, c, :]), ALU.mult, ALU.subtract)
                ins.then_inc(kT_lo, 1)
                for g in range(3):
                    dve.wait_ge(vg_hi, due(6, r, 6 + 3 * j + g + 1))
                    for first, size, t in VG_ROWS[g]:
                        ins = dve.scalar_tensor_tensor(vg_hl[:, j, LO, 2 * g + first:2 * g + first + size, :],
                                                       halves(BANK2["vg", 3 * j + g])[:, first:first + size, :], c_rs[:, j, t:t + 1],
                                                       f32(vg_hl[:, j, HI, 2 * g + first:2 * g + first + size, :]), ALU.mult, ALU.subtract)
                    ins.then_inc(vg_lo, 1)

            def cross(i, first=False, last=False):
                links[0] = 0

                def next_slots(j):
                    dve.wait_ge(uT_mm, due(2, i, j + 1))
                    dve.tensor_copy(slots[:, j, :, :], x1T[:, :, bass.ds((i + 1) * (2 * T) + j * T, T)]).then_inc(sl_ok, 1)

                def start(u):
                    dve.wait_ge(sq_ok, due(UNITS, i, u + 1))
                    dve.tensor_tensor(sq[:, 0, :], sq[:, 0, :], sq[:, 1, :], ALU.add).then_inc(sqs_ok, 1)

                def mean_square(u):
                    j = u % 2
                    dve.wait_ge(ss_mm, due(UNITS, i, u + 1))
                    dve.tensor_scalar(s_ms[:, j, :], bank[0][:, 0:NT], RMS_EPS, None, ALU.add).then_inc(ms_ok, 1)

                def soft(u):
                    j = u % 2
                    dve.wait_ge(sc_mm, due(UNITS, i, u + 1))
                    dve.wait_ge(rb_ok, due(UNITS, i, u + 1))
                    dve.wait_ge(c_kept, due(1, i, 1))
                    for t in range(NT):
                        r = dve.scalar_tensor_tensor(attn[:, j, t, :], halves(3)[:, t, :], c_now[:, j, t:t + 1], rs_bc[:, j, :],
                                                     ALU.mult, ALU.mult)
                    r.then_inc(sc_ok, 1)
                    dve.wait_ge(sc_ok, due(UNITS, i, u + 1))
                    dve.tensor_reduce(s_max[:, j, :], attn[:, j, :, :], AX.X, ALU.max, negate=True).then_inc(smax_ok, 1)

                def soft_sum(u):
                    j = u % 2
                    dve.wait_ge(e_ok, due(UNITS, i, u + 1))
                    dve.reciprocal(s_inv[:, j, :], s_sum[:, j, :]).then_inc(z_ok, 1)

                def totals(u):
                    dve.wait_ge(tt_mm, due(UNITS, i, u + 1))
                    dve.tensor_scalar(tot[:, :], bank[2][:, 0:T], RMS_EPS, None, ALU.add).then_inc(tt_ok, 1)
                    dve.wait_ge(tt_ok, due(UNITS, i, u + 1))
                    dve.reciprocal(inv_tot[:, :], tot[:, :]).then_inc(it_ok, 1)

                def weights(u):
                    j = u % 2
                    dve.wait_ge(it_ok, due(UNITS, i, u + 1))
                    for t in range(NT):
                        r = dve.scalar_tensor_tensor(attn[:, j, t, :], attn[:, j, t, :], s_inv[:, j, t:t + 1], inv_tot[:, :],
                                                     ALU.mult, ALU.mult)
                    r.then_inc(at_ok, 1)

                def reset_gate(u):
                    dve.wait_ge(r_ok, due(UNITS, i, u + 1))
                    dve.tensor_scalar(gate_r[:, :, :], gate_r[:, :, :], 0.5, 0.5, ALU.mult, ALU.add).then_inc(cross_chain, 1)
                    dve.wait_ge(cross_chain, i * CROSS_LINKS + next_link())
                    dve.wait_ge(hn_mm, due(UNITS, i, u + 1))
                    for c in range(NC):
                        r = dve.scalar_tensor_tensor(gate_r[:, c, :], halves(6)[:, c, :], bhh_col[:, 2 * NC + c:2 * NC + c + 1],
                                                     gate_r[:, c, :], ALU.add, ALU.mult)
                    r.then_inc(g_ok, 1)

                def gates(u):
                    j = u % 2
                    dve.wait_ge(g_ok, due(UNITS, i, u + 1))
                    dve.wait_ge(xn_mm, due(UNITS, i, u + 1))
                    dve.tensor_tensor(gate_r[:, :, :], halves(7), gate_r[:, :, :], ALU.add).then_inc(np_ok, 1)
                    dve.wait_ge(n_ok, due(UNITS, i, u + 1))
                    dve.tensor_tensor(diff[:, :, :], slots[:, j, :, :], cand[:, :, :], ALU.subtract).then_inc(cross_chain, 1)
                    dve.wait_ge(cross_chain, i * CROSS_LINKS + next_link())
                    dve.wait_ge(zt_ok, due(UNITS, i, u + 1))
                    dve.scalar_tensor_tensor(diff[:, :, :], gate_z[:, :, :], 1.0, diff[:, :, :], ALU.add, ALU.mult).then_inc(cross_chain, 1)
                    dve.wait_ge(cross_chain, i * CROSS_LINKS + next_link())
                    dve.scalar_tensor_tensor(slots[:, j, :, :], diff[:, :, :], 0.5, cand[:, :, :], ALU.mult, ALU.add).then_inc(sl_ok, 1)

                def residual(j):
                    dve.wait_ge(sl_ok, due(8, i, 7 + j))
                    dve.tensor_tensor(slots[:, j, :, :], slots[:, j, :, :],
                                      x1T[:, :, bass.ds(i * (2 * T) + j * T, T)], ALU.add).then_inc(uu_ok, 1)

                def between(u):
                    if u + 1 < UNITS:
                        start(u + 1)
                    if u < UNITS:
                        totals(u)
                    if u + 1 < UNITS:
                        mean_square(u + 1)
                    if u < UNITS:
                        weights(u)

                def norm(j):
                    dve.wait_ge(uT_mm, due(2, i, j + 1))
                    layer_norm(i, cross_chain, CROSS_LINKS, lambda t: halves(BANK2["uT", j])[:, t, :], stats2, mv2, std2, var2, rstd2, j + 1,
                               lambda t: x2[:, bass.ds(i * (2 * NT) + j * NT + t, 1), :], x2_ok)
                if first:
                    context_mean(i)
                    text_lo(i, 0)
                    context_lo(i, 0)
                    text_lo(i, 1)
                else:
                    soft(0)
                    soft_sum(0)
                    between(0)
                    for u in range(UNITS):
                        if u + 1 < UNITS:
                            soft(u + 1)
                        reset_gate(u)
                        if u + 1 < UNITS:
                            soft_sum(u + 1)
                        gates(u)
                        if u == 4 and not last:
                            text_lo(i, 0)
                        between(u + 1)
                        if u == 3 and not last:
                            context_mean(i)
                        if u == 4:
                            residual(0)
                            if not last:
                                context_lo(i, 0)
                                text_lo(i, 1)
                    residual(1)
                if not last:
                    next_slots(0)
                    context_lo(i, 1)
                    next_slots(1)
                    start(UNITS)
                    dve.wait_ge(c_rstd, due(2, i, 2 + 2))
                    dve.tensor_copy(c_now[:, :, :], c_rs[:, :, :]).then_inc(c_kept, 1)
                if not first:
                    norm(0)
                if not last:
                    mean_square(UNITS)
                if not first:
                    norm(1)
                    assert links[0] == CROSS_LINKS
            cross(-1, first=True)
            with dve.Fori(0, PAIRS - 1) as i:
                cross(i)
            cross(PAIRS - 1, last=True)
            dve.drain().then_inc(done[2], 1)
            dve.wait_ge(done[2], 4)

            def text_lo(i, j):
                dve.wait_ge(tT_hi, due(2, i, j + 1))
                sub_hi(x2T_hl[:, j, LO, :, :], halves(j), x2T_hl[:, j, HI, :, :]).then_inc(tT_lo, 1)

            def experts(i, last):
                links[0] = 0

                def logits(j):
                    dve.wait_ge(lg_mm, due(2, i, j + 1))
                    dve.tensor_copy(logT[:, j, :], bank[2][0:NE, 0:T]).then_inc(lg_ok, 1)

                def route(j):
                    dve.wait_ge(lx_ok, due(2, i, j + 1))
                    dve.tensor_scalar(prb[:, :, 0:NE], prb[:, :, 0:NE], 1.0, None, ALU.add).then_inc(expert_chain, 1)
                    dve.wait_ge(expert_chain, i * EXPERT_LINKS + next_link())
                    dve.reciprocal(prb[:, :, 0:NE], prb[:, :, 0:NE]).then_inc(expert_chain, 1)
                    dve.wait_ge(expert_chain, i * EXPERT_LINKS + next_link())
                    dve.sem_inc(passed, 1)
                    for t in range(NT):
                        r = dve.max(top8[:, t, :], prb[:, t, 0:NE])
                    r.then_inc(expert_chain, 1)
                    dve.wait_ge(expert_chain, i * EXPERT_LINKS + next_link())
                    dve.memset(top8[:, :, TOPK:], -1.0).then_inc(expert_chain, 1)
                    dve.wait_ge(expert_chain, i * EXPERT_LINKS + next_link())
                    dve.sem_inc(passed, 1)
                    for t in range(NT):
                        r = dve.match_replace(prbx[:, t, :], top8[:, t, :], prb[:, t, :], 0.0)
                    r.then_inc(expert_chain, 1)
                    dve.wait_ge(expert_chain, i * EXPERT_LINKS + next_link())
                    dve.tensor_tensor(gate[:, :, :], prb[:, :, 0:NE], prbx[:, :, 0:NE], ALU.subtract).then_inc(expert_chain, 1)
                    dve.wait_ge(expert_chain, i * EXPERT_LINKS + next_link())
                    dve.tensor_reduce(gsum[:, :], gate[:, :, :], AX.X, ALU.add).then_inc(expert_chain, 1)
                    dve.wait_ge(expert_chain, i * EXPERT_LINKS + next_link())
                    dve.tensor_scalar(gsum[:, :], gsum[:, :], 1e-9, None, ALU.max).then_inc(expert_chain, 1)
                    dve.wait_ge(expert_chain, i * EXPERT_LINKS + next_link())
                    dve.reciprocal(ginv[:, :], gsum[:, :]).then_inc(expert_chain, 1)
                    dve.wait_ge(expert_chain, i * EXPERT_LINKS + next_link())
                    for t in range(NT):
                        r = dve.tensor_scalar(gate[:, t, :], gate[:, t, :], ginv[:, t:t + 1], route_col[:, 0:1], ALU.mult, ALU.mult)
                    r.then_inc(gt_ok, 1)

                def gates_lo(j):
                    dve.wait_ge(gT_hi, due(2, i, j + 1))
                    sub_hi(gateT_hl[32:32 + NE, j, :], bank[1 - j][0:NE, 0:T], gateT_hl[0:NE, j, :]).then_inc(gT_lo, 1)

                def gated(n):
                    dve.wait_ge(h_relu, due(8, i, n + 1))
                    dve.wait_ge(gb_mm, due(8, i, n + 1))
                    dve.tensor_tensor(hid[:, n % 4, :, :], halves(6 + n % 2), hid[:, n % 4, :, :], ALU.mult).then_inc(h_ok, 1)
                logits(0)
                route(0)
                logits(1)
                gates_lo(0)
                gated(0)
                gated(1)
                route(1)
                gated(2)
                gates_lo(1)
                for n in range(3, 8):
                    gated(n)
                if not last:
                    text_lo(i + 1, 0)
                    text_lo(i + 1, 1)
                for j in range(2):
                    dve.wait_ge(o_mm, due(2, i, j + 1))
                    dve.wait_ge(y_ok, due(2, i, 1 if j else 2, back=1 - j))
                    dve.tensor_tensor(u3[:, :, :], halves(2 + j), x2[:, bass.ds(i * (2 * NT) + j * NT, NT), :], ALU.add).then_inc(u3_ok, 1)
                    dve.wait_ge(u3_ok, due(2, i, j + 1))
                    dve.wait_ge(stored[j], due(1, i, 1, back=1, step=16))
                    layer_norm(i, expert_chain, EXPERT_LINKS, lambda t: u3[:, t, :], stats3, mv3, std3, var3, rstd3, j + 1,
                               lambda t: y_out[:, j, t, :], y_ok)
                assert links[0] == EXPERT_LINKS
            text_lo(0, 0)
            text_lo(0, 1)
            with dve.Fori(0, PAIRS - 1) as i:
                experts(i, False)
            experts(PAIRS - 1, True)

        @block.tensor
        def _(pe):
            pe.wait_ge(consts, 9)
            pe.wait_ge(w_in[1], 96)
            for n, w in enumerate((st_hh, st_ih)):
                for c in range(NC):
                    for half in range(2):
                        for q in range(4 if half == 0 else 2):
                            mm = pe.transpose(bank[4 * n + 2 * c + half][:, q * P:(q + 1) * P],
                                              w[:, 4 * half + q, c * P:(c + 1) * P], ident[:, :])
                        mm.then_inc(prep_mm, 1)
            pe.wait_ge(prep_out, 1)
            for c in range(NC):
                mm = pe.transpose(bank[0][:, c * NE:(c + 1) * NE], st_esel[:, c * P:(c + 1) * P], ident[0:NE, 0:NE])
            mm.then_inc(prep_mm, 1)
            for c in range(NC):
                for o in range(NC):
                    mm = pe.matmul(bank[1 + c][:, 0:D], st_wk[:, o, c * P:(c + 1) * P], st_wq[:, o, :], start=o == 0, stop=o == 1)
                mm.then_inc(prep_mm, 1)
            for c in range(NC):
                for b, lo, size in ((3 + 2 * c, 0, 512), (4 + 2 * c, 512, 256)):
                    for o in range(NC):
                        mm = pe.matmul(bank[b][:, 0:size], st_wv[:, o, c * P:(c + 1) * P], st_ihT[:, o, lo:lo + size],
                                       start=o == 0, stop=o == 1)
                    mm.then_inc(prep_mm, 1)
            pe.drain().then_inc(done[0], 1)
            pe.wait_ge(done[0], 4)
            pe.wait_ge(consts, 10)

            with pe.Fori(0, PAIRS) as i:
                for j in range(2):
                    b, read, count = bank_free(jobs1, i, ("xT", j))
                    pe.wait_ge(read, count)
                    pe.wait_ge(x_arr[j], due(1, i, 1, step=16))
                    transpose4(pe, 0, lambda t, c: x_in[:, j, t, c * P:(c + 1) * P]).then_inc(xT_mm, 1)
                    pe.wait_ge(xT_lo, due(2, i, j + 1))
                    for name, ev, base in (("q", q_mm, 0), ("k", k_mm, D)):
                        b, read, count = bank_free(jobs1, i, (name, j))
                        pe.wait_ge(read, count)
                        for m in range(NC):
                            for c in range(NC):
                                cols = slice(base + m * P, base + (m + 1) * P)
                                mm = split3(pe, halves(b)[:, m, :], lambda a: wqkv_hl[:, a, c, cols],
                                            lambda a: xT_hl[:, a, c, :], c == 0, c == 1)
                        mm.then_inc(ev, 1)
                    b, read, count = bank_free(jobs1, i, ("v", j))
                    pe.wait_ge(read, count)
                    for t in range(NT):
                        for c in range(NC):
                            mm = split3(pe, halves(b)[:, t, :], lambda a: xT_hl[:, a, c, t * P:(t + 1) * P],
                                        lambda a: wqkv_hl[:, a, c, 2 * D:], c == 0, c == 1)
                    mm.then_inc(v_mm, 1)
                for j in range(2):
                    for hp in range(H // 2 + 2):
                        if hp < H // 2:
                            if hp % 2 == 0:
                                pe.wait_ge(ops_in[hp // 2], due(2, i, j + 1, step=16 * 6))
                            pair = head(2 * hp) // 2
                            for qt in range(NT):
                                n = 16 * j + 2 * hp + qt
                                b, read, count = bank_free(jobs1, i, ("s", n))
                                pe.wait_ge(read, count)
                                rows = slice(qt * P, (qt + 1) * P)
                                for e in range(2):
                                    pe.matmul(halves(b)[:, e, :], q_op[:, pair, e, rows], k_op[:, pair, :],
                                              start=e == 0, stop=False, skip_group_check=True)
                                pe.matmul(halves(b)[:, :, rows], ident16[:, :], mask16[:, :, :],
                                                      start=False, stop=True, skip_group_check=True).then_inc(s_mm, 1)
                        if 1 <= hp <= H // 2:
                            for e in range(2):
                                h = 2 * (hp - 1) + e
                                n = 16 * j + h
                                b, read, count = bank_free(jobs1, i, ("pT", n))
                                pe.wait_ge(read, count)
                                pe.wait_ge(exp_ok, due(32, i, 16 * j + 2 * hp))
                                for q, lo in enumerate((0, P, 2 * P)):
                                    mm = pe.transpose(bank[b][:, lo:lo + P], prob[:, (hp - 1) % 2, e, lo:lo + P], ident[:, :])
                                mm.then_inc(pT_mm, 1)
                        if hp >= 2:
                            if hp == 2:
                                b, read, count = bank_free(jobs1, i, ("y", j))
                                pe.wait_ge(read, count)
                                pe.wait_ge(vp_ok, due(2, i, j + 1))
                            for e in range(2):
                                h = 2 * (hp - 2) + e
                                pe.wait_ge((pT_even, pT_odd)[e], due(16, i, 8 * j + h // 2 + 1))
                                c = head(h) // 8
                                pe.matmul(halves(3)[:, c, :], v_pad[:, 0, head(h), :], probT[:, h % 4, 0:T],
                                          start=h == 0, stop=False, skip_group_check=True)
                                pe.matmul(halves(3)[:, c, P:], v_pad[:, 1, head(h), :], probT[:, h % 4, T:],
                                                       start=False, stop=h == H - 1, skip_group_check=True).then_inc(pv_mm, 1)
                    b, read, count = bank_free(jobs1, i, ("ib", j))
                    pe.wait_ge(read, count)
                    pe.wait_ge(inv_ok, due(2, i, j + 1))
                    for c in range(NC):
                        for t in range(NT):
                            mm = pe.matmul(halves(b)[:, c, t * P:(t + 1) * P], inv_wide[:, t, c * P:(c + 1) * P],
                                           ident[:, :], start=True, stop=True)
                    mm.then_inc(ib_mm, 1)
                    b, read, count = bank_free(jobs1, i, ("pr", j))
                    pe.wait_ge(read, count)
                    pe.wait_ge(y_lo, due(2, i, j + 1))
                    for t in range(NT):
                        for c in range(NC):
                            mm = split3(pe, halves(b)[:, t, :], lambda a: y_hl[:, a, c, t * P:(t + 1) * P],
                                        lambda a: wproj_hl[:, a, c, :], c == 0, c == 1)
                    mm.then_inc(pr_mm, 1)
                    b, read, count = bank_free(jobs1, i, ("x1T", j))
                    pe.wait_ge(read, count)
                    pe.wait_ge(x1_ok, due(2, i, j + 1))
                    transpose4(pe, b, lambda t, c: u1[:, t, c * P:(c + 1) * P]).then_inc(x1T_mm, 1)
            pe.drain().then_inc(done[1], 1)
            pe.wait_ge(done[1], 4)

            def context_text(r, j):
                b, read, count = bank_free(jobs2, r, ("cT", j))
                pe.wait_ge(read, count)
                pe.wait_ge(c_arr[j], due(1, r, 2, step=16))
                transpose4(pe, b, lambda t, c: c_in[:, j, t, c * P:(c + 1) * P]).then_inc(cT_mm, 1)

            def context_keys(r, j):
                pe.wait_ge(cT_lo, due(2, r, 2 + j + 1))
                b, read, count = bank_free(jobs2, r, ("kT", j))
                pe.wait_ge(read, count)
                for m in range(NC):
                    for c in range(NC):
                        mm = split3(pe, halves(b)[:, m, :], lambda a: qk_w_hl[:, a, c, m * P:(m + 1) * P],
                                    lambda a: cT_hl[:, a, c, :], c == 0, c == 1)
                mm.then_inc(kT_mm, 1)

            def context_values(r, j):
                for g in range(3):
                    b, read, count = bank_free(jobs2, r, ("vg", 3 * j + g))
                    pe.wait_ge(read, count)
                    for half in range(2):
                        t, blk = divmod(2 * g + half, 3)
                        for c in range(NC):
                            mm = split3(pe, halves(b)[:, half, :], lambda a: cT_hl[:, a, c, t * P:(t + 1) * P],
                                        lambda a: v_w_hl[:, a, c, blk * D:(blk + 1) * D], c == 0, c == 1)
                    mm.then_inc(vg_mm, 1)

            def cross(i, first=False, last=False):
                def start(u):
                    j = u % 2
                    b, read, count = bank_free(jobs2, i, ("ss", u))
                    pe.wait_ge(read, count)
                    pe.wait_ge(sqs_ok, due(UNITS, i, u + 1))
                    for t in range(NT):
                        mm = pe.matmul(bank[b][:, t:t + 1], sq[:, 0, t * P:(t + 1) * P], mean_col[:, :], start=True, stop=True)
                    mm.then_inc(ss_mm, 1)
                    b, read, count = bank_free(jobs2, i, ("sc", u))
                    pe.wait_ge(read, count)
                    pe.wait_ge(sl_hi, due(6, i, u + 1))
                    pe.wait_ge(kT_lo, due(2, i, j + 1 + (2 if u == UNITS else 0)))
                    for n, (k_part, s_part) in enumerate(HI_FIRST):
                        if s_part == LO:
                            pe.wait_ge(sl_lo, due(6, i, u + 1))
                        for t in range(NT):
                            for c in range(NC):
                                mm = pe.matmul(halves(b)[:, t, :], kT_hl[:, j, k_part, c, t * P:(t + 1) * P], slots_hl[:, j, s_part, c, :],
                                               start=n + t + c == 0, stop=n == 2, skip_group_check=True)
                    mm.then_inc(sc_mm, 1)
                    b, read, count = bank_free(jobs2, i, ("rb", u))
                    pe.wait_ge(read, count)
                    pe.wait_ge(rs_ok, due(UNITS, i, u + 1))
                    for t in range(NT):
                        mm = pe.matmul(bank[b][:, t * P:(t + 1) * P], s_rs[:, j, t:t + 1].to_broadcast([P, P]), ident[:, :],
                                       start=True, stop=True)
                    mm.then_inc(rb_mm, 1)

                def state(u):
                    j = u % 2
                    for n, name in enumerate(("r", "z", "hn")):
                        b, read, count = bank_free(jobs2, i, (name, u))
                        pe.wait_ge(read, count)
                        for m in range(NC):
                            cols = slice(n * D + m * P, n * D + (m + 1) * P)
                            for c in range(NC):
                                mm = split3(pe, halves(b)[:, m, :], lambda a: whhT_hl[:, a, c, cols],
                                            lambda a: slots_hl[:, j, a, c, :], m == 0 and c == 0, False)
                    mm.then_inc(hn_mm, 1)

                def totals(u):
                    j = u % 2
                    b, read, count = bank_free(jobs2, i, ("tt", u))
                    pe.wait_ge(read, count)
                    pe.wait_ge(z_ok, due(UNITS, i, u + 1))
                    for t in range(NT):
                        mm = pe.matmul(bank[b][:, 0:T], s_inv[:, j, t:t + 1].to_broadcast([P, P]), attn[:, j, t, :],
                                       start=t == 0, stop=t == 1)
                    mm.then_inc(tt_mm, 1)

                def inputs(u):
                    j = u % 2
                    pe.wait_ge(at_hi, due(UNITS, i, u + 1))
                    pe.wait_ge(vg_lo, due(6, i, 3 * j + 3))
                    for n, b, ev in ((0, 4, r_mm), (2, 7, xn_mm), (1, 5, z_mm)):
                        if n == 2:
                            b, read, count = bank_free(jobs2, i, ("xn", u))
                            pe.wait_ge(read, count)
                        for a, (v_part, at_part) in enumerate(HI_FIRST):
                            if n == 0 and at_part == LO:
                                pe.wait_ge(at_lo, due(UNITS, i, u + 1))
                            for m in range(NC):
                                for t in range(NT):
                                    r, q = divmod(n * D + m * P, D)
                                    mm = pe.matmul(halves(b)[:, m, :], vg_hl[:, j, v_part, 3 * t + r, q:q + P], attn_hl[:, j, at_part, t, :],
                                                   start=n == 2 and a + m + t == 0, stop=True, skip_group_check=True)
                        mm.then_inc(ev, 1)
                def text(j):
                    b, read, count = bank_free(jobs2, i, ("uT", j), last)
                    pe.wait_ge(read, count)
                    pe.wait_ge(uu_ok, due(2, i, j + 1))
                    transpose4(pe, b, lambda c, t: slots[:, j, c, t * P:(t + 1) * P]).then_inc(uT_mm, 1)
                if first:
                    context_text(i, 0)
                    context_keys(i, 0)
                    context_values(i, 0)
                    context_text(i, 1)
                else:
                    state(0)
                    totals(0)
                    for u in range(UNITS):
                        if u + 1 < UNITS:
                            start(u + 1)
                        inputs(u)
                        if u == 4 and not last:
                            context_text(i, 0)
                        if u + 1 < UNITS:
                            totals(u + 1)
                            state(u + 1)
                        if u == 4 and not last:
                            context_keys(i, 0)
                            context_values(i, 0)
                            context_text(i, 1)
                if not last:
                    context_keys(i, 1)
                if not first:
                    text(0)
                if not last:
                    context_values(i, 1)
                if not first:
                    text(1)
                if not last:
                    start(UNITS)
            cross(-1, first=True)
            with pe.Fori(0, PAIRS - 1) as i:
                cross(i)
            cross(PAIRS - 1, last=True)
            pe.drain().then_inc(done[2], 1)
            pe.wait_ge(done[2], 4)

            def text(j):
                transpose4(pe, j, lambda t, c: x2f[:, j, t, c * P:(c + 1) * P]).then_inc(tT_mm, 1)

            def experts(i, last):
                for name, n in EXPERT_ORDER:
                    if name == "tT" and last:
                        continue
                    b, read, count = bank_free(jobs3, i, (name, n))
                    pe.wait_ge(read, count)
                    j = n // 4 if name in ("h", "gb") else n
                    g = n % 4
                    if name == "tT":
                        pe.wait_ge(xf_ok, due(2, i, 2 + j + 1))
                        text(j)
                    elif name == "lg":
                        pe.wait_ge(tT_lo, due(2, i, j + 1))
                        for c in range(NC):
                            mm = split3(pe, bank[b][0:NE, 0:T], lambda a: eselT_hl[:, a, c, :], lambda a: x2T_hl[:, j, a, c, :], c == 0, c == 1)
                        mm.then_inc(lg_mm, 1)
                    elif name == "lT":
                        pe.wait_ge(lg_ok, due(2, i, j + 1))
                        pe.sem_inc(passed, 1)
                        for t in range(NT):
                            mm = pe.transpose(bank[b][:, t * NE:(t + 1) * NE], logT[:, j, t * P:(t + 1) * P], ident[0:NE, 0:NE])
                        mm.then_inc(lT_mm, 1)
                    elif name == "gT":
                        pe.wait_ge(gt_ok, due(2, i, j + 1))
                        for t in range(NT):
                            mm = pe.transpose(bank[b][0:NE, t * P:(t + 1) * P], gate[:, t, :], ident[:, :])
                        mm.then_inc(gT_mm, 1)
                    elif name == "h":
                        for half in range(2):
                            m = 2 * g + half
                            for c in range(NC):
                                mm = split3(pe, halves(b)[:, half, :], lambda a: keys_hl[:, a, c, m * P:(m + 1) * P],
                                            lambda a: x2T_hl[:, j, a, c, :], c == 0, c == 1)
                        mm.then_inc(h_mm, 1)
                    elif name == "gb":
                        pe.wait_ge(gT_lo, due(2, i, j + 1))
                        for half in range(2):
                            mm = pe.matmul(halves(b)[:, half, :], spread[:, 2 * g + half, :], gateT_hl[:, j, :], start=True, stop=True)
                        mm.then_inc(gb_mm, 1)
                    else:
                        pe.wait_ge(h_lo, due(8, i, 4 * j + 4))
                        for t in range(NT):
                            for m in range(NH):
                                mm = split3(pe, halves(b)[:, t, :], lambda a: hid_hl[:, j, a, m, t * P:(t + 1) * P],
                                            lambda a: values_hl[:, a, m, :], m == 0, m == NH - 1)
                        mm.then_inc(o_mm, 1)
            for j in range(2):
                pe.wait_ge(xf_ok, due(2, 0, j + 1))
                text(j)
            pe.wait_ge(consts, 16)
            with pe.Fori(0, PAIRS - 1) as i:
                experts(i, False)
            experts(PAIRS - 1, True)
        s3.close()


_INS = ['x', 'ctx_1024', 'L0_attn_w_qkv', 'L0_attn_b_qkv', 'L0_attn_w_proj', 'L0_attn_b_proj', 'L0_xattn_Wq',
        'L0_xattn_Wk', 'L0_xattn_Wv', 'L0_xattn_gru_wih', 'L0_xattn_gru_whh', 'L0_xattn_gru_bih', 'L0_xattn_gru_bhh',
        'L0_xattn_slot_norm_w', 'L0_xattn_input_norm_w', 'L0_ffn_expert_sel', 'L0_ffn_keys', 'L0_ffn_values',
        'L0_ffn_route_scale']


def kernel(**inputs):
    import numpy as _np
    import concourse.bacc as _bacc
    from concourse import mybir as _mybir
    from concourse.bass_utils import run_bass_kernel_spmd as _run

    nc = _bacc.Bacc("TRN2", target_bir_lowering=False, num_devices=1)
    arrays, args = {}, []
    for name in _INS:
        a = _np.ascontiguousarray(inputs[name])
        arrays[f"in_{name}_dram"] = a
        args.append(nc.dram_tensor(f"in_{name}_dram", a.shape, _mybir.dt.from_np(a.dtype), kind="ExternalInput").ap())
    args.append(nc.dram_tensor("out_dram", (B, T, D), _mybir.dt.float32, kind="ExternalOutput").ap())
    decoder_layer(nc, *args)
    r = _run(nc, [arrays], core_ids=[0])
    return r.results[0]["out_dram"]
```

```python
from contextlib import ExitStack

import concourse.bass as bass
from concourse import mybir

F32, F32R, BF16 = mybir.dt.float32, mybir.dt.float32r, mybir.dt.bfloat16
ALU = mybir.AluOpType
ACT = mybir.ActivationFunctionType
AX = mybir.AxisListType

B, T, D = 8, 256, 256
P = 128
H, DH = 16, 16
NT = T // P
NC = D // P
G3 = 3 * D
NE, EH, TOPK = 16, 64, 4
NH = NE * EH // P
ITERS = 3
PAIRS = B // 2
LN_EPS, RMS_EPS = 1e-5, 1e-6
MASKED = -1e30
HI, LO = 0, 1
PASSES = ((HI, HI), (HI, LO), (LO, HI))
HI_FIRST = ((HI, HI), (LO, HI), (HI, LO))
FIRST = -1
UNITS = 2 * ITERS
SQ = 384


ATTN_LINKS = 2 * 3
CROSS_LINKS = UNITS * 3 + 2 * 2
EXPERT_LINKS = 2 * 11


def head(n):
    pair = 4 * (n // 2 % 2) + n // 4
    return 2 * pair + n % 2


def due(per, i, k, back=0, step=1):
    return (i * per + (1 - back) * per + k) * step


def decoder_layer(nc, x, ctx_in, w_qkv, b_qkv, w_proj, b_proj, wq, wk, wv, wih, whh, bih, bhh,
                  slot_w, input_w, expert_sel, keys, values, route_scale, out):
    stack = ExitStack()
    with stack:
        def sb(name, shape, dt=F32, where=stack):
            return where.enter_context(nc.sbuf_tensor(name, shape, dt))

        def sem(name):
            return stack.enter_context(nc.semaphore(name))

        events = []
        passed = sem("passed")

        def event(name, per, step=1):
            events.append((sem(name), per * step))
            return events[-1][0]

        ident = sb("ident", [P, P])
        ident16 = sb("ident16", [P, P], BF16)
        mask16 = sb("mask16", [P, 2, P], BF16)
        mask32 = sb("mask32", [P, P])
        mean_col = sb("mean_col", [P, 1])
        half_neg = sb("half_neg", [P, 2])
        wqkv_hl = sb("wqkv_hl", [P, 2, NC, G3], F32R)
        wproj_hl = sb("wproj_hl", [P, 2, NC, D], F32R)
        qk_w_hl = sb("qk_w_hl", [P, 2, NC, D], F32R)
        v_w_hl = sb("v_w_hl", [P, 2, NC, G3], F32R)
        whhT_hl = sb("whhT_hl", [P, 2, NC, G3], F32R)
        eselT_hl = sb("eselT_hl", [P, 2, NC, NE], F32R)
        keys_hl = sb("keys_hl", [P, 2, NC, NE * EH], F32R)
        values_hl = sb("values_hl", [P, 2, NH, D], F32R)
        bq_col = sb("bq_col", [P, 2 * NC])
        bv_row = sb("bv_row", [P, D])
        bp_row = sb("bp_row", [P, D])
        bih_col = sb("bih_col", [P, 6])
        bhh_col = sb("bhh_col", [P, 6])
        brz_col = sb("brz_col", [P, 4])
        slot_col = sb("slot_col", [P, NC])
        input_col = sb("input_col", [P, NC])
        route_col = sb("route_col", [P, 1])
        member = sb("member", [P, 2])
        x1T = sb("x1T", [P, NC, B * T])

        s0 = ExitStack()
        st_qkv = sb("st_qkv", [P, NC, G3], where=s0)
        st_proj = sb("st_proj", [P, NC, D], where=s0)
        st_wq = sb("st_wq", [P, NC, D], where=s0)
        st_wk = sb("st_wk", [P, NC, D], where=s0)
        st_wv = sb("st_wv", [P, NC, D], where=s0)
        st_ih = sb("st_ih", [P, 6, D], where=s0)
        st_hh = sb("st_hh", [P, 6, D], where=s0)
        st_ihT = sb("st_ihT", [P, NC, G3], where=s0)
        st_keys = sb("st_keys", [P, NC, NE * EH], where=s0)
        st_values = sb("st_values", [P, NH, D], where=s0)
        st_esel = sb("st_esel", [NE, D], where=s0)
        s0.close()

        s1 = ExitStack()
        x_in = sb("x_in", [P, 2, NT, D], where=s1)
        xr = sb("xr", [P, 2, NT, D], where=s1)
        xT_hl = sb("xT_hl", [P, 2, NC, T], F32R, where=s1)
        q_hl = sb("q_hl", [P, 2, NC, T], F32R, where=s1)
        q_sep = sb("q_sep", [P, 2, 2, NC, 2, T], F32R, where=s1)
        k_hl = sb("k_hl", [P, 2, 2, NC, T], F32R, where=s1)
        v_sb = sb("v_sb", [P, 2, NT, D], where=s1)
        k_op = sb("k_op", [3 * 32, H // 2, T], F32R, where=s1)
        q_op = sb("q_op", [3 * 32, H // 2, 2, T], F32R, where=s1)
        v_pad = sb("v_pad", [P, NT, H, P], where=s1)
        prob = sb("prob", [P, 2, 2, SQ], where=s1)
        probT = sb("probT", [P, 4, SQ], where=s1)
        neg_max = sb("neg_max", [P, H // 2, NT, 2], where=s1)
        row_sum = sb("row_sum", [P, 2, NT, H], where=s1)
        inv_sum = sb("inv_sum", [P, NT, H], where=s1)
        inv_wide = sb("inv_wide", [P, NT, D], where=s1)
        inv_bc = sb("inv_bc", [P, NC, T], where=s1)
        yn = sb("yn", [P, NC, T], where=s1)
        y_hl = sb("y_hl", [P, 2, NC, T], F32R, where=s1)
        u1 = sb("u1", [P, NT, D], where=s1)
        stats1 = sb("stats1", [P, NT, 6], where=s1)
        mv1 = sb("mv1", [P, NT, 2], where=s1)
        std1 = sb("std1", [P, 2, NT], where=s1)
        s1.close()

        x2 = sb("x2", [P, B * NT, D])
        s2 = ExitStack()
        c_in = sb("c_in", [P, 2, NT, D], where=s2)
        junk = sb("junk", [P, 2, NT, D], where=s2)
        c_ss = sb("c_ss", [P, 2, NT], where=s2)
        c_ms = sb("c_ms", [P, 2, NT], where=s2)
        c_rs = sb("c_rs", [P, 2, NT], where=s2)
        c_now = sb("c_now", [P, 2, NT], where=s2)
        cT_hl = sb("cT_hl", [P, 2, NC, T], F32R, where=s2)
        kT_hl = sb("kT_hl", [P, 2, 2, NC, T], F32R, where=s2)
        vg_hl = sb("vg_hl", [P, 2, 2, 6, D], F32R, where=s2)
        slots = sb("slots", [P, 2, NC, T], where=s2)
        slots_hl = sb("slots_hl", [P, 2, 2, NC, T], F32R, where=s2)
        sq = sb("sq", [P, NC, T], where=s2)
        s_ms = sb("s_ms", [P, 2, NT], where=s2)
        s_rs = sb("s_rs", [P, 2, NT], where=s2)
        rs_bc = sb("rs_bc", [P, 2, T], where=s2)
        attn = sb("attn", [P, 2, NT, T], where=s2)
        attn_hl = sb("attn_hl", [P, 2, 2, NT, T], F32R, where=s2)
        s_max = sb("s_max", [P, 2, NT], where=s2)
        s_sum = sb("s_sum", [P, 2, NT], where=s2)
        s_inv = sb("s_inv", [P, 2, NT], where=s2)
        tot = sb("tot", [P, T], where=s2)
        inv_tot = sb("inv_tot", [P, T], where=s2)
        gate_r = sb("gate_r", [P, NC, T], where=s2)
        gate_z = sb("gate_z", [P, NC, T], where=s2)
        cand = sb("cand", [P, NC, T], where=s2)
        diff = sb("diff", [P, NC, T], where=s2)
        stats2 = sb("stats2", [P, NT, 6], where=s2)
        mv2 = sb("mv2", [P, NT, 2], where=s2)
        std2 = sb("std2", [P, 2, NT], where=s2)
        s2.close()

        s3 = ExitStack()
        x2f = sb("x2f", [P, 2, NT, D], where=s3)
        x2T_hl = sb("x2T_hl", [P, 2, 2, NC, T], F32R, where=s3)
        logT = sb("logT", [NE, 2, T], where=s3)
        prb = sb("prb", [P, NT, 24], where=s3)
        prbx = sb("prbx", [P, NT, 24], where=s3)
        top8 = sb("top8", [P, NT, 8], where=s3)
        gate = sb("gate", [P, NT, NE], where=s3)
        gsum = sb("gsum", [P, NT], where=s3)
        ginv = sb("ginv", [P, NT], where=s3)
        gateT_hl = sb("gateT_hl", [P, 2, T], F32R, where=s3)
        spread = sb("spread", [P, NH, P], F32R, where=s3)
        spread32 = sb("spread32", [P, NH, P], where=s3)
        hid = sb("hid", [P, 4, 2, T], where=s3)
        hid_hl = sb("hid_hl", [P, 2, 2, NH, T], F32R, where=s3)
        u3 = sb("u3", [P, NT, D], where=s3)
        y_out = sb("y_out", [P, 2, NT, D], where=s3)
        stats3 = sb("stats3", [P, NT, 6], where=s3)
        mv3 = sb("mv3", [P, NT, 2], where=s3)
        std3 = sb("std3", [P, 2, NT], where=s3)

        bank = [stack.enter_context(nc.psum_tensor(f"bank{n}", [P, 512], F32)) for n in range(8)]

        def halves(b):
            return bank[b][:, :].rearrange("p (a n) -> p a n", a=2)

        w_in = [sem(f"w_in{n}") for n in range(6)]
        consts = sem("consts")
        prep_mm = sem("prep_mm")
        prep_out = sem("prep_out")
        prep_act = sem("prep_act")
        prep_pool = sem("prep_pool")
        prep_dve = sem("prep_dve")
        done = [sem(f"phase_done{n}") for n in range(3)]

        x_arr = [event(f"x_arr{j}", 1, 16) for j in range(2)]
        xr_ok = event("xr_ok", 2)
        xT_mm, xT_hi, xT_lo = event("xT_mm", 2), event("xT_hi", 2), event("xT_lo", 2)
        q_mm, q_hi, q_lo = event("q_mm", 2), event("q_hi", 2), event("q_lo", 2)
        k_mm, k_hi, k_lo = event("k_mm", 2), event("k_hi", 2), event("k_lo", 2)
        v_mm, v_ok = event("v_mm", 2), event("v_ok", 2)
        vp_ok = event("vp_ok", 2)
        q_set = event("q_set", 2)
        ops_in = [event(f"ops_in{strip}", 2, 16 * 6) for strip in range(4)]
        s_mm, max_ok, exp_ok = event("s_mm", 32), event("max_ok", 32), event("exp_ok", 32)
        pT_mm = event("pT_mm", 32)
        pT_even, pT_odd = event("pT_even", 16), event("pT_odd", 16)
        pv_mm = event("pv_mm", 32)
        inv_ok, ib_mm, ib_ok = event("inv_ok", 2), event("ib_mm", 2), event("ib_ok", 2)
        yn_ok, y_hi, y_lo = event("yn_ok", 2), event("y_hi", 2), event("y_lo", 2)
        pr_mm, u1_ok = event("pr_mm", 2), event("u1_ok", 2)
        var1, rstd1, x1_ok = event("var1", 2), event("rstd1", 2), event("x1_ok", 2)
        x1T_mm, x1T_ok = event("x1T_mm", 2), event("x1T_ok", 2)
        c_arr = [event(f"c_arr{j}", 1, 16) for j in range(2)]
        c_sq, c_mean, c_rstd, c_kept = event("c_sq", 2), event("c_mean", 2), event("c_rstd", 2), event("c_kept", 1)
        cT_mm, cT_hi, cT_lo = event("cT_mm", 2), event("cT_hi", 2), event("cT_lo", 2)
        kT_mm, kT_hi, kT_lo = event("kT_mm", 2), event("kT_hi", 2), event("kT_lo", 2)
        vg_mm, vg_hi, vg_lo = event("vg_mm", 6), event("vg_hi", 6), event("vg_lo", 6)
        sl_ok, sl_hi, sl_lo = event("sl_ok", 8), event("sl_hi", 6), event("sl_lo", 6)
        sq_ok, sqs_ok = event("sq_ok", UNITS), event("sqs_ok", UNITS)
        ss_mm, ms_ok, rs_ok = event("ss_mm", UNITS), event("ms_ok", UNITS), event("rs_ok", UNITS)
        rb_mm, rb_ok = event("rb_mm", UNITS), event("rb_ok", UNITS)
        sc_mm, sc_ok = event("sc_mm", UNITS), event("sc_ok", UNITS)
        smax_ok, e_ok, z_ok = event("smax_ok", UNITS), event("e_ok", UNITS), event("z_ok", UNITS)
        tt_mm, tt_ok, it_ok = event("tt_mm", UNITS), event("tt_ok", UNITS), event("it_ok", UNITS)
        at_ok, at_hi, at_lo = event("at_ok", UNITS), event("at_hi", UNITS), event("at_lo", UNITS)
        r_mm, z_mm, hn_mm, xn_mm = (event(n, UNITS) for n in ("r_mm", "z_mm", "hn_mm", "xn_mm"))
        r_ok, zt_ok, g_ok, np_ok, n_ok = (event(n, UNITS) for n in ("r_ok", "zt_ok", "g_ok", "np_ok", "n_ok"))
        uu_ok, uT_mm = event("uu_ok", 2), event("uT_mm", 2)
        var2, rstd2, x2_ok = event("var2", 2), event("rstd2", 2), event("x2_ok", 2)
        xf_ok = event("xf_ok", 2)
        tT_mm, tT_hi, tT_lo = event("tT_mm", 2), event("tT_hi", 2), event("tT_lo", 2)
        lg_mm, lg_ok, lT_mm, lx_ok = event("lg_mm", 2), event("lg_ok", 2), event("lT_mm", 2), event("lx_ok", 2)
        gt_ok, gT_mm, gT_hi, gT_lo = event("gt_ok", 2), event("gT_mm", 2), event("gT_hi", 2), event("gT_lo", 2)
        h_mm, h_relu, gb_mm = event("h_mm", 8), event("h_relu", 8), event("gb_mm", 8)
        h_ok, h_hi, h_lo = event("h_ok", 8), event("h_hi", 8), event("h_lo", 8)
        o_mm, u3_ok = event("o_mm", 2), event("u3_ok", 2)
        var3, rstd3, y_ok = event("var3", 2), event("rstd3", 2), event("y_ok", 2)
        stored = [event(f"stored{j}", 1, 16) for j in range(2)]

        attn_chain, cross_chain, expert_chain = sem("attn_chain"), sem("cross_chain"), sem("expert_chain")
        links = [0]

        def next_link():
            links[0] += 1
            return links[0]


        BESIDE = {1: [("xT", 1)], 3: [("q", 1)], 4: [("k", 1)], 5: [("v", 1)], 9: [("ib", 0)], 10: [("pr", 0)],
                  13: [("x1T", 0), ("xT", 2)], 14: [("q", 2)], 15: [("k", 2)],
                  17: [("ib", 1), ("v", 2), ("pr", 1), ("x1T", 1)]}
        ATTN_ORDER = []
        for step in range(H + 2):
            ATTN_ORDER += [("s", step)] if step < H else []
            ATTN_ORDER += [("pT", step - 1)] if 1 <= step <= H else []
            ATTN_ORDER += [("pv", step - 2)] if step >= 2 else []
            ATTN_ORDER += BESIDE.get(step, [])
        jobs1 = []
        for name, n in ATTN_ORDER:
            if name == "s":
                jobs1 += [((name, 2 * n + qt), 4 + qt, exp_ok, 32, 2 * n + qt + 1) for qt in range(NT)]
            elif name == "pT":
                jobs1 += [((name, 2 * n), 6, pT_even, 16, n + 1), ((name, 2 * n + 1), 7, pT_odd, 16, n + 1)]
            elif name == "pv":
                jobs1 += [(("y", n // 8), 3, yn_ok, 2, n // 8 + 1)] if n % 8 == 0 else []
            else:
                b, signal = {"xT": (0, xT_lo), "q": (1, q_lo), "k": (2, k_lo), "v": (0, v_ok),
                             "ib": (1, ib_ok), "pr": (2, u1_ok), "x1T": (1, x1T_ok)}[name]
                jobs1.append(((name, n), b, signal, 2, n + 1))

        def context(j):
            cT, kT, *vg = ((0, 1, 3, 2, 0), (1, 3, 2, 4, 5))[j]
            jobs = [(("cT", j), cT, cT_lo, 2, 2 + j + 1), (("kT", j), kT, kT_lo, 2, 2 + j + 1)]
            return jobs + [(("vg", 3 * j + g), vg[g], vg_lo, 6, 6 + 3 * j + g + 1) for g in range(3)]

        def front(u):
            return [(("ss", u), 0, ms_ok, UNITS, u + 1), (("sc", u), 3, sc_ok, UNITS, u + 1), (("rb", u), 1, rb_ok, UNITS, u + 1)]

        def mid(u):
            return [(("r", u), 4, r_ok, UNITS, u + 1), (("z", u), 5, zt_ok, UNITS, u + 1), (("hn", u), 6, g_ok, UNITS, u + 1),
                    (("tt", u), 2, tt_ok, UNITS, u + 1)]

        def back(u):
            return [(("xn", u), 7, np_ok, UNITS, u + 1)]

        jobs2 = mid(0)
        for u in range(UNITS):
            jobs2 += (front(u + 1) if u + 1 < UNITS else []) + back(u)
            jobs2 += context(0)[:1] if u == 4 else []
            jobs2 += mid(u + 1) if u + 1 < UNITS else []
            jobs2 += context(0)[1:] + context(1)[:1] if u == 4 else []
        jobs2 += context(1)[1:2] + [(("uT", 0), 0, x2_ok, 2, 1)] + context(1)[2:]
        jobs2 += [(("uT", 1), 6, x2_ok, 2, 2)] + front(UNITS)
        BANK2 = {job[0]: job[1] for job in jobs2}
        EXPERT_ORDER = [("lg", 0), ("h", 0), ("h", 1), ("lT", 0), ("lg", 1), ("h", 2), ("gT", 0), ("h", 3),
                        ("gb", 0), ("lT", 1), ("gb", 1), ("h", 4), ("gb", 2), ("gT", 1), ("gb", 3),
                        ("h", 5), ("gb", 4), ("h", 6), ("gb", 5), ("h", 7), ("gb", 6), ("gb", 7)]
        EXPERT_ORDER += [("tT", 0), ("tT", 1), ("o", 0), ("o", 1)]
        jobs3 = []
        for name, n in EXPERT_ORDER:
            b, signal, per = {"tT": (n, tT_lo, 2), "lg": (2, lg_ok, 2), "lT": (0, lx_ok, 2), "gT": (1 - n, gT_lo, 2),
                              "h": (4 + n % 2, h_relu, 8), "gb": (6 + n % 2, h_ok, 8), "o": (2 + n, u3_ok, 2)}[name]
            jobs3.append(((name, n), b, signal, per, n + 1 + (per if name == "tT" else 0)))

        def bank_free(jobs, i, key, final=False):
            at = [job[0] for job in jobs].index(key)
            b = jobs[at][1]
            before = [job for job in jobs[:at] if job[1] == b and not (final and job[4] > job[3])]
            last = [job for job in jobs if job[1] == b][-1]
            _, _, signal, per, k = before[-1] if before else last
            return b, signal, due(per, i, k, back=0 if before else 1)

        def split3(pe, dst, left, right, first, last):
            for n, (a, b) in enumerate(PASSES):
                mm = pe.matmul(dst, left(a), right(b), start=first and n == 0, stop=last and n == 2,
                               skip_group_check=True)
            return mm

        def transpose4(pe, b, src):
            for c in range(2):
                for t in range(2):
                    mm = pe.transpose(halves(b)[:, c, t * P:(t + 1) * P], src(t, c), ident[:, :])
            return mm

        VG_ROWS = (((0, 2, 0),), ((0, 1, 0), (1, 1, 1)), ((0, 2, 1),))

        def f32(ap):
            return ap.bitcast(F32)

        block = stack.enter_context(nc.Block())

        @block.sync
        def _(sp):
            for signal, count in events:
                sp.sem_inc(signal, count)
            def rows(w, n):
                return w.rearrange("(c p) n -> p c n", p=P)
            with nc.allow_non_contiguous_dma("biases by column"):
                sp.dma_start(st_qkv[:, :, :], rows(w_qkv, NC)).then_inc(w_in[0], 16)
                sp.dma_start(st_hh[:, :, :], rows(whh, 6)).then_inc(w_in[1], 16)
                sp.dma_start(st_ih[:, :, :], rows(wih, 6)).then_inc(w_in[4], 16)
                sp.dma_start(bq_col[:, :], b_qkv[0:2 * D].rearrange("(c p) -> p c", p=P)).then_inc(w_in[0], 16)
                sp.dma_start(bv_row[:, :], b_qkv[2 * D:3 * D].partition_broadcast(P)).then_inc(w_in[0], 16)
                sp.dma_start(bp_row[:, :], b_proj.partition_broadcast(P)).then_inc(w_in[0], 16)
                sp.dma_start(st_esel[:, :], expert_sel).then_inc(w_in[5], 16)
                sp.dma_start(st_wk[:, :, :], rows(wk, NC)).then_inc(w_in[5], 16)
                sp.dma_start(st_wq[:, :, :], rows(wq, NC)).then_inc(w_in[5], 16)
                sp.dma_start(st_wv[:, :, :], rows(wv, NC)).then_inc(w_in[5], 16)
                sp.dma_start(bih_col[:, :], bih.rearrange("(c p) -> p c", p=P)).then_inc(w_in[2], 16)
                sp.dma_start(bhh_col[:, :], bhh.rearrange("(c p) -> p c", p=P)).then_inc(w_in[2], 16)
                sp.dma_start(slot_col[:, :], slot_w.rearrange("(c p) -> p c", p=P)).then_inc(w_in[2], 16)
                sp.dma_start(input_col[:, :], input_w.rearrange("(c p) -> p c", p=P)).then_inc(w_in[2], 16)
                sp.dma_start(route_col[:, :], route_scale.partition_broadcast(P)).then_inc(w_in[2], 16)
                sp.dma_start(st_proj[:, :, :], rows(w_proj, NC)).then_inc(w_in[3], 16)
                for c in range(NC):
                    sp.dma_start(st_keys[:, c, :].rearrange("p (e h) -> p e h", e=NE),
                                 keys[:, c * P:(c + 1) * P, :].rearrange("e p h -> p e h")).then_inc(w_in[3], 16)
                sp.dma_start(st_values[:, :, :],
                             values.rearrange("e h v -> (e h) v").rearrange("(c p) v -> p c v", p=P)
                             ).then_inc(w_in[3], 16)
            sp.wait_ge(prep_act, 2)
            sp.wait_ge(prep_dve, 2)

            def attention(i, first=False, last=False):
                def load(j):
                    sp.wait_ge(xT_mm, due(2, i, j + 1))
                    sp.sem_inc(passed, 1)
                    sp.wait_ge(xr_ok, due(2, i, j + 1))
                    sp.sem_inc(passed, 1)
                    sp.dma_start(x_in[:, j, :, :], x[(i + 1) * 2 + j, :, :].rearrange("(t p) d -> p t d", p=P)).then_inc(x_arr[j], 16)

                def operands(n):
                    j = n % 2
                    sp.wait_ge(k_lo, due(2, i, n + 1))
                    sp.sem_inc(passed, 1)
                    sp.wait_ge(q_set, due(2, i, n + 1))
                    sp.sem_inc(passed, 1)
                    for strip in range(4):
                        sp.wait_ge(s_mm, due(32, i, 16 * (n - 1) + 4 * (strip + 1)))
                        sp.sem_inc(passed, 1)
                        rows_in = slice(32 * strip, 32 * strip + 32)
                        for quad, part in enumerate((HI, LO, HI)):
                            sp.dma_start(f32(k_op[32 * quad:32 * quad + 32, :, :]).rearrange("p (c s) t -> p c s t", s=4)[:, :, strip, :],
                                         f32(k_hl[rows_in, j, part, :, :])).then_inc(ops_in[strip], 16)
                        for quad, part in enumerate((HI, HI, LO)):
                            sp.dma_start(f32(q_op[32 * quad:32 * quad + 32, :, :, :]).rearrange("p (c s) e t -> p c s (e t)", s=4)[:, :, strip, :],
                                         f32(q_sep[rows_in, j, part, :, :, :]).rearrange("p c e t -> p c (e t)")
                                         ).then_inc(ops_in[strip], 16)
                if not last:
                    load(0)
                if not first:
                    operands(1)
                if not last:
                    load(1)
                    operands(2)
            attention(-1, first=True)
            with sp.Fori(0, PAIRS - 1) as i:
                attention(i)
            attention(PAIRS - 1, last=True)
            sp.wait_ge(done[1], 4)
            with sp.Fori(0, PAIRS) as i:
                for j in range(2):
                    sp.wait_ge(cT_mm, due(2, i, j + 1, back=1))
                    sp.sem_inc(passed, 1)
                    sp.wait_ge(c_sq, due(2, i, j + 1, back=1))
                    sp.sem_inc(passed, 1)
                    sp.dma_start(c_in[:, j, :, :], ctx_in[i * 2 + j, :, :].rearrange("(t p) d -> p t d", p=P)).then_inc(c_arr[j], 16)
            sp.wait_ge(done[2], 4)
            with sp.Fori(0, PAIRS) as i:
                for j in range(2):
                    sp.wait_ge(y_ok, due(2, i, j + 1))
                    sp.sem_inc(passed, 1)
                    sp.dma_start(out[i * 2 + j, :, :].rearrange("(t p) d -> p t d", p=P), y_out[:, j, :, :]).then_inc(stored[j], 16)
            for j in range(2):
                sp.wait_ge(stored[j], 16 * (PAIRS + 1))

        @block.gpsimd
        def _(pool):
            pool.memset(ident[:, :], 0.0).then_inc(consts, 1)
            pool.memset(mask32[:, :], 0.0).then_inc(consts, 1)
            pool.wait_ge(consts, 2)
            pool.affine_select(out=ident[:, :], in_=ident[:, :], compare_op=ALU.not_equal, fill=1.0,
                               base=0, pattern=[[-1, P]], channel_multiplier=1).then_inc(consts, 1)
            pool.affine_select(out=mask32[:, :], in_=mask32[:, :], compare_op=ALU.is_ge, fill=MASKED,
                               base=0, pattern=[[-1, P]], channel_multiplier=1).then_inc(consts, 1)
            pool.wait_ge(consts, 4)
            pool.tensor_copy(ident16[:, :], ident[:, :]).then_inc(consts, 1)
            for e in range(2):
                pool.tensor_copy(mask16[:, e, :], mask32[:, :]).then_inc(consts, 1)
            pool.memset(mean_col[:, :], 1.0 / D).then_inc(consts, 1)
            pool.memset(half_neg[:, :], -0.5).then_inc(consts, 1)
            pool.wait_ge(consts, 9)
            for n, (part, staged) in enumerate(((wproj_hl, st_proj), (keys_hl, st_keys))):
                pool.wait_ge(prep_act, 16 + n)
                pool.tensor_tensor(part[:, LO, :, :], staged[:, :, :], f32(part[:, HI, :, :]), ALU.subtract).then_inc(prep_pool, 1)
            pool.wait_ge(prep_pool, 2)
            pool.drain().then_inc(done[0], 1)
            pool.wait_ge(done[0], 4)
            pool.memset(v_pad[:, :, :, :], 0.0).then_inc(consts, 1)
            pool.wait_ge(consts, 10)

            def rstd(i, var, ev, std, k, slot):
                pool.wait_ge(var, due(2, i, k))
                pool.tensor_tensor(std[:, 1, :], std[:, 0, :], half_neg[:, :], ALU.pow).then_inc(ev, 1)

            def attention(i, first=False, last=False):
                def residual(j):
                    pool.wait_ge(x_arr[j], due(1, i, 2, step=16))
                    pool.wait_ge(u1_ok, due(2, i, j + 1))
                    for t in range(NT):
                        r = pool.tensor_tensor(xr[:, j, t, :], x_in[:, j, t, :], bp_row[:, :], ALU.add)
                    r.then_inc(xr_ok, 1)

                def values(n):
                    pool.wait_ge(v_ok, due(2, i, n + 1))
                    pool.wait_ge(pv_mm, due(32, i, 16 * n))
                    pool.sem_inc(passed, 1)
                    for t in range(NT):
                        for c in range(NC):
                            dst = v_pad[:, t, 8 * c:8 * c + 8, :].rearrange("p h n -> p (h n)")
                            diag = bass.AP(tensor=dst.tensor, offset=dst.offset,
                                           ap=[list(dst.ap[0]), [P + DH, 8], [1, DH]])
                            r = pool.tensor_tensor(diag, v_sb[:, n % 2, t, c * P:(c + 1) * P].rearrange("p (h d) -> p h d", d=DH),
                                                   bv_row[:, c * P:(c + 1) * P].rearrange("p (h d) -> p h d", d=DH), ALU.add)
                    r.then_inc(vp_ok, 1)

                def heads_lo(j):
                    pool.wait_ge(y_hi, due(2, i, j + 1))
                    pool.tensor_tensor(y_hl[:, LO, :, :], yn[:, :, :], f32(y_hl[:, HI, :, :]), ALU.subtract).then_inc(y_lo, 1)
                if not first:
                    values(1)
                    heads_lo(0)
                    rstd(i, var1, rstd1, std1, 1, 0)
                if not last:
                    residual(0)
                if not first:
                    heads_lo(1)
                    rstd(i, var1, rstd1, std1, 2, 1)
                if not last:
                    values(2)
                    residual(1)
            attention(-1, first=True)
            with pool.Fori(0, PAIRS - 1) as i:
                attention(i)
            attention(PAIRS - 1, last=True)
            pool.drain().then_inc(done[1], 1)
            pool.wait_ge(done[1], 4)
            def cross(i, first=False, last=False):
                def context_scale():
                    for j in range(2):
                        pool.wait_ge(c_mean, due(2, i, 2 + j + 1))
                        pool.tensor_tensor(c_rs[:, j, :], c_ms[:, j, :], half_neg[:, :], ALU.pow).then_inc(c_rstd, 1)

                def next_slots_lo(j):
                    pool.wait_ge(sl_hi, due(6, i, 6 + j + 1))
                    pool.wait_ge(sl_ok, due(8, i, 8 + j + 1))
                    pool.tensor_tensor(slots_hl[:, j, LO, :, :], slots[:, j, :, :],
                                       f32(slots_hl[:, j, HI, :, :]), ALU.subtract).then_inc(sl_lo, 1)

                def norm(u):
                    j = u % 2
                    pool.wait_ge(ms_ok, due(UNITS, i, u + 1))
                    pool.tensor_tensor(s_rs[:, j, :], s_ms[:, j, :], half_neg[:, :], ALU.pow).then_inc(rs_ok, 1)

                def attn_lo(u):
                    j = u % 2
                    pool.wait_ge(at_hi, due(UNITS, i, u + 1))
                    pool.tensor_tensor(attn_hl[:, j, LO, :, :], attn[:, j, :, :],
                                                    f32(attn_hl[:, j, HI, :, :]), ALU.subtract).then_inc(at_lo, 1)
                if first:
                    context_scale()
                for u in range(0 if first else UNITS):
                    if u + 1 < UNITS:
                        norm(u + 1)
                    attn_lo(u)
                    if u < UNITS - 2:
                        j = u % 2
                        pool.wait_ge(sl_hi, due(6, i, 2 + u + 1))
                        pool.tensor_tensor(slots_hl[:, j, LO, :, :], slots[:, j, :, :],
                                                        f32(slots_hl[:, j, HI, :, :]), ALU.subtract).then_inc(sl_lo, 1)
                    if u == 3 and not last:
                        context_scale()
                if not last:
                    next_slots_lo(0)
                if not first:
                    rstd(i, var2, rstd2, std2, 1, 0)
                if not last:
                    next_slots_lo(1)
                    norm(UNITS)
                if not first:
                    rstd(i, var2, rstd2, std2, 2, 1)
            cross(-1, first=True)
            with pool.Fori(0, PAIRS - 1) as i:
                cross(i)
            cross(PAIRS - 1, last=True)
            pool.drain().then_inc(done[2], 1)
            pool.wait_ge(done[2], 4)
            pool.memset(spread32[:, :, :], 0.0).then_inc(consts, 1)
            pool.memset(f32(gateT_hl[:, :, :]), 0.0).then_inc(consts, 1)
            pool.memset(prb[:, :, NE:], -1.0).then_inc(consts, 1)
            pool.wait_ge(consts, 13)
            for n, off in enumerate((0, 32)):
                rows = spread32[off:off + 32, :, :].rearrange("p c (e m) -> p (c e) m", e=2)
                pool.affine_select(out=rows, in_=rows, compare_op=ALU.not_equal, fill=1.0, base=0,
                                   pattern=[[-1, NE], [0, EH]], channel_multiplier=1).then_inc(consts, 1)
            pool.wait_ge(consts, 15)
            pool.tensor_copy(spread[:, :, :], spread32[:, :, :]).then_inc(consts, 1)
            with pool.Fori(0, PAIRS) as i:
                for j in range(2):
                    for g in range(4):
                        n = 4 * j + g
                        pool.wait_ge(h_hi, due(8, i, n + 1))
                        pool.tensor_tensor(hid_hl[:, j, LO, 2 * g:2 * g + 2, :], hid[:, g, :, :],
                                                       f32(hid_hl[:, j, HI, 2 * g:2 * g + 2, :]), ALU.subtract).then_inc(h_lo, 1)
                for j in range(2):
                    rstd(i, var3, rstd3, std3, j + 1, j)

        @block.scalar
        def _(act):
            def copy(dst, src, **kw):
                return act.activation(dst, src, ACT.Copy, **kw)
            act.wait_ge(w_in[0], 64)
            copy(wqkv_hl[:, HI, :, 0:D], st_qkv[:, :, 0:D], scale=float(DH) ** -0.5).then_inc(prep_act, 1)
            copy(wqkv_hl[:, HI, :, D:], st_qkv[:, :, D:]).then_inc(prep_act, 1)
            for c in range(NC):
                for half, blocks in enumerate((slice(0, 4 * P), slice(4 * P, G3))):
                    act.wait_ge(prep_mm, 2 * c + half + 1)
                    copy(whhT_hl[:, HI, c, blocks], bank[2 * c + half][:, 0:blocks.stop - blocks.start]).then_inc(prep_act, 1)
            for c in range(NC):
                for half, blocks in enumerate((slice(0, 4 * P), slice(4 * P, G3))):
                    act.wait_ge(prep_mm, 4 + 2 * c + half + 1)
                    copy(st_ihT[:, c, blocks], bank[4 + 2 * c + half][:, 0:blocks.stop - blocks.start]).then_inc(prep_act, 1)
            act.wait_ge(prep_mm, 9)
            copy(eselT_hl[:, HI, :, :], bank[0][:, 0:NC * NE].rearrange("p (c e) -> p c e", c=NC)).then_inc(prep_act, 1)
            act.wait_ge(w_in[2], 80)
            for c in range(NC):
                act.wait_ge(prep_mm, 10 + c)
                act.activation(qk_w_hl[:, HI, c, :], bank[1 + c][:, 0:D], ACT.Identity, scale=input_col[:, c:c + 1]).then_inc(prep_act, 1)
            for c in range(NC):
                if c == 1:
                    act.wait_ge(w_in[3], 64)
                    copy(wproj_hl[:, HI, :, :], st_proj[:, :, :]).then_inc(prep_act, 1)
                    copy(keys_hl[:, HI, :, :], st_keys[:, :, :]).then_inc(prep_act, 1)
                    copy(values_hl[:, HI, :, :], st_values[:, :, :]).then_inc(prep_act, 1)
                for half, blocks in enumerate((slice(0, 4 * P), slice(4 * P, G3))):
                    act.wait_ge(prep_mm, 12 + 2 * c + half)
                    act.activation(v_w_hl[:, HI, c, blocks], bank[3 + 2 * c + half][:, 0:blocks.stop - blocks.start],
                                   ACT.Identity, scale=input_col[:, c:c + 1]).then_inc(prep_act, 1)
            act.drain().then_inc(done[0], 1)
            act.wait_ge(done[0], 4)

            def attention(i, last=False):
                def text_hi(n):
                    act.wait_ge(xT_mm, due(2, i, n + 1))
                    act.wait_ge(v_mm, due(2, i, n))
                    copy(xT_hl[:, HI, :, :], halves(0)).then_inc(xT_hi, 1)

                def queries_hi(n):
                    act.wait_ge(q_mm, due(2, i, n + 1))
                    act.wait_ge(q_set, due(2, i, n))
                    for c in range(NC):
                        r = act.activation(q_hl[:, HI, c, :], halves(1)[:, c, :], ACT.Identity, bias=bq_col[:, c:c + 1])
                    r.then_inc(q_hi, 1)

                def keys_hi(n):
                    act.wait_ge(k_mm, due(2, i, n + 1))
                    for strip in range(4):
                        act.wait_ge(ops_in[strip], due(2, i, n - 1, step=16 * 6))
                    for c in range(NC):
                        r = act.activation(k_hl[:, n % 2, HI, c, :], halves(2)[:, c, :], ACT.Identity, bias=bq_col[:, NC + c:NC + c + 1])
                    r.then_inc(k_hi, 1)

                def scale_heads(j):
                    act.wait_ge(ib_mm, due(2, i, j + 1))
                    copy(inv_bc[:, :, :], halves(1)).then_inc(ib_ok, 1)

                def heads_hi(j):
                    act.wait_ge(yn_ok, due(2, i, j + 1))
                    copy(y_hl[:, HI, :, :], yn[:, :, :]).then_inc(y_hi, 1)

                def text_out(j):
                    act.wait_ge(x1T_mm, due(2, i, j + 1))
                    copy(x1T[:, :, bass.ds(i * (2 * T) + j * T, T)], halves(1)).then_inc(x1T_ok, 1)

                def exps(step):
                    j, hp = step // 8, step % 8
                    for qt in range(NT):
                        lo, size = (0, P) if qt == 0 else (P, 2 * P)
                        act.wait_ge(max_ok, due(32, i, 2 * step + qt + 1))
                        act.wait_ge(pT_mm, due(32, i, 2 * step - 2))
                        for e in range(2):
                            h = head(2 * hp + e)
                            r = act.activation(prob[:, hp % 2, e, lo:lo + size], halves(4 + qt)[:, e, 0:size],
                                               ACT.Exp, bias=neg_max[:, hp, qt, e:e + 1], accum_out=row_sum[:, j, qt, h:h + 1])
                        r.then_inc(exp_ok, 1)

                def probs_out(step):
                    n = 2 * step + 1
                    act.wait_ge(pT_mm, due(32, i, n + 1))
                    act.wait_ge(pv_mm, due(32, i, n - 3))
                    copy(probT[:, n % 4, :], bank[7][:, 0:SQ]).then_inc(pT_odd, 1)

                def steps(first, end):
                    for step in range(first, end):
                        if step == 10:
                            heads_hi(0)
                        if step < H:
                            exps(step)
                        if step >= 1:
                            probs_out(step - 1)
                        if step == 1:
                            text_hi(1)
                        elif step == 3:
                            queries_hi(1)
                        elif step == 4:
                            keys_hi(1)
                        elif step == 9:
                            scale_heads(0)
                        elif step == 13:
                            text_out(0)
                if i is not FIRST:
                    steps(0, 14)
                if not last:
                    text_hi(2)
                if i is not FIRST:
                    steps(14, 15)
                if not last:
                    queries_hi(2)
                if i is not FIRST:
                    steps(15, 16)
                if not last:
                    keys_hi(2)
                if i is not FIRST:
                    steps(16, 17)
                    scale_heads(1)
                    heads_hi(1)
                    text_out(1)
            attention(FIRST)
            with act.Fori(0, PAIRS - 1) as i:
                attention(i)
            attention(PAIRS - 1, last=True)
            act.drain().then_inc(done[1], 1)
            act.wait_ge(done[1], 4)
            def context_squares(r):
                for j in range(2):
                    act.wait_ge(c_arr[j], due(1, r, 2, step=16))
                    for t in range(NT):
                        ins = act.activation(junk[:, j, t, :], c_in[:, j, t, :], ACT.Square, accum_out=c_ss[:, j, t:t + 1])
                    ins.then_inc(c_sq, 1)

            def text_hi(r, j):
                act.wait_ge(cT_mm, due(2, r, 2 + j + 1))
                act.wait_ge(vg_mm, due(6, r, 6 + 3 * j))
                copy(cT_hl[:, HI, :, :], halves(BANK2["cT", j])).then_inc(cT_hi, 1)

            def context_hi(r, j):
                act.wait_ge(kT_mm, due(2, r, 2 + j + 1))
                for c in range(NC):
                    ins = act.activation(kT_hl[:, j, HI, c, :], halves(BANK2["kT", j])[:, c, :], ACT.Identity, scale=slot_col[:, c:c + 1])
                ins.then_inc(kT_hi, 1)
                act.wait_ge(c_rstd, due(2, r, 2 + j + 1))
                for g in range(3):
                    act.wait_ge(vg_mm, due(6, r, 6 + 3 * j + g + 1))
                    for first, size, t in VG_ROWS[g]:
                        ins = act.activation(vg_hl[:, j, HI, 2 * g + first:2 * g + first + size, :],
                                             halves(BANK2["vg", 3 * j + g])[:, first:first + size, :],
                                             ACT.Identity, scale=c_rs[:, j, t:t + 1])
                    ins.then_inc(vg_hi, 1)

            def cross(i, first=False, last=False):
                def next_slots_hi(j):
                    act.wait_ge(hn_mm, due(UNITS, i, 5 + j))
                    copy(slots_hl[:, j, HI, :, :], x1T[:, :, bass.ds((i + 1) * (2 * T) + j * T, T)]).then_inc(sl_hi, 1)

                def start(u):
                    j = u % 2
                    act.wait_ge(sl_ok, due(8, i, u + 1 if u < UNITS else 8 + 1))
                    act.wait_ge(sqs_ok, due(UNITS, i, u))
                    act.activation(sq[:, :, :], slots[:, j, :, :], ACT.Square).then_inc(sq_ok, 1)

                def scale(u):
                    act.wait_ge(rb_mm, due(UNITS, i, u + 1))
                    copy(rs_bc[:, u % 2, :], bank[1][:, 0:T]).then_inc(rb_ok, 1)

                def soft(u):
                    j = u % 2
                    act.wait_ge(smax_ok, due(UNITS, i, u + 1))
                    for t in range(NT):
                        r = act.activation(attn[:, j, t, :], attn[:, j, t, :], ACT.Exp, bias=s_max[:, j, t:t + 1],
                                           accum_out=s_sum[:, j, t:t + 1])
                    r.then_inc(e_ok, 1)

                def attn_hi(u):
                    j = u % 2
                    act.wait_ge(at_ok, due(UNITS, i, u + 1))
                    copy(attn_hl[:, j, HI, :, :], attn[:, j, :, :]).then_inc(at_hi, 1)

                def reset_gate(u):
                    act.wait_ge(r_mm, due(UNITS, i, u + 1))
                    for c in range(NC):
                        r = act.activation(gate_r[:, c, :], halves(4)[:, c, :], ACT.Tanh, scale=0.5, bias=brz_col[:, c:c + 1])
                    r.then_inc(r_ok, 1)

                def gates(u):
                    act.wait_ge(np_ok, due(UNITS, i, u + 1))
                    for c in range(NC):
                        r = act.activation(cand[:, c, :], gate_r[:, c, :], ACT.Tanh, bias=bih_col[:, 2 * NC + c:2 * NC + c + 1])
                    r.then_inc(n_ok, 1)
                    act.wait_ge(z_mm, due(UNITS, i, u + 1))
                    for c in range(NC):
                        r = act.activation(gate_z[:, c, :], halves(5)[:, c, :], ACT.Tanh, scale=0.5, bias=brz_col[:, NC + c:NC + c + 1])
                    r.then_inc(zt_ok, 1)

                def slots_hi(u):
                    j = u % 2
                    if u < UNITS - 2:
                        act.wait_ge(sl_ok, due(8, i, 2 + u + 1))
                        copy(slots_hl[:, j, HI, :, :], slots[:, j, :, :]).then_inc(sl_hi, 1)
                if first:
                    context_squares(i)
                    text_hi(i, 0)
                    context_hi(i, 0)
                    text_hi(i, 1)
                else:
                    scale(0)
                    soft(0)
                    start(1)
                    attn_hi(0)
                    for u in range(UNITS):
                        if u + 1 < UNITS:
                            scale(u + 1)
                        reset_gate(u)
                        if u + 1 < UNITS:
                            soft(u + 1)
                        gates(u)
                        if u + 2 < UNITS:
                            start(u + 2)
                        slots_hi(u)
                        if u == 3 and not last:
                            context_squares(i)
                        if u == 4 and not last:
                            text_hi(i, 0)
                        if u + 1 < UNITS:
                            attn_hi(u + 1)
                        if u == 4 and not last:
                            context_hi(i, 0)
                            text_hi(i, 1)
                if not last:
                    next_slots_hi(0)
                    start(UNITS)
                    context_hi(i, 1)
                    next_slots_hi(1)
            cross(-1, first=True)
            with act.Fori(0, PAIRS - 1) as i:
                cross(i)
            cross(PAIRS - 1, last=True)
            act.drain().then_inc(done[2], 1)
            act.wait_ge(done[2], 4)
            def text(i, j):
                act.wait_ge(tT_mm, due(2, i, j + 1, back=1))
                copy(x2f[:, j, :, :], x2[:, bass.ds(i * (2 * NT) + j * NT, NT), :]).then_inc(xf_ok, 1)

            def text_hi(i, j):
                act.wait_ge(tT_mm, due(2, i, j + 1))
                act.wait_ge(h_mm, due(8, i, 4 * j + 4, back=1))
                copy(x2T_hl[:, j, HI, :, :], halves(j)).then_inc(tT_hi, 1)

            def experts(i, last):
                def exp_logits(j):
                    act.wait_ge(lT_mm, due(2, i, j + 1))
                    if j:
                        act.wait_ge(gt_ok, due(2, i, 1))
                    else:
                        act.wait_ge(gt_ok, due(2, i, 2, back=1))
                    act.activation(prb[:, :, 0:NE], bank[0][:, 0:NT * NE].rearrange("p (t e) -> p t e", t=NT),
                                   ACT.Exp, scale=-1.0).then_inc(lx_ok, 1)

                def gates_hi(j):
                    act.wait_ge(gT_mm, due(2, i, j + 1))
                    act.wait_ge(gb_mm, due(8, i, 4 * j + 4, back=1))
                    copy(gateT_hl[0:NE, j, :], bank[1 - j][0:NE, 0:T]).then_inc(gT_hi, 1)

                def relu(n):
                    act.wait_ge(h_mm, due(8, i, n + 1))
                    if n >= 4:
                        act.wait_ge(h_lo, due(8, i, n - 3))
                    else:
                        act.wait_ge(h_lo, due(8, i, 8 + n - 3, back=1))
                    act.activation(hid[:, n % 4, :, :], halves(4 + n % 2), ACT.Relu).then_inc(h_relu, 1)

                def hidden_hi(n):
                    j, g = n // 4, n % 4
                    act.wait_ge(h_ok, due(8, i, n + 1))
                    act.wait_ge(o_mm, due(2, i, j + 1, back=1))
                    copy(hid_hl[:, j, HI, 2 * g:2 * g + 2, :], hid[:, g, :, :]).then_inc(h_hi, 1)
                relu(0)
                relu(1)
                exp_logits(0)
                relu(2)
                gates_hi(0)
                relu(3)
                exp_logits(1)
                hidden_hi(0)
                hidden_hi(1)
                relu(4)
                hidden_hi(2)
                gates_hi(1)
                for n in range(3, 6):
                    hidden_hi(n)
                    relu(n + 2)
                if not last:
                    text(i + 1, 0)
                    text(i + 1, 1)
                hidden_hi(6)
                hidden_hi(7)
                if not last:
                    text_hi(i + 1, 0)
                    text_hi(i + 1, 1)
            text(0, 0)
            text(0, 1)
            text_hi(0, 0)
            text_hi(0, 1)
            with act.Fori(0, PAIRS - 1) as i:
                experts(i, False)
            experts(PAIRS - 1, True)

        @block.vector
        def _(dve):
            def sub_hi(dst, src, hi):
                return dve.tensor_tensor(dst, src, f32(hi), ALU.subtract)

            prep = [0]

            def step(ins):
                ins.then_inc(prep_dve, 1)
                prep[0] += 1
                dve.wait_ge(prep_dve, prep[0])

            dve.wait_ge(prep_act, 1)
            step(dve.scalar_tensor_tensor(wqkv_hl[:, LO, :, 0:D], st_qkv[:, :, 0:D], float(DH) ** -0.5,
                                          f32(wqkv_hl[:, HI, :, 0:D]), ALU.mult, ALU.subtract))
            dve.wait_ge(prep_act, 2)
            step(sub_hi(wqkv_hl[:, LO, :, D:], st_qkv[:, :, D:], wqkv_hl[:, HI, :, D:]))
            step(dve.tensor_scalar(bq_col[:, 0:NC], bq_col[:, 0:NC], float(DH) ** -0.5, None, ALU.mult))
            for c in range(NC):
                for half, blocks in enumerate((slice(0, 4 * P), slice(4 * P, G3))):
                    dve.wait_ge(prep_act, 3 + 2 * c + half)
                    step(sub_hi(whhT_hl[:, LO, c, blocks], bank[2 * c + half][:, 0:blocks.stop - blocks.start], whhT_hl[:, HI, c, blocks]))
            dve.drain().then_inc(prep_out, 1)
            dve.wait_ge(w_in[2], 80)
            step(dve.tensor_tensor(brz_col[:, :], bih_col[:, 0:4], bhh_col[:, 0:4], ALU.add))
            step(dve.tensor_scalar(brz_col[:, :], brz_col[:, :], 0.5, None, ALU.mult))
            step(dve.tensor_scalar(slot_col[:, :], slot_col[:, :], float(D) ** -0.5, None, ALU.mult))
            dve.wait_ge(consts, 9)
            for e in range(2):
                step(dve.tensor_reduce(member[:, e:e + 1], ident[:, :].rearrange("p (h e d) -> p e h d", e=2, d=DH)[:, e, :, :],
                                       AX.XY, ALU.add))
            dve.wait_ge(prep_act, 11)
            step(sub_hi(eselT_hl[:, LO, :, :], bank[0][:, 0:NC * NE].rearrange("p (c e) -> p c e", c=NC), eselT_hl[:, HI, :, :]))
            for c in range(NC):
                dve.wait_ge(prep_act, 12 + c)
                step(dve.scalar_tensor_tensor(qk_w_hl[:, LO, c, :], bank[1 + c][:, 0:D], input_col[:, c:c + 1],
                                              f32(qk_w_hl[:, HI, c, :]), ALU.mult, ALU.subtract))
            for c in range(NC):
                if c == 1:
                    dve.wait_ge(prep_act, 18)
                    step(sub_hi(values_hl[:, LO, :, :], st_values[:, :, :], values_hl[:, HI, :, :]))
                for half, blocks in enumerate((slice(0, 4 * P), slice(4 * P, G3))):
                    dve.wait_ge(prep_act, (14, 19)[c] + half)
                    step(dve.scalar_tensor_tensor(v_w_hl[:, LO, c, blocks], bank[3 + 2 * c + half][:, 0:blocks.stop - blocks.start],
                                                  input_col[:, c:c + 1], f32(v_w_hl[:, HI, c, blocks]), ALU.mult, ALU.subtract))
            dve.drain().then_inc(done[0], 1)
            dve.wait_ge(done[0], 4)

            def moments(i, chain, per, src, stats, mv, std, var):
                for t in range(NT):
                    ins = dve.bn_stats(stats[:, t, :], src(t))
                ins.then_inc(chain, 1)
                dve.wait_ge(chain, i * per + next_link())
                dve.sem_inc(passed, 1)
                for t in range(NT):
                    ins = dve.bn_aggr(mv[:, t, :], stats[:, t, :])
                ins.then_inc(chain, 1)
                dve.wait_ge(chain, i * per + next_link())
                dve.tensor_scalar(std[:, 0, :], mv[:, :, 1], LN_EPS, None, ALU.add).then_inc(var, 1)

            def layer_norm(i, chain, per, src, stats, mv, std, var, rstd, k, result, ok):
                moments(i, chain, per, src, stats, mv, std, var)
                normal(i, src, mv, std, rstd, k, result, ok)

            def normal(i, src, mv, std, rstd, k, result, ok):
                dve.wait_ge(rstd, due(2, i, k))
                for t in range(NT):
                    ins = dve.tensor_scalar(result(t), src(t), mv[:, t, 0:1], std[:, 1, t:t + 1], ALU.subtract, ALU.mult)
                ins.then_inc(ok, 1)

            def attention(i, last=False):
                links[0] = 0

                def text_lo(n):
                    dve.wait_ge(xT_hi, due(2, i, n + 1))
                    sub_hi(xT_hl[:, LO, :, :], halves(0), xT_hl[:, HI, :, :]).then_inc(xT_lo, 1)

                def queries_lo(n):
                    dve.wait_ge(q_hi, due(2, i, n + 1))
                    for c in range(NC):
                        r = dve.scalar_tensor_tensor(q_hl[:, LO, c, :], halves(1)[:, c, :], bq_col[:, c:c + 1],
                                                     f32(q_hl[:, HI, c, :]), ALU.add, ALU.subtract)
                    r.then_inc(q_lo, 1)
                    dve.wait_ge(q_lo, due(2, i, n + 1))
                    for strip in range(4):
                        dve.wait_ge(ops_in[strip], due(2, i, n - 1, step=16 * 6))
                    for e in range(2):
                        r = dve.tensor_scalar(q_sep[:, n % 2, :, :, e, :].rearrange("p a c t -> p (a c) t"),
                                              f32(q_hl[:, :, :, :]).rearrange("p a c t -> p (a c) t"),
                                              member[:, e:e + 1], None, ALU.mult)
                    r.then_inc(q_set, 1)

                def keys_lo(n):
                    dve.wait_ge(k_hi, due(2, i, n + 1))
                    for c in range(NC):
                        r = dve.scalar_tensor_tensor(k_hl[:, n % 2, LO, c, :], halves(2)[:, c, :], bq_col[:, NC + c:NC + c + 1],
                                                     f32(k_hl[:, n % 2, HI, c, :]), ALU.add, ALU.subtract)
                    r.then_inc(k_lo, 1)

                def values_out(n):
                    dve.wait_ge(v_mm, due(2, i, n + 1))
                    dve.wait_ge(vp_ok, due(2, i, n - 1))
                    for t in range(NT):
                        r = dve.tensor_copy(v_sb[:, n % 2, t, :], halves(0)[:, t, :])
                    r.then_inc(v_ok, 1)

                def maxima(step):
                    for qt in range(NT):
                        n = 2 * step + qt
                        dve.wait_ge(s_mm, due(32, i, n + 1))
                        dve.wait_ge(exp_ok, due(32, i, n - 15))
                        dve.tensor_reduce(neg_max[:, step % 8, qt, :], halves(4 + qt)[:, :, 0:(qt + 1) * P],
                                          AX.X, ALU.max, negate=True).then_inc(max_ok, 1)

                def probs_out(step):
                    n = 2 * step
                    dve.wait_ge(pT_mm, due(32, i, n + 1))
                    dve.wait_ge(pv_mm, due(32, i, n - 3))
                    dve.tensor_copy(probT[:, n % 4, :], bank[6][:, 0:SQ]).then_inc(pT_even, 1)

                def inverse_sums(j):
                    dve.wait_ge(exp_ok, due(32, i, 16 * (j + 1)))
                    dve.reciprocal(inv_sum[:, :, :], row_sum[:, j, :, :]).then_inc(attn_chain, 1)
                    dve.wait_ge(attn_chain, i * ATTN_LINKS + next_link())
                    dve.tensor_copy(inv_wide[:, :, :].rearrange("p t (h d) -> p (t h) d", d=DH),
                                    inv_sum[:, :, :].rearrange("p t h -> p (t h)").unsqueeze(2)
                                    .to_broadcast([P, NT * H, DH])).then_inc(inv_ok, 1)

                def heads(j):
                    dve.wait_ge(ib_ok, due(2, i, j + 1))
                    dve.wait_ge(pv_mm, due(32, i, 16 * (j + 1)))
                    dve.tensor_tensor(yn[:, :, :], halves(3), inv_bc[:, :, :], ALU.mult).then_inc(yn_ok, 1)

                def residual(j):
                    dve.wait_ge(pr_mm, due(2, i, j + 1))
                    dve.wait_ge(xr_ok, due(2, i, j + 1))
                    dve.tensor_tensor(u1[:, :, :], halves(2), xr[:, j, :, :], ALU.add).then_inc(u1_ok, 1)
                    dve.wait_ge(u1_ok, due(2, i, j + 1))
                    moments(i, attn_chain, ATTN_LINKS, lambda t: u1[:, t, :], stats1, mv1, std1, var1)

                def norm(j):
                    normal(i, lambda t: u1[:, t, :], mv1, std1, rstd1, j + 1, lambda t: u1[:, t, :], x1_ok)

                def steps(first, end):
                    for step in range(first, end):
                        if step < H:
                            maxima(step)
                        if step >= 1:
                            probs_out(step - 1)
                        if step == 1:
                            text_lo(1)
                        elif step == 3:
                            queries_lo(1)
                        elif step == 4:
                            keys_lo(1)
                        elif step == 5:
                            values_out(1)
                        elif step == 8:
                            inverse_sums(0)
                        elif step == 9:
                            heads(0)
                        elif step == 11:
                            residual(0)
                        elif step == 12:
                            norm(0)
                if i is not FIRST:
                    steps(0, 14)
                if not last:
                    text_lo(2)
                if i is not FIRST:
                    steps(14, 15)
                if not last:
                    queries_lo(2)
                if i is not FIRST:
                    steps(15, 16)
                if not last:
                    keys_lo(2)
                if i is not FIRST:
                    steps(16, 17)
                    inverse_sums(1)
                    heads(1)
                if not last:
                    values_out(2)
                if i is not FIRST:
                    residual(1)
                    norm(1)
                    assert links[0] == ATTN_LINKS
            attention(FIRST)
            with dve.Fori(0, PAIRS - 1) as i:
                attention(i)
            attention(PAIRS - 1, last=True)
            dve.drain().then_inc(done[1], 1)
            dve.wait_ge(done[1], 4)

            def context_mean(r):
                for j in range(2):
                    dve.wait_ge(c_sq, due(2, r, 2 + j + 1))
                    dve.tensor_scalar(c_ms[:, j, :], c_ss[:, j, :], 1.0 / D, RMS_EPS, ALU.mult, ALU.add).then_inc(c_mean, 1)

            def text_lo(r, j):
                dve.wait_ge(cT_hi, due(2, r, 2 + j + 1))
                sub_hi(cT_hl[:, LO, :, :], halves(BANK2["cT", j]), cT_hl[:, HI, :, :]).then_inc(cT_lo, 1)

            def context_lo(r, j):
                dve.wait_ge(kT_hi, due(2, r, 2 + j + 1))
                for c in range(NC):
                    ins = dve.scalar_tensor_tensor(kT_hl[:, j, LO, c, :], halves(BANK2["kT", j])[:, c, :], slot_col[:, c:c + 1],
                                                   f32(kT_hl[:, j, HI, c, :]), ALU.mult, ALU.subtract)
                ins.then_inc(kT_lo, 1)
                for g in range(3):
                    dve.wait_ge(vg_hi, due(6, r, 6 + 3 * j + g + 1))
                    for first, size, t in VG_ROWS[g]:
                        ins = dve.scalar_tensor_tensor(vg_hl[:, j, LO, 2 * g + first:2 * g + first + size, :],
                                                       halves(BANK2["vg", 3 * j + g])[:, first:first + size, :], c_rs[:, j, t:t + 1],
                                                       f32(vg_hl[:, j, HI, 2 * g + first:2 * g + first + size, :]), ALU.mult, ALU.subtract)
                    ins.then_inc(vg_lo, 1)

            def cross(i, first=False, last=False):
                links[0] = 0

                def next_slots(j):
                    dve.wait_ge(uT_mm, due(2, i, j + 1))
                    dve.tensor_copy(slots[:, j, :, :], x1T[:, :, bass.ds((i + 1) * (2 * T) + j * T, T)]).then_inc(sl_ok, 1)

                def start(u):
                    dve.wait_ge(sq_ok, due(UNITS, i, u + 1))
                    dve.tensor_tensor(sq[:, 0, :], sq[:, 0, :], sq[:, 1, :], ALU.add).then_inc(sqs_ok, 1)

                def mean_square(u):
                    j = u % 2
                    dve.wait_ge(ss_mm, due(UNITS, i, u + 1))
                    dve.tensor_scalar(s_ms[:, j, :], bank[0][:, 0:NT], RMS_EPS, None, ALU.add).then_inc(ms_ok, 1)

                def soft(u):
                    j = u % 2
                    dve.wait_ge(sc_mm, due(UNITS, i, u + 1))
                    dve.wait_ge(rb_ok, due(UNITS, i, u + 1))
                    dve.wait_ge(c_kept, due(1, i, 1))
                    for t in range(NT):
                        r = dve.scalar_tensor_tensor(attn[:, j, t, :], halves(3)[:, t, :], c_now[:, j, t:t + 1], rs_bc[:, j, :],
                                                     ALU.mult, ALU.mult)
                    r.then_inc(sc_ok, 1)
                    dve.wait_ge(sc_ok, due(UNITS, i, u + 1))
                    dve.tensor_reduce(s_max[:, j, :], attn[:, j, :, :], AX.X, ALU.max, negate=True).then_inc(smax_ok, 1)

                def soft_sum(u):
                    j = u % 2
                    dve.wait_ge(e_ok, due(UNITS, i, u + 1))
                    dve.reciprocal(s_inv[:, j, :], s_sum[:, j, :]).then_inc(z_ok, 1)

                def totals(u):
                    dve.wait_ge(tt_mm, due(UNITS, i, u + 1))
                    dve.tensor_scalar(tot[:, :], bank[2][:, 0:T], RMS_EPS, None, ALU.add).then_inc(tt_ok, 1)
                    dve.wait_ge(tt_ok, due(UNITS, i, u + 1))
                    dve.reciprocal(inv_tot[:, :], tot[:, :]).then_inc(it_ok, 1)

                def weights(u):
                    j = u % 2
                    dve.wait_ge(it_ok, due(UNITS, i, u + 1))
                    for t in range(NT):
                        r = dve.scalar_tensor_tensor(attn[:, j, t, :], attn[:, j, t, :], s_inv[:, j, t:t + 1], inv_tot[:, :],
                                                     ALU.mult, ALU.mult)
                    r.then_inc(at_ok, 1)

                def reset_gate(u):
                    dve.wait_ge(r_ok, due(UNITS, i, u + 1))
                    dve.tensor_scalar(gate_r[:, :, :], gate_r[:, :, :], 0.5, 0.5, ALU.mult, ALU.add).then_inc(cross_chain, 1)
                    dve.wait_ge(cross_chain, i * CROSS_LINKS + next_link())
                    dve.wait_ge(hn_mm, due(UNITS, i, u + 1))
                    for c in range(NC):
                        r = dve.scalar_tensor_tensor(gate_r[:, c, :], halves(6)[:, c, :], bhh_col[:, 2 * NC + c:2 * NC + c + 1],
                                                     gate_r[:, c, :], ALU.add, ALU.mult)
                    r.then_inc(g_ok, 1)

                def gates(u):
                    j = u % 2
                    dve.wait_ge(g_ok, due(UNITS, i, u + 1))
                    dve.wait_ge(xn_mm, due(UNITS, i, u + 1))
                    dve.tensor_tensor(gate_r[:, :, :], halves(7), gate_r[:, :, :], ALU.add).then_inc(np_ok, 1)
                    dve.wait_ge(n_ok, due(UNITS, i, u + 1))
                    dve.tensor_tensor(diff[:, :, :], slots[:, j, :, :], cand[:, :, :], ALU.subtract).then_inc(cross_chain, 1)
                    dve.wait_ge(cross_chain, i * CROSS_LINKS + next_link())
                    dve.wait_ge(zt_ok, due(UNITS, i, u + 1))
                    dve.scalar_tensor_tensor(diff[:, :, :], gate_z[:, :, :], 1.0, diff[:, :, :], ALU.add, ALU.mult).then_inc(cross_chain, 1)
                    dve.wait_ge(cross_chain, i * CROSS_LINKS + next_link())
                    dve.scalar_tensor_tensor(slots[:, j, :, :], diff[:, :, :], 0.5, cand[:, :, :], ALU.mult, ALU.add).then_inc(sl_ok, 1)

                def residual(j):
                    dve.wait_ge(sl_ok, due(8, i, 7 + j))
                    dve.tensor_tensor(slots[:, j, :, :], slots[:, j, :, :],
                                      x1T[:, :, bass.ds(i * (2 * T) + j * T, T)], ALU.add).then_inc(uu_ok, 1)

                def between(u):
                    if u < UNITS:
                        totals(u)
                    if u + 1 < UNITS:
                        start(u + 1)
                    if u < UNITS:
                        weights(u)
                    if u + 1 < UNITS:
                        mean_square(u + 1)

                def norm(j):
                    dve.wait_ge(uT_mm, due(2, i, j + 1))
                    layer_norm(i, cross_chain, CROSS_LINKS, lambda t: halves(BANK2["uT", j])[:, t, :], stats2, mv2, std2, var2, rstd2, j + 1,
                               lambda t: x2[:, bass.ds(i * (2 * NT) + j * NT + t, 1), :], x2_ok)
                if first:
                    context_mean(i)
                    text_lo(i, 0)
                    context_lo(i, 0)
                    text_lo(i, 1)
                else:
                    soft(0)
                    soft_sum(0)
                    between(0)
                    for u in range(UNITS):
                        if u + 1 < UNITS:
                            soft(u + 1)
                        reset_gate(u)
                        if u + 1 < UNITS:
                            soft_sum(u + 1)
                        gates(u)
                        if u == 4 and not last:
                            text_lo(i, 0)
                        between(u + 1)
                        if u == 3 and not last:
                            context_mean(i)
                        if u == 4:
                            residual(0)
                            if not last:
                                context_lo(i, 0)
                                text_lo(i, 1)
                    residual(1)
                if not last:
                    next_slots(0)
                    start(UNITS)
                if not first:
                    norm(0)
                if not last:
                    context_lo(i, 1)
                    next_slots(1)
                    dve.wait_ge(c_rstd, due(2, i, 2 + 2))
                    dve.tensor_copy(c_now[:, :, :], c_rs[:, :, :]).then_inc(c_kept, 1)
                    mean_square(UNITS)
                if not first:
                    norm(1)
                    assert links[0] == CROSS_LINKS
            cross(-1, first=True)
            with dve.Fori(0, PAIRS - 1) as i:
                cross(i)
            cross(PAIRS - 1, last=True)
            dve.drain().then_inc(done[2], 1)
            dve.wait_ge(done[2], 4)

            def text_lo(i, j):
                dve.wait_ge(tT_hi, due(2, i, j + 1))
                sub_hi(x2T_hl[:, j, LO, :, :], halves(j), x2T_hl[:, j, HI, :, :]).then_inc(tT_lo, 1)

            def experts(i, last):
                links[0] = 0

                def logits(j):
                    dve.wait_ge(lg_mm, due(2, i, j + 1))
                    dve.tensor_copy(logT[:, j, :], bank[2][0:NE, 0:T]).then_inc(lg_ok, 1)

                def route(j):
                    dve.wait_ge(lx_ok, due(2, i, j + 1))
                    dve.tensor_scalar(prb[:, :, 0:NE], prb[:, :, 0:NE], 1.0, None, ALU.add).then_inc(expert_chain, 1)
                    dve.wait_ge(expert_chain, i * EXPERT_LINKS + next_link())
                    dve.reciprocal(prb[:, :, 0:NE], prb[:, :, 0:NE]).then_inc(expert_chain, 1)
                    dve.wait_ge(expert_chain, i * EXPERT_LINKS + next_link())
                    dve.sem_inc(passed, 1)
                    for t in range(NT):
                        r = dve.max(top8[:, t, :], prb[:, t, 0:NE])
                    r.then_inc(expert_chain, 1)
                    dve.wait_ge(expert_chain, i * EXPERT_LINKS + next_link())
                    dve.memset(top8[:, :, TOPK:], -1.0).then_inc(expert_chain, 1)
                    dve.wait_ge(expert_chain, i * EXPERT_LINKS + next_link())
                    dve.sem_inc(passed, 1)
                    for t in range(NT):
                        r = dve.match_replace(prbx[:, t, :], top8[:, t, :], prb[:, t, :], 0.0)
                    r.then_inc(expert_chain, 1)
                    dve.wait_ge(expert_chain, i * EXPERT_LINKS + next_link())
                    dve.tensor_tensor(gate[:, :, :], prb[:, :, 0:NE], prbx[:, :, 0:NE], ALU.subtract).then_inc(expert_chain, 1)
                    dve.wait_ge(expert_chain, i * EXPERT_LINKS + next_link())
                    dve.tensor_reduce(gsum[:, :], gate[:, :, :], AX.X, ALU.add).then_inc(expert_chain, 1)
                    dve.wait_ge(expert_chain, i * EXPERT_LINKS + next_link())
                    dve.tensor_scalar(gsum[:, :], gsum[:, :], 1e-9, None, ALU.max).then_inc(expert_chain, 1)
                    dve.wait_ge(expert_chain, i * EXPERT_LINKS + next_link())
                    dve.reciprocal(ginv[:, :], gsum[:, :]).then_inc(expert_chain, 1)
                    dve.wait_ge(expert_chain, i * EXPERT_LINKS + next_link())
                    for t in range(NT):
                        r = dve.tensor_scalar(gate[:, t, :], gate[:, t, :], ginv[:, t:t + 1], route_col[:, 0:1], ALU.mult, ALU.mult)
                    r.then_inc(gt_ok, 1)

                def gates_lo(j):
                    dve.wait_ge(gT_hi, due(2, i, j + 1))
                    sub_hi(gateT_hl[32:32 + NE, j, :], bank[1 - j][0:NE, 0:T], gateT_hl[0:NE, j, :]).then_inc(gT_lo, 1)

                def gated(n):
                    dve.wait_ge(h_relu, due(8, i, n + 1))
                    dve.wait_ge(gb_mm, due(8, i, n + 1))
                    dve.tensor_tensor(hid[:, n % 4, :, :], halves(6 + n % 2), hid[:, n % 4, :, :], ALU.mult).then_inc(h_ok, 1)
                logits(0)
                route(0)
                logits(1)
                gates_lo(0)
                gated(0)
                gated(1)
                route(1)
                gated(2)
                gates_lo(1)
                for n in range(3, 8):
                    gated(n)
                if not last:
                    text_lo(i + 1, 0)
                    text_lo(i + 1, 1)
                for j in range(2):
                    dve.wait_ge(o_mm, due(2, i, j + 1))
                    dve.wait_ge(y_ok, due(2, i, 1 if j else 2, back=1 - j))
                    dve.tensor_tensor(u3[:, :, :], halves(2 + j), x2[:, bass.ds(i * (2 * NT) + j * NT, NT), :], ALU.add).then_inc(u3_ok, 1)
                    dve.wait_ge(u3_ok, due(2, i, j + 1))
                    dve.wait_ge(stored[j], due(1, i, 1, back=1, step=16))
                    layer_norm(i, expert_chain, EXPERT_LINKS, lambda t: u3[:, t, :], stats3, mv3, std3, var3, rstd3, j + 1,
                               lambda t: y_out[:, j, t, :], y_ok)
                assert links[0] == EXPERT_LINKS
            text_lo(0, 0)
            text_lo(0, 1)
            with dve.Fori(0, PAIRS - 1) as i:
                experts(i, False)
            experts(PAIRS - 1, True)

        @block.tensor
        def _(pe):
            pe.wait_ge(consts, 9)
            for n, (w, arrived) in enumerate(((st_hh, w_in[1]), (st_ih, w_in[4]))):
                pe.wait_ge(arrived, 16)
                for c in range(NC):
                    for half in range(2):
                        for q in range(4 if half == 0 else 2):
                            mm = pe.transpose(bank[4 * n + 2 * c + half][:, q * P:(q + 1) * P],
                                              w[:, 4 * half + q, c * P:(c + 1) * P], ident[:, :])
                        mm.then_inc(prep_mm, 1)
            pe.wait_ge(prep_out, 1)
            pe.wait_ge(prep_act, 10)
            pe.wait_ge(w_in[5], 64)
            for c in range(NC):
                mm = pe.transpose(bank[0][:, c * NE:(c + 1) * NE], st_esel[:, c * P:(c + 1) * P], ident[0:NE, 0:NE])
            mm.then_inc(prep_mm, 1)
            for c in range(NC):
                for o in range(NC):
                    mm = pe.matmul(bank[1 + c][:, 0:D], st_wk[:, o, c * P:(c + 1) * P], st_wq[:, o, :], start=o == 0, stop=o == 1)
                mm.then_inc(prep_mm, 1)
            for c in range(NC):
                for b, lo, size in ((3 + 2 * c, 0, 512), (4 + 2 * c, 512, 256)):
                    for o in range(NC):
                        mm = pe.matmul(bank[b][:, 0:size], st_wv[:, o, c * P:(c + 1) * P], st_ihT[:, o, lo:lo + size],
                                       start=o == 0, stop=o == 1)
                    mm.then_inc(prep_mm, 1)
            pe.drain().then_inc(done[0], 1)
            pe.wait_ge(done[0], 4)

            def attention(i, last=False):
                def ready_bank(key):
                    b, read, count = bank_free(jobs1, i, key, last)
                    pe.wait_ge(read, count)
                    return b
                for name, n in ATTN_ORDER:
                    ahead = name in ("xT", "q", "k", "v") and n == 2
                    if (last and ahead) or (i is FIRST and not ahead):
                        continue
                    if name == "xT":
                        b = ready_bank((name, n))
                        pe.wait_ge(x_arr[n % 2], due(1, i, 1 + n // 2, step=16))
                        transpose4(pe, b, lambda t, c: x_in[:, n % 2, t, c * P:(c + 1) * P]).then_inc(xT_mm, 1)
                    elif name in ("q", "k"):
                        b = ready_bank((name, n))
                        pe.wait_ge(xT_lo, due(2, i, n + 1))
                        for m in range(NC):
                            for c in range(NC):
                                at = (D if name == "k" else 0) + m * P
                                mm = split3(pe, halves(b)[:, m, :], lambda a: wqkv_hl[:, a, c, at:at + P],
                                            lambda a: xT_hl[:, a, c, :], c == 0, c == 1)
                        mm.then_inc(q_mm if name == "q" else k_mm, 1)
                    elif name == "v":
                        b = ready_bank((name, n))
                        for t in range(NT):
                            for c in range(NC):
                                mm = split3(pe, halves(b)[:, t, :], lambda a: xT_hl[:, a, c, t * P:(t + 1) * P],
                                            lambda a: wqkv_hl[:, a, c, 2 * D:], c == 0, c == 1)
                        mm.then_inc(v_mm, 1)
                    elif name == "s":
                        j, hp = n // 8, n % 8
                        pair = head(2 * hp) // 2
                        if hp % 2 == 0:
                            pe.wait_ge(ops_in[hp // 2], due(2, i, j + 1, step=16 * 6))
                        for qt in range(NT):
                            b = ready_bank(("s", 2 * n + qt))
                            rows = slice(qt * P, (qt + 1) * P)
                            for e in range(2):
                                pe.matmul(halves(b)[:, e, :], q_op[:, pair, e, rows], k_op[:, pair, :],
                                          start=e == 0, stop=False, skip_group_check=True)
                            pe.matmul(halves(b)[:, :, rows], ident16[:, :], mask16[:, :, :],
                                      start=False, stop=True, skip_group_check=True).then_inc(s_mm, 1)
                    elif name == "pT":
                        for e in range(2):
                            b = ready_bank(("pT", 2 * n + e))
                            pe.wait_ge(exp_ok, due(32, i, 2 * n + 2))
                            for lo in (0, P, 2 * P):
                                mm = pe.transpose(bank[b][:, lo:lo + P], prob[:, n % 2, e, lo:lo + P], ident[:, :])
                            mm.then_inc(pT_mm, 1)
                    elif name == "pv":
                        j = n // 8
                        if n % 8 == 0:
                            ready_bank(("y", j))
                            pe.wait_ge(vp_ok, due(2, i, j + 1))
                        for e in range(2):
                            pe.wait_ge((pT_even, pT_odd)[e], due(16, i, n + 1))
                            at = 2 * (n % 8) + e
                            c = head(at) // 8
                            pe.matmul(halves(3)[:, c, :], v_pad[:, 0, head(at), :], probT[:, at % 4, 0:T],
                                      start=at == 0, stop=False, skip_group_check=True)
                            pe.matmul(halves(3)[:, c, P:], v_pad[:, 1, head(at), :], probT[:, at % 4, T:],
                                      start=False, stop=at == H - 1, skip_group_check=True).then_inc(pv_mm, 1)
                    elif name == "ib":
                        b = ready_bank((name, n))
                        pe.wait_ge(inv_ok, due(2, i, n + 1))
                        for c in range(NC):
                            for t in range(NT):
                                mm = pe.matmul(halves(b)[:, c, t * P:(t + 1) * P], inv_wide[:, t, c * P:(c + 1) * P],
                                               ident[:, :], start=True, stop=True)
                        mm.then_inc(ib_mm, 1)
                    elif name == "pr":
                        b = ready_bank((name, n))
                        pe.wait_ge(y_lo, due(2, i, n + 1))
                        for t in range(NT):
                            for c in range(NC):
                                mm = split3(pe, halves(b)[:, t, :], lambda a: y_hl[:, a, c, t * P:(t + 1) * P],
                                            lambda a: wproj_hl[:, a, c, :], c == 0, c == 1)
                        mm.then_inc(pr_mm, 1)
                    else:
                        b = ready_bank((name, n))
                        pe.wait_ge(x1_ok, due(2, i, n + 1))
                        transpose4(pe, b, lambda t, c: u1[:, t, c * P:(c + 1) * P]).then_inc(x1T_mm, 1)
            attention(FIRST)
            with pe.Fori(0, PAIRS - 1) as i:
                attention(i)
            attention(PAIRS - 1, last=True)
            pe.drain().then_inc(done[1], 1)
            pe.wait_ge(done[1], 4)

            def context_text(r, j):
                b, read, count = bank_free(jobs2, r, ("cT", j))
                pe.wait_ge(read, count)
                pe.wait_ge(c_arr[j], due(1, r, 2, step=16))
                transpose4(pe, b, lambda t, c: c_in[:, j, t, c * P:(c + 1) * P]).then_inc(cT_mm, 1)

            def context_keys(r, j):
                pe.wait_ge(cT_lo, due(2, r, 2 + j + 1))
                b, read, count = bank_free(jobs2, r, ("kT", j))
                pe.wait_ge(read, count)
                for m in range(NC):
                    for c in range(NC):
                        mm = split3(pe, halves(b)[:, m, :], lambda a: qk_w_hl[:, a, c, m * P:(m + 1) * P],
                                    lambda a: cT_hl[:, a, c, :], c == 0, c == 1)
                mm.then_inc(kT_mm, 1)

            def context_values(r, j):
                for g in range(3):
                    b, read, count = bank_free(jobs2, r, ("vg", 3 * j + g))
                    pe.wait_ge(read, count)
                    for half in range(2):
                        t, blk = divmod(2 * g + half, 3)
                        for c in range(NC):
                            mm = split3(pe, halves(b)[:, half, :], lambda a: cT_hl[:, a, c, t * P:(t + 1) * P],
                                        lambda a: v_w_hl[:, a, c, blk * D:(blk + 1) * D], c == 0, c == 1)
                    mm.then_inc(vg_mm, 1)

            def cross(i, first=False, last=False):
                def start(u):
                    j = u % 2
                    b, read, count = bank_free(jobs2, i, ("ss", u))
                    pe.wait_ge(read, count)
                    pe.wait_ge(sqs_ok, due(UNITS, i, u + 1))
                    for t in range(NT):
                        mm = pe.matmul(bank[b][:, t:t + 1], sq[:, 0, t * P:(t + 1) * P], mean_col[:, :], start=True, stop=True)
                    mm.then_inc(ss_mm, 1)
                    b, read, count = bank_free(jobs2, i, ("sc", u))
                    pe.wait_ge(read, count)
                    pe.wait_ge(sl_hi, due(6, i, u + 1))
                    pe.wait_ge(kT_lo, due(2, i, j + 1 + (2 if u == UNITS else 0)))
                    for n, (k_part, s_part) in enumerate(HI_FIRST):
                        if s_part == LO:
                            pe.wait_ge(sl_lo, due(6, i, u + 1))
                        for t in range(NT):
                            for c in range(NC):
                                mm = pe.matmul(halves(b)[:, t, :], kT_hl[:, j, k_part, c, t * P:(t + 1) * P], slots_hl[:, j, s_part, c, :],
                                               start=n + t + c == 0, stop=n == 2, skip_group_check=True)
                    mm.then_inc(sc_mm, 1)
                    b, read, count = bank_free(jobs2, i, ("rb", u))
                    pe.wait_ge(read, count)
                    pe.wait_ge(rs_ok, due(UNITS, i, u + 1))
                    for t in range(NT):
                        mm = pe.matmul(bank[b][:, t * P:(t + 1) * P], s_rs[:, j, t:t + 1].to_broadcast([P, P]), ident[:, :],
                                       start=True, stop=True)
                    mm.then_inc(rb_mm, 1)

                def state(u):
                    j = u % 2
                    for n, name in enumerate(("r", "z", "hn")):
                        b, read, count = bank_free(jobs2, i, (name, u))
                        pe.wait_ge(read, count)
                        for m in range(NC):
                            cols = slice(n * D + m * P, n * D + (m + 1) * P)
                            for c in range(NC):
                                mm = split3(pe, halves(b)[:, m, :], lambda a: whhT_hl[:, a, c, cols],
                                            lambda a: slots_hl[:, j, a, c, :], m == 0 and c == 0, False)
                    mm.then_inc(hn_mm, 1)

                def totals(u):
                    j = u % 2
                    b, read, count = bank_free(jobs2, i, ("tt", u))
                    pe.wait_ge(read, count)
                    pe.wait_ge(z_ok, due(UNITS, i, u + 1))
                    for t in range(NT):
                        mm = pe.matmul(bank[b][:, 0:T], s_inv[:, j, t:t + 1].to_broadcast([P, P]), attn[:, j, t, :],
                                       start=t == 0, stop=t == 1)
                    mm.then_inc(tt_mm, 1)

                def inputs(u):
                    j = u % 2
                    pe.wait_ge(at_hi, due(UNITS, i, u + 1))
                    pe.wait_ge(vg_lo, due(6, i, 3 * j + 3))
                    for n, b, ev in ((0, 4, r_mm), (2, 7, xn_mm), (1, 5, z_mm)):
                        if n == 2:
                            b, read, count = bank_free(jobs2, i, ("xn", u))
                            pe.wait_ge(read, count)
                        for a, (v_part, at_part) in enumerate(HI_FIRST):
                            if n == 0 and at_part == LO:
                                pe.wait_ge(at_lo, due(UNITS, i, u + 1))
                            for m in range(NC):
                                for t in range(NT):
                                    r, q = divmod(n * D + m * P, D)
                                    mm = pe.matmul(halves(b)[:, m, :], vg_hl[:, j, v_part, 3 * t + r, q:q + P], attn_hl[:, j, at_part, t, :],
                                                   start=n == 2 and a + m + t == 0, stop=True, skip_group_check=True)
                        mm.then_inc(ev, 1)
                def text(j):
                    b, read, count = bank_free(jobs2, i, ("uT", j), last)
                    pe.wait_ge(read, count)
                    pe.wait_ge(uu_ok, due(2, i, j + 1))
                    transpose4(pe, b, lambda c, t: slots[:, j, c, t * P:(t + 1) * P]).then_inc(uT_mm, 1)
                if first:
                    context_text(i, 0)
                    context_keys(i, 0)
                    context_values(i, 0)
                    context_text(i, 1)
                else:
                    state(0)
                    totals(0)
                    for u in range(UNITS):
                        if u + 1 < UNITS:
                            start(u + 1)
                        inputs(u)
                        if u == 4 and not last:
                            context_text(i, 0)
                        if u + 1 < UNITS:
                            totals(u + 1)
                            state(u + 1)
                        if u == 4 and not last:
                            context_keys(i, 0)
                            context_values(i, 0)
                            context_text(i, 1)
                if not last:
                    context_keys(i, 1)
                if not first:
                    text(0)
                if not last:
                    context_values(i, 1)
                if not first:
                    text(1)
                if not last:
                    start(UNITS)
            cross(-1, first=True)
            with pe.Fori(0, PAIRS - 1) as i:
                cross(i)
            cross(PAIRS - 1, last=True)
            pe.drain().then_inc(done[2], 1)
            pe.wait_ge(done[2], 4)

            def text(j):
                transpose4(pe, j, lambda t, c: x2f[:, j, t, c * P:(c + 1) * P]).then_inc(tT_mm, 1)

            def experts(i, last):
                for name, n in EXPERT_ORDER:
                    if name == "tT" and last:
                        continue
                    b, read, count = bank_free(jobs3, i, (name, n))
                    pe.wait_ge(read, count)
                    j = n // 4 if name in ("h", "gb") else n
                    g = n % 4
                    if name == "tT":
                        pe.wait_ge(xf_ok, due(2, i, 2 + j + 1))
                        text(j)
                    elif name == "lg":
                        pe.wait_ge(tT_lo, due(2, i, j + 1))
                        for c in range(NC):
                            mm = split3(pe, bank[b][0:NE, 0:T], lambda a: eselT_hl[:, a, c, :], lambda a: x2T_hl[:, j, a, c, :], c == 0, c == 1)
                        mm.then_inc(lg_mm, 1)
                    elif name == "lT":
                        pe.wait_ge(lg_ok, due(2, i, j + 1))
                        pe.sem_inc(passed, 1)
                        for t in range(NT):
                            mm = pe.transpose(bank[b][:, t * NE:(t + 1) * NE], logT[:, j, t * P:(t + 1) * P], ident[0:NE, 0:NE])
                        mm.then_inc(lT_mm, 1)
                    elif name == "gT":
                        pe.wait_ge(gt_ok, due(2, i, j + 1))
                        for t in range(NT):
                            mm = pe.transpose(bank[b][0:NE, t * P:(t + 1) * P], gate[:, t, :], ident[:, :])
                        mm.then_inc(gT_mm, 1)
                    elif name == "h":
                        for half in range(2):
                            m = 2 * g + half
                            for c in range(NC):
                                mm = split3(pe, halves(b)[:, half, :], lambda a: keys_hl[:, a, c, m * P:(m + 1) * P],
                                            lambda a: x2T_hl[:, j, a, c, :], c == 0, c == 1)
                        mm.then_inc(h_mm, 1)
                    elif name == "gb":
                        pe.wait_ge(gT_lo, due(2, i, j + 1))
                        for half in range(2):
                            mm = pe.matmul(halves(b)[:, half, :], spread[:, 2 * g + half, :], gateT_hl[:, j, :], start=True, stop=True)
                        mm.then_inc(gb_mm, 1)
                    else:
                        pe.wait_ge(h_lo, due(8, i, 4 * j + 4))
                        for t in range(NT):
                            for m in range(NH):
                                mm = split3(pe, halves(b)[:, t, :], lambda a: hid_hl[:, j, a, m, t * P:(t + 1) * P],
                                            lambda a: values_hl[:, a, m, :], m == 0, m == NH - 1)
                        mm.then_inc(o_mm, 1)
            for j in range(2):
                pe.wait_ge(xf_ok, due(2, 0, j + 1))
                text(j)
            pe.wait_ge(consts, 16)
            with pe.Fori(0, PAIRS - 1) as i:
                experts(i, False)
            experts(PAIRS - 1, True)
        s3.close()


_INS = ['x', 'ctx_1024', 'L0_attn_w_qkv', 'L0_attn_b_qkv', 'L0_attn_w_proj', 'L0_attn_b_proj', 'L0_xattn_Wq',
        'L0_xattn_Wk', 'L0_xattn_Wv', 'L0_xattn_gru_wih', 'L0_xattn_gru_whh', 'L0_xattn_gru_bih', 'L0_xattn_gru_bhh',
        'L0_xattn_slot_norm_w', 'L0_xattn_input_norm_w', 'L0_ffn_expert_sel', 'L0_ffn_keys', 'L0_ffn_values',
        'L0_ffn_route_scale']


def kernel(**inputs):
    import numpy as _np
    import concourse.bacc as _bacc
    from concourse import mybir as _mybir
    from concourse.bass_utils import run_bass_kernel_spmd as _run

    nc = _bacc.Bacc("TRN2", target_bir_lowering=False, num_devices=1)
    arrays, args = {}, []
    for name in _INS:
        a = _np.ascontiguousarray(inputs[name])
        arrays[f"in_{name}_dram"] = a
        args.append(nc.dram_tensor(f"in_{name}_dram", a.shape, _mybir.dt.from_np(a.dtype), kind="ExternalInput").ap())
    args.append(nc.dram_tensor("out_dram", (B, T, D), _mybir.dt.float32, kind="ExternalOutput").ap())
    decoder_layer(nc, *args)
    r = _run(nc, [arrays], core_ids=[0])
    return r.results[0]["out_dram"]
```
